# Optimizing a Trainium2 kernel written in Bass

```python
import numpy as np
import jax
import jax.numpy as jnp

def _softmax(x, axis=-1):
    return jax.nn.softmax(x, axis=axis)

def _gelu(x):
    return jax.nn.gelu(x, approximate=True)

def _silu(x):
    return jax.nn.silu(x)

def _sigmoid(x):
    return jax.nn.sigmoid(x)

def _layernorm(x, axis=-1, eps=1e-05):
    m = jnp.mean(x, axis=axis, keepdims=True)
    v = jnp.var(x, axis=axis, keepdims=True)
    return (x - m) / jnp.sqrt(v + eps)

def _scatter_add(tgt, idx, src, axis=0):
    return tgt.at[idx].add(src)

def _segment_sum(src, seg, n):
    return jax.ops.segment_sum(src, seg, n)
kernel_name = 'mk_cond_seq_d4_seqx_r4_3bf96e'

def setup_inputs(seed: int=0):
    np.random.seed(seed)
    _w = jnp.asarray

    def _rec_inputs():
        import jax
        import jax.numpy as jnp
        _rk = jax.random.key(seed)
        x = -0.000125 + 0.9999 * jax.random.normal(jax.random.fold_in(_rk, 1), (32, 256, 256), jnp.float32)
        _lenS = 256 - jax.random.randint(jax.random.fold_in(_rk, 7), (32,), 0, max(1, 256 // 4) + 1, jnp.int32)
        _lenS2 = 256 - jax.random.randint(jax.random.fold_in(_rk, 8), (32,), 0, max(1, 256 // 4) + 1, jnp.int32)
        cond_256 = 0.000887014 + 1.03683 * jax.random.normal(jax.random.fold_in(_rk, 11), (32, 64), jnp.float32)
        return (x, cond_256)
    x, cond_256 = _rec_inputs()

    def _L0_cond_setup():
        import jax, jax.numpy as jnp
        import numpy as np
        EPS = 1e-05
        key = jax.random.key(seed)
        k1, k2, k3, k4 = jax.random.split(key, 4)
        b, t, d, num_con = (8, 1024, 256, 64)
        return {'input': jax.random.normal(k1, (b, t, d), dtype=jnp.float32), 'convInfo': jax.random.normal(k2, (b, num_con), dtype=jnp.float32), 'weight': jnp.ones((d,), dtype=jnp.float32), 'bias': jnp.zeros((d,), dtype=jnp.float32), 'lin_w': jax.random.normal(k3, (d, num_con), dtype=jnp.float32) * (1.0 / np.sqrt(num_con)), 'lin_b': jax.random.normal(k4, (d,), dtype=jnp.float32) * 0.01}
    _L0_cond_all = _L0_cond_setup()
    _L0_cond_in = {k: v for k, v in _L0_cond_all.items() if k in ('weight', 'bias', 'lin_w', 'lin_b')}
    del _L0_cond_all

    def _L1_cond_setup():
        import jax, jax.numpy as jnp
        import numpy as np
        from math import sqrt
        D_MODEL = 256
        N_HEADS = 16
        D_T = 64
        D_HID = 4 * D_MODEL
        EPS = 1e-06

        def _rmsnorm(x):
            return x * jax.lax.rsqrt(jnp.mean(x * x, axis=-1, keepdims=True) + EPS)

        def _ada_rmsnorm(x, t, gamma_w, beta_w):
            gamma = (t @ gamma_w.T)[:, None, :]
            beta = (t @ beta_w.T)[:, None, :]
            return gamma * _rmsnorm(x) + beta

        def _attention(x, W_q, W_k, W_v, W_o):
            b, l, dm = x.shape
            d_head = dm // N_HEADS
            scale = sqrt(N_HEADS / dm)

            def split(y):
                return y.reshape(b, l, N_HEADS, d_head).transpose(0, 2, 1, 3)
            q = split(x @ W_q.T)
            k = split(x @ W_k.T)
            v = split(x @ W_v.T)
            attn = jax.nn.softmax(scale * jnp.einsum('bnqd,bnkd->bnqk', q, k), axis=-1)
            o = jnp.einsum('bnqk,bnkd->bnqd', attn, v)
            o = o.transpose(0, 2, 1, 3).reshape(b, l, dm)
            return o @ W_o.T

        def _swiglu(x, gate_w, hidden_w, out_w, out_b):
            return jax.nn.silu(x @ gate_w.T) * (x @ hidden_w.T) @ out_w.T + out_b
        key = jax.random.key(seed)
        ks = jax.random.split(key, 16)
        s = 0.02
        inp = {'x': jax.random.normal(ks[0], (4, 512, D_MODEL), dtype=jnp.float32), 't': jax.random.normal(ks[1], (4, D_T), dtype=jnp.float32), 'attn_gamma_w': jax.random.normal(ks[2], (D_MODEL, D_T), dtype=jnp.float32) * s, 'attn_beta_w': jax.random.normal(ks[3], (D_MODEL, D_T), dtype=jnp.float32) * s, 'W_q': jax.random.normal(ks[4], (D_MODEL, D_MODEL), dtype=jnp.float32) * s, 'W_k': jax.random.normal(ks[5], (D_MODEL, D_MODEL), dtype=jnp.float32) * s, 'W_v': jax.random.normal(ks[6], (D_MODEL, D_MODEL), dtype=jnp.float32) * s, 'W_o': jax.random.normal(ks[7], (D_MODEL, D_MODEL), dtype=jnp.float32) * s, 'attn_alpha_w': jax.random.normal(ks[8], (D_MODEL, D_T), dtype=jnp.float32) * s, 'ffn_gamma_w': jax.random.normal(ks[9], (D_MODEL, D_T), dtype=jnp.float32) * s, 'ffn_beta_w': jax.random.normal(ks[10], (D_MODEL, D_T), dtype=jnp.float32) * s, 'gate_w': jax.random.normal(ks[11], (D_HID, D_MODEL), dtype=jnp.float32) * s, 'hidden_w': jax.random.normal(ks[12], (D_HID, D_MODEL), dtype=jnp.float32) * s, 'out_w': jax.random.normal(ks[13], (D_MODEL, D_HID), dtype=jnp.float32) * s, 'out_b': jnp.zeros((D_MODEL,), dtype=jnp.float32), 'ffn_alpha_w': jax.random.normal(ks[14], (D_MODEL, D_T), dtype=jnp.float32) * s}
        return inp
    _L1_cond_all = _L1_cond_setup()
    _L1_cond_in = {k: v for k, v in _L1_cond_all.items() if k in ('attn_gamma_w', 'attn_beta_w', 'W_q', 'W_k', 'W_v', 'W_o', 'attn_alpha_w', 'ffn_gamma_w', 'ffn_beta_w', 'gate_w', 'hidden_w', 'out_w', 'out_b', 'ffn_alpha_w')}
    del _L1_cond_all

    def _L2_cond_setup():
        import jax, jax.numpy as jnp
        import numpy as np
        DIM = 256
        BN = 128
        H = 64
        DELTA_SCALE = 0.1
        key = jax.random.key(seed)
        ks = jax.random.split(key, 10)
        B, L = (16, 512)

        def init(k, shape, fan_in):
            bound = 1.0 / np.sqrt(fan_in)
            return jax.random.uniform(k, shape, jnp.float32, -bound, bound)
        return {'x': jax.random.normal(ks[0], (B, L, DIM), jnp.float32), 'h_lang': jax.random.normal(ks[1], (B, H), jnp.float32), 'Wd': init(ks[2], (BN, DIM), DIM), 'bd': init(ks[3], (BN,), DIM), 'Wu': init(ks[4], (DIM, BN), BN), 'bu': init(ks[5], (DIM,), BN), 'Wdd': init(ks[6], (BN * DIM, H), H), 'bdd': init(ks[7], (BN * DIM,), H), 'Wdu': init(ks[8], (DIM * BN, H), H), 'bdu': init(ks[9], (DIM * BN,), H)}
    _L2_cond_all = _L2_cond_setup()
    _L2_cond_in = {k: v for k, v in _L2_cond_all.items() if k in ('Wd', 'bd', 'Wu', 'bu', 'Wdd', 'bdd', 'Wdu', 'bdu')}
    del _L2_cond_all

    def _L3_cond_setup():
        import jax, jax.numpy as jnp
        import numpy as np
        EPS = 1e-06

        def act_quant(x):
            scale = 127.0 / jnp.clip(jnp.max(jnp.abs(x), axis=-1, keepdims=True), 1e-05, None)
            return jnp.clip(jnp.round(x * scale), -128.0, 127.0) / scale

        def weight_quant(w):
            scale = 1.0 / jnp.clip(jnp.mean(jnp.abs(w)), 1e-05, None)
            return jnp.clip(jnp.round(w * scale), -1.0, 1.0) / scale
        key = jax.random.key(seed)
        k0, k1, k2, k3, k4 = jax.random.split(key, 5)
        B, S, D, FF, C = (4, 1024, 256, 1024, 64)
        return {'x': jax.random.normal(k0, (B, S, D), jnp.float32), 'cond': jax.random.normal(k1, (B, C), jnp.float32), 'norm_w': jax.random.normal(k2, (D, C), jnp.float32) * 0.02, 'up_w': jax.random.normal(k3, (2 * FF, D), jnp.float32) * 0.02, 'down_w': jax.random.normal(k4, (D, FF), jnp.float32) * 0.02}
    _L3_cond_all = _L3_cond_setup()
    _L3_cond_in = {k: v for k, v in _L3_cond_all.items() if k in ('norm_w', 'up_w', 'down_w')}
    del _L3_cond_all
    return {'x': x, 'cond_256': cond_256, 'L0_cond_weight': _L0_cond_in['weight'], 'L0_cond_bias': _L0_cond_in['bias'], 'L0_cond_lin_w': _L0_cond_in['lin_w'], 'L0_cond_lin_b': _L0_cond_in['lin_b'], 'L1_cond_attn_gamma_w': _L1_cond_in['attn_gamma_w'], 'L1_cond_attn_beta_w': _L1_cond_in['attn_beta_w'], 'L1_cond_W_q': _L1_cond_in['W_q'], 'L1_cond_W_k': _L1_cond_in['W_k'], 'L1_cond_W_v': _L1_cond_in['W_v'], 'L1_cond_W_o': _L1_cond_in['W_o'], 'L1_cond_attn_alpha_w': _L1_cond_in['attn_alpha_w'], 'L1_cond_ffn_gamma_w': _L1_cond_in['ffn_gamma_w'], 'L1_cond_ffn_beta_w': _L1_cond_in['ffn_beta_w'], 'L1_cond_gate_w': _L1_cond_in['gate_w'], 'L1_cond_hidden_w': _L1_cond_in['hidden_w'], 'L1_cond_out_w': _L1_cond_in['out_w'], 'L1_cond_out_b': _L1_cond_in['out_b'], 'L1_cond_ffn_alpha_w': _L1_cond_in['ffn_alpha_w'], 'L2_cond_Wd': _L2_cond_in['Wd'], 'L2_cond_bd': _L2_cond_in['bd'], 'L2_cond_Wu': _L2_cond_in['Wu'], 'L2_cond_bu': _L2_cond_in['bu'], 'L2_cond_Wdd': _L2_cond_in['Wdd'], 'L2_cond_bdd': _L2_cond_in['bdd'], 'L2_cond_Wdu': _L2_cond_in['Wdu'], 'L2_cond_bdu': _L2_cond_in['bdu'], 'L3_cond_norm_w': _L3_cond_in['norm_w'], 'L3_cond_up_w': _L3_cond_in['up_w'], 'L3_cond_down_w': _L3_cond_in['down_w']}

def reference(x, cond_256, L0_cond_weight, L0_cond_bias, L0_cond_lin_w, L0_cond_lin_b, L1_cond_attn_gamma_w, L1_cond_attn_beta_w, L1_cond_W_q, L1_cond_W_k, L1_cond_W_v, L1_cond_W_o, L1_cond_attn_alpha_w, L1_cond_ffn_gamma_w, L1_cond_ffn_beta_w, L1_cond_gate_w, L1_cond_hidden_w, L1_cond_out_w, L1_cond_out_b, L1_cond_ffn_alpha_w, L2_cond_Wd, L2_cond_bd, L2_cond_Wu, L2_cond_bu, L2_cond_Wdd, L2_cond_bdd, L2_cond_Wdu, L2_cond_bdu, L3_cond_norm_w, L3_cond_up_w, L3_cond_down_w):
    import jax
    import jax.numpy as jnp

    def _L0_cond_ref(input, convInfo, weight, bias, lin_w, lin_b):
        import jax, jax.numpy as jnp
        import numpy as np
        EPS = 1e-05
        mean = jnp.mean(input, axis=-1, keepdims=True)
        var = jnp.mean(jnp.square(input - mean), axis=-1, keepdims=True)
        out = (input - mean) * jax.lax.rsqrt(var + EPS) * weight + bias
        tar_bias = jnp.tanh(convInfo @ lin_w.T + lin_b)[:, None, :]
        out = out + tar_bias
        return out * weight + bias

    def _L1_cond_ref(x, t, attn_gamma_w, attn_beta_w, W_q, W_k, W_v, W_o, attn_alpha_w, ffn_gamma_w, ffn_beta_w, gate_w, hidden_w, out_w, out_b, ffn_alpha_w):
        import jax, jax.numpy as jnp
        import numpy as np
        from math import sqrt
        D_MODEL = 256
        N_HEADS = 16
        D_T = 64
        D_HID = 4 * D_MODEL
        EPS = 1e-06

        def _rmsnorm(x):
            return x * jax.lax.rsqrt(jnp.mean(x * x, axis=-1, keepdims=True) + EPS)

        def _ada_rmsnorm(x, t, gamma_w, beta_w):
            gamma = (t @ gamma_w.T)[:, None, :]
            beta = (t @ beta_w.T)[:, None, :]
            return gamma * _rmsnorm(x) + beta

        def _attention(x, W_q, W_k, W_v, W_o):
            b, l, dm = x.shape
            d_head = dm // N_HEADS
            scale = sqrt(N_HEADS / dm)

            def split(y):
                return y.reshape(b, l, N_HEADS, d_head).transpose(0, 2, 1, 3)
            q = split(x @ W_q.T)
            k = split(x @ W_k.T)
            v = split(x @ W_v.T)
            attn = jax.nn.softmax(scale * jnp.einsum('bnqd,bnkd->bnqk', q, k), axis=-1)
            o = jnp.einsum('bnqk,bnkd->bnqd', attn, v)
            o = o.transpose(0, 2, 1, 3).reshape(b, l, dm)
            return o @ W_o.T

        def _swiglu(x, gate_w, hidden_w, out_w, out_b):
            return jax.nn.silu(x @ gate_w.T) * (x @ hidden_w.T) @ out_w.T + out_b
        a_alpha = (t @ attn_alpha_w.T)[:, None, :]
        x = x + a_alpha * _attention(_ada_rmsnorm(x, t, attn_gamma_w, attn_beta_w), W_q, W_k, W_v, W_o)
        f_alpha = (t @ ffn_alpha_w.T)[:, None, :]
        return x + f_alpha * _swiglu(_ada_rmsnorm(x, t, ffn_gamma_w, ffn_beta_w), gate_w, hidden_w, out_w, out_b)

    def _L2_cond_ref(x, h_lang, Wd, bd, Wu, bu, Wdd, bdd, Wdu, bdu):
        import jax, jax.numpy as jnp
        import numpy as np
        DIM = 256
        BN = 128
        H = 64
        DELTA_SCALE = 0.1
        B, L, D = x.shape
        dWd = ((h_lang @ Wdd.T + bdd) * DELTA_SCALE).reshape(B, BN, D)
        dWu = ((h_lang @ Wdu.T + bdu) * DELTA_SCALE).reshape(B, D, BN)
        Wd_b = Wd + dWd
        Wu_b = Wu + dWu
        down = jax.nn.relu(jnp.einsum('bld,bnd->bln', x, Wd_b) + bd)
        up = jnp.einsum('bln,bdn->bld', down, Wu_b) + bu
        return x + up

    def _L3_cond_ref(x, cond, norm_w, up_w, down_w):
        import jax, jax.numpy as jnp
        import numpy as np
        EPS = 1e-06

        def act_quant(x):
            scale = 127.0 / jnp.clip(jnp.max(jnp.abs(x), axis=-1, keepdims=True), 1e-05, None)
            return jnp.clip(jnp.round(x * scale), -128.0, 127.0) / scale

        def weight_quant(w):
            scale = 1.0 / jnp.clip(jnp.mean(jnp.abs(w)), 1e-05, None)
            return jnp.clip(jnp.round(w * scale), -1.0, 1.0) / scale
        scale = cond @ norm_w.T + 1.0
        ms = jnp.mean(x * x, axis=-1, keepdims=True)
        h = x * (scale[:, None, :] * jax.lax.rsqrt(ms + EPS))
        u = h @ up_w.T
        val, gate = jnp.split(u, 2, axis=-1)
        h = val * jax.nn.gelu(gate, approximate=False)
        hq = h + jax.lax.stop_gradient(act_quant(h) - h)
        wq = down_w + jax.lax.stop_gradient(weight_quant(down_w) - down_w)
        y = hq @ wq.T
        return y + x
    x = _L0_cond_ref(x, cond_256, L0_cond_weight, L0_cond_bias, L0_cond_lin_w, L0_cond_lin_b)
    x = _L1_cond_ref(x, cond_256, L1_cond_attn_gamma_w, L1_cond_attn_beta_w, L1_cond_W_q, L1_cond_W_k, L1_cond_W_v, L1_cond_W_o, L1_cond_attn_alpha_w, L1_cond_ffn_gamma_w, L1_cond_ffn_beta_w, L1_cond_gate_w, L1_cond_hidden_w, L1_cond_out_w, L1_cond_out_b, L1_cond_ffn_alpha_w)
    x = _L2_cond_ref(x, cond_256, L2_cond_Wd, L2_cond_bd, L2_cond_Wu, L2_cond_bu, L2_cond_Wdd, L2_cond_bdd, L2_cond_Wdu, L2_cond_bdu)
    x = _L3_cond_ref(x, cond_256, L3_cond_norm_w, L3_cond_up_w, L3_cond_down_w)
    return x

_drawn_inputs = setup_inputs


def setup_inputs(seed=0):
    import zlib

    import numpy as np

    out = dict(_drawn_inputs(seed))
    spreads = {'L0_cond_weight': (1.0, 0.2), 'L0_cond_bias': (0.0, 0.1), 'L1_cond_out_b': (0.0, 2.0)}
    factors = {'L0_cond_lin_b': 8.0,
     'L1_cond_attn_gamma_w': 8.0,
     'L1_cond_attn_beta_w': 8.0,
     'L1_cond_W_q': 8.0,
     'L1_cond_W_k': 8.0,
     'L1_cond_W_v': 8.0,
     'L1_cond_W_o': 8.0,
     'L1_cond_attn_alpha_w': 8.0,
     'L1_cond_ffn_gamma_w': 8.0,
     'L1_cond_ffn_beta_w': 8.0,
     'L1_cond_gate_w': 8.0,
     'L1_cond_hidden_w': 8.0,
     'L1_cond_out_w': 8.0,
     'L1_cond_ffn_alpha_w': 5.076,
     'L2_cond_bd': 200.0,
     'L3_cond_norm_w': 8.0,
     'L3_cond_up_w': 3.816,
     'L3_cond_down_w': 3.811,
     'L2_cond_bu': 64.0}
    for name, (base, spread) in spreads.items():
        noise = np.random.default_rng([zlib.crc32(name.encode()), seed]).standard_normal(out[name].shape)
        drawn = base * np.exp(spread * noise) if base else spread * noise
        out[name] = jnp.asarray(drawn.astype(out[name].dtype))
    for name, factor in factors.items():
        out[name] = (out[name] * factor).astype(out[name].dtype)
    return out
```

```python
from contextlib import ExitStack

import concourse.bass as bass
from concourse import mybir

F32 = mybir.dt.float32
F32R = mybir.dt.float32r
BF16 = mybir.dt.bfloat16
ALU = mybir.AluOpType
ACT = mybir.ActivationFunctionType
AX = mybir.AxisListType

P = 128
SEQS, L, D, C = 32, 256, 256, 64
T = L // P
K = D // P
HEADS, DH = 16, 16
PAIRS = HEADS // 2
SLOT = 64
SHIFT_ROW = 3 * DH
HID = 1024
FT = HID // P
BN = 128
UNITS = 2 * BN + D
DELTA = 0.1
EPS_LN, EPS_RMS, EPS_Q = 1e-5, 1e-6, 1e-5
QMAX = 127.0
ROUND = 12582912.0
SCORE_SCALE = 0.25
KV_BUFS, P_BUFS = 4, 3
PASSES = ((0, 0), (0, 1), (1, 0))


def at(seq, per, n):
    reg, off = seq
    return off * per + n if reg is None else reg * per + (off * per + n)


def shifted(seq, by):
    return (seq[0], seq[1] + by)


def setup_block(nc, ctx, d, t):
    with ExitStack() as tmp:
        def sb(name, shape, dt=F32):
            return tmp.enter_context(nc.sbuf_tensor(name, shape, dt))

        def sem(name):
            return tmp.enter_context(nc.semaphore(name))

        BANK_UNITS, LOAD_BUFS, BANKS = 16, 4, 4
        HALF = 16
        stage_w = sb("stage_w", [P, 2, 2048])
        hload = sb("hload", [C + 1, LOAD_BUFS, BANK_UNITS * P])
        hbase = sb("hbase", [P, UNITS])
        hout = sb("hout", [P, 2, SEQS, P])
        cond1 = sb("cond1", [C + 1, SEQS])
        lin1 = sb("lin1", [C + 1, D])
        colw = sb("colw", [C, 5, D])
        roww = sb("roww", [C, 2, D])
        lnw = sb("lnw", [P, D])
        lnb = sb("lnb", [SEQS, D])
        outb = sb("outb", [SEQS, D])
        cols = sb("cols", [P, SEQS, 10])
        rows = sb("rows", [SEQS, 4, D])
        ones = sb("ones", [P, P])
        wsum = sb("wsum", [P, 1])
        wrec = sb("wrec", [P, 1])
        ps = tmp.enter_context(nc.psum_tensor("ps_setup", [P, 8, 512], F32))

        s_small = sem("small_loaded")
        s_w = sem("w_loaded")
        s_w2 = sem("w_loaded_odd")
        s_whi = sem("w_hi_ready")
        s_wlo = sem("w_lo_ready")
        s_h = [sem(f"h_loaded{n}") for n in range(LOAD_BUFS)]
        s_hmm = sem("h_product_ready")
        s_hev = sem("h_scaled")
        s_hst = [sem(f"h_stored{n}") for n in range(2)]
        s_ms = sem("constants_ready")
        s_cmm = sem("cond_products_ready")
        s_tanh = sem("tanh_ready")
        s_row = sem("row_steps")
        s_col = sem("col_steps")
        s_st = sem("cond_stored")
        s_abs = sem("down_abs_steps")
        s_sum = sem("down_sum_ready")
        s_dn = sem("down_quantised")

        def pieces():
            yield d["wqkv"].rearrange("(k p) n -> p k n", p=P), t["wqkv"], K, 768
            yield d["wo"].rearrange("(k p) n -> p k n", p=P), t["wo"], K, D
            for k in range(K):
                yield d["wgh"][k * P:(k + 1) * P, :].unsqueeze(1), [w[:, k:k + 1, :] for w in t["wgh"]], 1, 2 * HID
            yield d["wout"].rearrange("(k p) n -> p k n", p=P), t["wout"], FT, D
            for k in range(K):
                yield d["wup"][k * P:(k + 1) * P, :].unsqueeze(1), [w[:, k:k + 1, :] for w in t["wup"]], 1, 2 * HID

        PIECES = list(pieces())
        N_SMALL = 11

        block = tmp.enter_context(nc.Block())

        def staged(n, k, cols_):
            return stage_w[:, n % 2, 0:k * cols_].rearrange("p (k n) -> p k n", k=k)

        @block.sync
        def _(sp):
            for dst, src in ((cond1[0:C, :], d["condT"]), (lin1[:, :], d["lin"]), (colw[:, :, :], d["colw"]),
                             (roww[:, :, :], d["roww"]), (lnw[:, :], d["ln_w"].partition_broadcast(P)),
                             (lnb[:, :], d["ln_b"].partition_broadcast(SEQS)),
                             (outb[:, :], d["out_b"].partition_broadcast(SEQS)), (hbase[:, :], d["hbase"]),
                             (t["ident"][:, :], d["ident"]), (t["bd"][:, :], d["bd"]),
                             (t["bu"][:, :], d["bu"].partition_broadcast(P))):
                sp.dma_start(dst, src).then_inc(s_small, 16)
            for half in range(2):
                sp.sem_inc(s_hst[half], 16)
            with sp.Fori(0, 2) as r:
                for n in range(HALF):
                    sp.wait_ge(s_hmm, r * HALF + (n + 1))
                    sp.dma_start(hload[:, n % LOAD_BUFS, :],
                                 d["hyper"][:, r * HALF + n, :]).then_inc(s_h[n % LOAD_BUFS], 16)
                for half in range(2):
                    sp.wait_ge(s_hev, r * HALF + (BANKS + 8 * (half + 1)))
                    sp.dma_start(d["hyp"][:, :, r, half, :].rearrange("b p u -> p b u"),
                                 hout[:, half, :, :]).then_inc(s_hst[half], 16)
            sp.wait_ge(s_col, 2)
            sp.dma_start(d["cols"].rearrange("b p v -> p b v"), cols[:, :, :]).then_inc(s_st, 16)
            sp.wait_ge(s_row, 6)
            sp.dma_start(d["rows"], rows[:, :, :]).then_inc(s_st, 16)
            sp.wait_ge(s_st, 32)
            sp.wait_ge(s_hst[0], 3 * 16)
            sp.wait_ge(s_hst[1], 3 * 16)

        @block.scalar
        def _(act):
            act.dma_start(stage_w[:, 0, :].rearrange("p (k n) -> p k n", k=FT),
                          d["wdn"].rearrange("(k p) n -> p k n", p=P)).then_inc(s_w, 16)
            act.dma_start(staged(1, PIECES[0][2], PIECES[0][3]), PIECES[0][0]).then_inc(s_w2, 16)
            act.wait_ge(s_cmm, 1)
            nc.scalar.activation(rows[:, 0, :], ps[0:SEQS, 6, 0:D], ACT.Tanh).then_inc(s_tanh, 1)
            act.wait_ge(s_small, 16 * N_SMALL)
            nc.scalar.copy(t["ident_r"][:, :], t["ident"][:, :]).then_inc(s_ms, 1)
            nc.scalar.copy(t["ident_b"][:, :], t["ident"][:, :]).then_inc(s_ms, 1)
            for n, (src, tiles, k, cols_) in enumerate(PIECES):
                m = n + 1
                if m < len(PIECES):
                    if n >= 1:
                        act.wait_ge(s_wlo, n)
                    else:
                        act.wait_ge(s_dn, 3)
                    act.dma_start(staged(m + 1, PIECES[m][2], PIECES[m][3]),
                                  PIECES[m][0]).then_inc(s_w if (m + 1) % 2 == 0 else s_w2, 16)
                buf = (n + 1) % 2
                act.wait_ge(s_w2 if buf else s_w, 16 * (n // 2 + 1 + (0 if buf else 1)))
                nc.scalar.copy(tiles[0][:, 0:k, :], staged(buf, k, cols_)).then_inc(s_whi, 1)

        @block.vector
        def _(dve):
            dve.memset(ones[:, :], 1.0).then_inc(s_abs, 1)
            dve.memset(cond1[C:C + 1, :], 1.0).then_inc(s_abs, 1)
            wdn = stage_w[:, 0, :]
            dve.wait_ge(s_w, 16)
            dve.tensor_reduce(wsum[:, :], wdn, AX.X, ALU.add, apply_absolute_value=True).then_inc(s_abs, 1)
            dve.wait_ge(s_sum, 1)
            dve.tensor_scalar(t["wmean"][:, :], ps[:, 7, 0:1], 1.0 / (HID * D), EPS_Q, ALU.mult,
                              ALU.max).then_inc(s_abs, 1)
            dve.wait_ge(s_abs, 4)
            dve.reciprocal(wrec[:, :], t["wmean"][:, :]).then_inc(s_abs, 1)
            dve.wait_ge(s_abs, 5)
            dve.tensor_scalar(wdn, wdn, wrec[:, 0:1], ROUND, ALU.mult, ALU.add).then_inc(s_dn, 1)
            dve.wait_ge(s_dn, 1)
            dve.tensor_scalar(wdn, wdn, ROUND, 1.0, ALU.subtract, ALU.min).then_inc(s_dn, 1)
            dve.wait_ge(s_dn, 2)
            dve.tensor_scalar(t["wdq"][:, :, :], wdn.rearrange("p (k n) -> p k n", k=FT), -1.0, None,
                              ALU.max).then_inc(s_dn, 1)
            dve.wait_ge(s_cmm, 3)
            cps = ps[:, 4, 0:10 * SEQS].rearrange("p (v b) -> p v b", b=SEQS)
            cview = cols[:, :, :].rearrange("p b v -> p v b")
            dve.tensor_copy(cview[:, 0:8, :], cps[:, 0:8, :]).then_inc(s_col, 1)
            dve.tensor_scalar(cview[:, 8:10, :], cps[:, 8:10, :], 1.0, None, ALU.add).then_inc(s_col, 1)
            dve.wait_ge(s_small, 16 * N_SMALL)
            dve.tensor_copy(rows[:, 1:3, :], ps[0:SEQS, 5, :].rearrange("p (a n) -> p a n", a=2)).then_inc(s_row, 1)
            dve.wait_ge(s_tanh, 1)
            dve.tensor_tensor(rows[:, 0, :], rows[:, 0, :], lnb[:, :], ALU.add).then_inc(s_row, 1)
            dve.wait_ge(s_row, 2)
            dve.tensor_tensor(rows[:, 0, :], rows[:, 0, :], lnw[0:SEQS, :], ALU.mult).then_inc(s_row, 1)
            dve.wait_ge(s_row, 3)
            dve.tensor_tensor(rows[:, 0, :], rows[:, 0, :], lnb[:, :], ALU.add).then_inc(s_row, 1)
            dve.tensor_tensor(rows[:, 3, :], rows[:, 2, :], outb[:, :], ALU.mult).then_inc(s_row, 1)
            dve.tensor_tensor(t["w2"][:, :], lnw[:, :], lnw[:, :], ALU.mult).then_inc(s_row, 1)
            dve.tensor_scalar(t["wmean"][:, :], t["wmean"][:, :], 1.0 / QMAX, None, ALU.mult).then_inc(s_abs, 1)
            for n, (src, tiles, k, cols_) in enumerate(PIECES):
                dve.wait_ge(s_whi, n + 1)
                dve.tensor_tensor(tiles[1][:, 0:k, :], staged((n + 1) % 2, k, cols_), tiles[0][:, 0:k, :],
                                  ALU.subtract).then_inc(s_wlo, 1)
            dve.sem_inc(s_hev, BANKS)
            with dve.Fori(0, 2) as r:
                for n in range(HALF):
                    dve.wait_ge(s_hmm, r * HALF + (LOAD_BUFS + n + 1))
                    half, u = n // 8, (n % 8) * BANK_UNITS
                    dve.wait_ge(s_hst[half], r * 16 + 16)
                    base = hbase[:, bass.ds(r * 256 + n * BANK_UNITS, BANK_UNITS)]
                    dve.scalar_tensor_tensor(
                        out=hout[:, half, :, u:u + BANK_UNITS].rearrange("p b u -> p u b"),
                        in0=ps[:, n % BANKS, :].rearrange("p (u b) -> p u b", b=SEQS), scalar=DELTA,
                        in1=base.unsqueeze(2).to_broadcast([P, BANK_UNITS, SEQS]), op0=ALU.mult,
                        op1=ALU.add).then_inc(s_hev, 1)

        @block.tensor
        def _(pe):
            pe.wait_ge(s_small, 16 * N_SMALL)
            pe.wait_ge(s_abs, 2)
            pe.matmul(ps[0:SEQS, 6, 0:D], cond1[:, :], lin1[:, :], start=True, stop=True).then_inc(s_cmm, 1)
            pe.matmul(ps[0:SEQS, 5, :], cond1[0:C, :], roww[:, :, :], start=True, stop=True).then_inc(s_cmm, 1)
            for v in range(5):
                for k in range(K):
                    c = (2 * v + k) * SEQS
                    mm = pe.matmul(ps[:, 4, c:c + SEQS], colw[:, v, k * P:(k + 1) * P], cond1[0:C, :],
                                   start=True, stop=True)
            mm.then_inc(s_cmm, 1)
            pe.wait_ge(s_abs, 3)
            pe.matmul(ps[:, 7, 0:1], ones[:, :], wsum[:, :], start=True, stop=True).then_inc(s_sum, 1)
            pe.sem_inc(s_hmm, LOAD_BUFS)
            with pe.Fori(0, 2) as r:
                for n in range(HALF):
                    pe.wait_ge(s_h[n % LOAD_BUFS], r * (16 * (HALF // LOAD_BUFS)) + 16 * (n // LOAD_BUFS + 1))
                    pe.wait_ge(s_hev, r * HALF + (n + 1))
                    for u in range(BANK_UNITS):
                        mm = pe.matmul(ps[:, n % BANKS, u * SEQS:(u + 1) * SEQS],
                                       hload[:, n % LOAD_BUFS, u * P:(u + 1) * P], cond1[:, :], start=True, stop=True)
                    mm.then_inc(s_hmm, 1)


def main_block(nc, ctx, d, t):
    def sb(name, shape, dt=F32):
        return ctx.enter_context(nc.sbuf_tensor(name, shape, dt))

    def over(name, host, offset, shape, dt):
        return nc.alloc_sbuf_tensor_at(name, shape, dt, offset=nc.lookup_mloc(host).addr + offset)

    def sem(name):
        return ctx.enter_context(nc.semaphore(name))

    KB = 1024
    xin = sb("xin", [P, T, D])
    xf = sb("xf", [P, T, D])
    xc = sb("xc", [P, T, D])
    q_st = sb("q_st", [P, T, HEADS, SLOT], F32R)
    k_st = sb("k_st", [P, T, HEADS, SLOT], F32R)
    v_ext = sb("v_ext", [P, T, HEADS, 2 * DH])
    k_even = sb("k_even", [P, KV_BUFS, L], F32R)
    k_odd = sb("k_odd", [P, KV_BUFS, L], F32R)
    q_t = sb("q_t", [P, KV_BUFS, L], F32R)
    probs = sb("probs", [P, P_BUFS, 2, T, L])
    o_t = sb("o_t", [P, HEADS // 4, L])
    xr = sb("xr", [P, T, D])
    o_tok = over("o_tok", probs, 0, [P, T, HEADS, DH], F32)
    oh = over("oh", probs, 2 * KB, [P, K, L], F32R)
    ol = over("ol", probs, 4 * KB, [P, K, L], F32R)
    xt = over("xt", probs, 6 * KB, [P, K, L], F32)
    xh = over("xh", probs, 8 * KB, [P, K, L], F32R)
    xl = over("xl", probs, 10 * KB, [P, K, L], F32R)
    xs = sb("xs", [P, T, D])
    bs = sb("bs", [P, T, D])
    bt = sb("bt", [P, K, L])
    bh = sb("bh", [P, K, L], F32R)
    bl = sb("bl", [P, K, L], F32R)
    xb = sb("xb", [P, T, D])
    th = sb("th", [P, T, D])
    gp = sb("gp", [P, L])
    hf = sb("hf", [P, 2, L])
    hh = sb("hh", [P, FT, L], F32R)
    hl = sb("hl", [P, FT, L], F32R)
    x2 = sb("x2", [P, T, D])
    x3 = sb("x3", [P, T, D])
    hyp = sb("hyp", [P, UNITS])
    hq = sb("hq", [P, T, HID], BF16)
    zt = over("zt", gp, 0, [P, L], F32)
    h3 = over("h3", hl, 0, [P, T, HID], F32)
    ge = over("ge", hh, 0, [P, 2, 512], F32)
    hq_t = over("hq_t", hh, 4 * KB, [P, FT, L], BF16)
    c0 = sb("c0", [P, D])
    alpha = sb("alpha", [P, D])
    frow = sb("frow", [P, 2, D])
    col_a = sb("col_a", [P, 4])
    col_b = sb("col_b", [P, 6])
    stat = sb("stat", [P, T, 6])
    mv = sb("mv", [P, T, 3])
    v0 = sb("v0", [P, 4, T])
    r0 = sb("r0", [P, 4, T])
    ss = sb("ss", [P, 3, T])
    eps = sb("eps", [P, T])
    half = sb("half", [P, T])
    mx = sb("mx", [P, T, HEADS])
    rden = sb("rden", [P, T, HEADS])
    am = sb("am", [P, T])
    qs = sb("qs", [P, T])
    qi = sb("qi", [P, T])

    def bank(name, n):
        return ctx.enter_context(nc.psum_tensor(name, [P, n, 512], F32))

    S = bank("S", 2)
    ST = bank("ST", 2)
    TB = bank("TB", 1)
    OB = bank("OB", 1)
    M = bank("M", 2)
    M0, M1 = M[:, 0, :], M[:, 1, :]

    names = """x_loaded c0_loaded col_a_loaded alpha_loaded frow_loaded col_b_loaded hyp_loaded out_stored
        init_dve init_pool init_act stat_ready mean_steps mean_ready var0_ready rstd0_ready norm_steps w2_ready xf_ready ss1_ready
        var1_ready r1_ready xs_ready xt_full xt_ready xh_ready xl_ready qk_full qk_hi qk_lo v_full v_ready carried
        t_full kq_ready s_full max_ready shift_ready tm_full qm_ready st_full exp_ready pv_done ot_ready otok_full
        rden_ready otok_ready ont_full oh_ready ol_ready y_full y_ready xr_ready
        ss2_ready var2_ready r2_ready bs_ready xb_ready bt_full bt_ready bh_ready bl_ready gu_full th_ready gp_ready
        hf_ready hh_ready hl_ready f_full fy_ready x2_ready x2b_ready at_full at_ready z_full z_ready up_full x3_ready
        ss3_ready var3_ready r3_ready cs_ready ct_full ch_ready cl_ready gate_full ge_ready val_full h3_ready am_ready
        quant_steps hr_ready hq_ready hqt_full hqt_ready ly_full out_ready""".split()
    s = {n: sem(n) for n in names}

    block = ctx.enter_context(nc.Block())

    def run(iteration):
        def one(i, reg=None):
            here = (reg, i)
            flag = (lambda o: True) if reg is not None else (lambda o: 0 <= i + o < SEQS)
            iteration(here, flag(1), flag(0), flag(-1), flag(-2))
        return one

    def both(eng, iteration):
        one = run(iteration)
        for i in (-1, 0, 1):
            one(i)
        with eng.Fori(0, SEQS - 3) as r:
            one(2, r)
        for i in (SEQS - 1, SEQS, SEQS + 1):
            one(i)

    def rows_of(x):
        return x.rearrange("(p t) n -> p t n", t=T)

    @block.sync
    def _(sp):
        def index(seq):
            reg, off = seq
            return off if reg is None else reg + off

        def iteration(i, front, pairs, ffn, tail):
            a, b, c = shifted(i, 1), shifted(i, -1), shifted(i, -2)
            if ffn:
                sp.wait_ge(s["xb_ready"], at(b, 1, 0))
                sp.wait_ge(s["fy_ready"], at(b, 1, 0))
                sp.dma_start(frow[:, :, :], d["rows"][index(b), 2:4, :].partition_broadcast(P)
                             ).then_inc(s["frow_loaded"], 16)
            if front:
                sp.wait_ge(s["norm_steps"], at(a, 2, 0))
                sp.dma_start(xin[:, :, :], rows_of(d["x"][index(a)])).then_inc(s["x_loaded"], 16)
                sp.wait_ge(s["xf_ready"], at(a, 1, 0))
                sp.dma_start(c0[:, :], d["rows"][index(a), 0, :].partition_broadcast(P)
                             ).then_inc(s["c0_loaded"], 16)
                sp.wait_ge(s["xt_ready"], at(a, 2, 0))
                sp.dma_start(col_a[:, :], d["cols"][index(a), :, 0:4]).then_inc(s["col_a_loaded"], 16)
            if ffn:
                sp.wait_ge(s["cl_ready"], at(b, 2, 0))
                sp.dma_start(col_b[:, :], d["cols"][index(b), :, 4:10]).then_inc(s["col_b_loaded"], 16)
                sp.wait_ge(s["up_full"], at(b, 1, 0))
                sp.dma_start(hyp[:, :].rearrange("p (r h u) -> p r h u", r=2, h=2),
                             d["hyp"][index(b)]).then_inc(s["hyp_loaded"], 16)
            if pairs:
                sp.wait_ge(s["y_ready"], at(i, 1, 0))
                sp.dma_start(alpha[:, :], d["rows"][index(i), 1, :].partition_broadcast(P)
                             ).then_inc(s["alpha_loaded"], 16)
            if tail:
                sp.wait_ge(s["out_ready"], at(c, 2, 2))
                sp.dma_start(rows_of(d["out"][index(c)]), th[:, :, :]).then_inc(s["out_stored"], 16)

        both(sp, iteration)
        sp.wait_ge(s["out_stored"], 16 * SEQS)

    @block.tensor
    def _(pe):
        ident, ident_r, ident_b = t["ident"], t["ident_r"], t["ident_b"]

        def product(out, left, right, chunks, start=True, stop=True):
            for k in range(chunks):
                for n, (x, y) in enumerate(PASSES):
                    mm = pe.matmul(out, left(x, k), right(y, k), start=(start and k == 0 and n == 0),
                                   stop=(stop and k == chunks - 1 and n == len(PASSES) - 1))
            return mm

        def to_features(out, src):
            for k in range(K):
                for tt in range(T):
                    c = (k * T + tt) * P
                    mm = pe.transpose(out[:, c:c + P], src[:, tt, k * P:(k + 1) * P], ident[:, :])
            return mm

        xparts, bparts, oparts = (xh, xl), (bh, bl), (oh, ol)

        def pair_in(i, p):
            if p == 0:
                pe.wait_ge(s["qk_lo"], at(i, 4, 4))
                pe.wait_ge(s["v_ready"], at(i, 1, 1))
            elif p <= 2:
                pe.wait_ge(s["kq_ready"], at(i, 3 * PAIRS, 3 * p))
            else:
                pe.wait_ge(s["qm_ready"], at(i, PAIRS, p - 2))
            for c, st in ((0, k_st), (L, q_st)):
                for tt in range(T):
                    mm = pe.transpose(TB[:, 0, c + tt * P:c + (tt + 1) * P].bitcast(F32R),
                                      st[:, tt, 2 * p:2 * p + 2, :], ident_r[:, :])
            mm.then_inc(s["t_full"], 1)

        def scores(i, p):
            pe.wait_ge(s["kq_ready"], at(i, 3 * PAIRS, 3 * p + 3))
            if p >= 1:
                pe.wait_ge(s["max_ready"], at(i, PAIRS, p))
            for tt in range(T):
                for h, kk in enumerate((k_even, k_odd)):
                    mm = pe.matmul(S[:, tt, h * L:(h + 1) * L], q_t[:, p % KV_BUFS, tt * P:(tt + 1) * P],
                                   kk[:, p % KV_BUFS, :], start=True, stop=True)
            mm.then_inc(s["s_full"], 1)

        def pair_shift(i, p):
            pe.wait_ge(s["shift_ready"], at(i, PAIRS, p + 1))
            if p == 0:
                pe.wait_ge(s["kq_ready"], at(i, 3 * PAIRS, 9))
            elif p < PAIRS - 2:
                pe.wait_ge(s["kq_ready"], at(i, 3 * PAIRS, 3 * (p + 3)))
            else:
                pe.wait_ge(s["qm_ready"], at(i, PAIRS, p))
            for tt in range(T):
                mm = pe.transpose(TB[:, 0, tt * P:(tt + 1) * P].bitcast(F32R), q_st[:, tt, 2 * p:2 * p + 2, :],
                                  ident_r[:, :])
            mm.then_inc(s["tm_full"], 1)

        def key_scores(i, p):
            pe.wait_ge(s["qm_ready"], at(i, PAIRS, p + 1))
            if p >= 1:
                pe.wait_ge(s["exp_ready"], at(i, PAIRS, p))
            else:
                pe.wait_ge(s["ol_ready"], at(i, 1, 0))
            for h, kk in enumerate((k_even, k_odd)):
                for kb in range(T):
                    mm = pe.matmul(ST[:, h, kb * L:(kb + 1) * L], kk[:, p % KV_BUFS, kb * P:(kb + 1) * P],
                                   q_t[:, p % KV_BUFS, :], start=True, stop=True)
            mm.then_inc(s["st_full"], 1)

        def values(i, g):
            pe.wait_ge(s["exp_ready"], at(i, PAIRS, 2 * g + 2))
            if g == 0:
                pe.wait_ge(s["y_ready"], at(i, 1, 0))
            if g == 2:
                pe.wait_ge(s["ot_ready"], at(i, 2, 1))
            for kb in range(T):
                for j in range(4):
                    mm = pe.matmul(OB[32 * j:32 * j + 32, 0, (g % 2) * L:(g % 2 + 1) * L],
                                   v_ext[:, kb, 4 * g + j, :], probs[:, (2 * g + j // 2) % P_BUFS, j % 2, kb, :],
                                   start=(kb == 0), stop=(kb == T - 1))
            mm.then_inc(s["pv_done"], 1)

        def iteration(i, front, pairs, ffn, tail):
            a, b, c = shifted(i, 1), shifted(i, -1), shifted(i, -2)
            for slot in range(PAIRS + 4):
                if pairs and slot < PAIRS:
                    pair_in(i, slot)
                if tail and slot == 0:
                    for tt, bk in enumerate((M0, M1)):
                        pe.wait_ge(s["hq_ready"], at(c, 2, tt + 1))
                        if tt == 0:
                            pe.wait_ge(s["ge_ready"], at(c, 4, 4))
                        else:
                            pe.wait_ge(s["h3_ready"], at(c, 4, 4))
                        for f in range(FT):
                            mm = pe.transpose(bk.bitcast(BF16)[:, f * P:(f + 1) * P],
                                              hq[:, tt, f * P:(f + 1) * P], ident_b[:, :])
                        mm.then_inc(s["hqt_full"], 1)
                if tail and slot == 1:
                    pe.wait_ge(s["hqt_ready"], at(c, 2, 2))
                    for tt in range(T):
                        for f in range(FT):
                            mm = pe.matmul(M0[:, tt * D:(tt + 1) * D], hq_t[:, f, tt * P:(tt + 1) * P],
                                           t["wdq"][:, f, :], start=(f == 0), stop=(f == FT - 1))
                    mm.then_inc(s["ly_full"], 1)
                if pairs and 1 <= slot <= PAIRS:
                    scores(i, slot - 1)
                if ffn and slot == 2:
                    pe.wait_ge(s["bs_ready"], at(b, 2, 2))
                    pe.wait_ge(s["out_ready"], at(b, 2, 0))
                    to_features(M0, bs).then_inc(s["bt_full"], 1)
                if ffn and 3 <= slot < 3 + FT:
                    f = slot - 3
                    bk = (M1, M0)[f % 2]
                    if f == 0:
                        pe.wait_ge(s["bl_ready"], at(b, 1, 1))
                        pe.wait_ge(s["hqt_ready"], at(b, 2, 0))
                    if f >= 2:
                        pe.wait_ge(s["hf_ready"], at(b, FT, f - 1))
                    for g in range(2):
                        mm = product(bk[:, g * L:(g + 1) * L],
                                     lambda x, k: t["wgh"][x][:, k, g * HID + f * P:g * HID + (f + 1) * P],
                                     lambda y, k: bparts[y][:, k, :], K)
                    mm.then_inc(s["gu_full"], 1)
                if pairs and 2 <= slot < PAIRS + 2:
                    pair_shift(i, slot - 2)
                if pairs and 3 <= slot < PAIRS + 3:
                    key_scores(i, slot - 3)
                if pairs and slot >= 5 and slot % 2:
                    values(i, (slot - 5) // 2)
            if ffn:
                pe.wait_ge(s["hl_ready"], at(b, FT, FT))
                for tt in range(T):
                    mm = product(M1[:, tt * D:(tt + 1) * D], lambda x, k: (hh, hl)[x][:, k, tt * P:(tt + 1) * P],
                                 lambda y, k: t["wout"][y][:, k, :], FT)
                mm.then_inc(s["f_full"], 1)
            if pairs:
                pe.wait_ge(s["ot_ready"], at(i, 2, 2))
                pe.wait_ge(s["max_ready"], at(i, PAIRS, PAIRS))
                for tt in range(T):
                    for g in range(HEADS // 4):
                        mm = pe.transpose(S[:, tt, g * P:(g + 1) * P], o_t[:, g, tt * P:(tt + 1) * P], ident[:, :])
                    mm.then_inc(s["otok_full"], 1)
            if front:
                pe.wait_ge(s["xs_ready"], at(a, 2, 2))
                pe.wait_ge(s["qm_ready"], at(a, PAIRS, 0))
                to_features(TB[:, 0, :], xs).then_inc(s["xt_full"], 1)
            if ffn:
                pe.wait_ge(s["x2_ready"], at(b, 1, 1))
                to_features(M0, x2).then_inc(s["at_full"], 1)
            if pairs:
                pe.wait_ge(s["otok_ready"], at(i, 2, 2))
                pe.wait_ge(s["exp_ready"], at(i, PAIRS, PAIRS))
                to_features(ST[:, 0, :], o_tok[:, :, :, :].rearrange("p t h e -> p t (h e)")
                            ).then_inc(s["ont_full"], 1)

            def project(tt):
                mm = product(S[:, tt, :], lambda x, k: xparts[x][:, k, tt * P:(tt + 1) * P],
                             lambda y, k: t["wqkv"][y][:, k, 0:2 * D], K)
                mm.then_inc(s["qk_full"], 1)

            if front:
                pe.wait_ge(s["xl_ready"], at(a, 1, 1))
                pe.wait_ge(s["otok_ready"], at(a, 2, 0))
                project(0)
            if ffn:
                pe.wait_ge(s["at_ready"], at(b, 1, 1))
                pe.wait_ge(s["hyp_loaded"], at(b, 16, 16))
                for k in range(K):
                    mm = pe.matmul(M1[:, 0:L], hyp[:, k * BN:(k + 1) * BN], bt[:, k, :], start=(k == 0),
                                   stop=(k == K - 1))
                mm.then_inc(s["z_full"], 1)
            if front:
                project(1)
            if ffn:
                pe.wait_ge(s["z_ready"], at(b, 1, 1))
                for tt in range(T):
                    mm = pe.matmul(M0[:, tt * D:(tt + 1) * D], zt[:, tt * P:(tt + 1) * P], hyp[:, K * BN:UNITS],
                                   start=True, stop=True)
                mm.then_inc(s["up_full"], 1)
            if front:
                for tt in range(T):
                    mm = product(TB[:, 0, tt * D:(tt + 1) * D], lambda x, k: xparts[x][:, k, tt * P:(tt + 1) * P],
                                 lambda y, k: t["wqkv"][y][:, k, 2 * D:3 * D], K)
                mm.then_inc(s["v_full"], 1)
            if pairs:
                pe.wait_ge(s["ol_ready"], at(i, 1, 1))
                for tt in range(T):
                    mm = product(OB[:, 0, tt * D:(tt + 1) * D], lambda x, k: oparts[x][:, k, tt * P:(tt + 1) * P],
                                 lambda y, k: t["wo"][y][:, k, :], K)
                mm.then_inc(s["y_full"], 1)
            if ffn:
                pe.wait_ge(s["cs_ready"], at(b, 2, 2))
                to_features(M1, bs).then_inc(s["ct_full"], 1)
                for r in range(2 * T):
                    tt, n = r // 2, r % 2
                    if r == 0:
                        pe.wait_ge(s["cl_ready"], at(b, 2, 2))
                        pe.wait_ge(s["x3_ready"], at(b, 1, 1))
                    else:
                        pe.wait_ge(s["ge_ready"], at(b, 4, r))
                    product(M0, lambda x, k: bparts[x][:, k, tt * P:(tt + 1) * P],
                            lambda y, k: t["wup"][y][:, k, HID + n * 512:HID + (n + 1) * 512], K
                            ).then_inc(s["gate_full"], 1)
                    if r >= 1:
                        pe.wait_ge(s["h3_ready"], at(b, 4, r))
                    product(M1, lambda x, k: bparts[x][:, k, tt * P:(tt + 1) * P],
                            lambda y, k: t["wup"][y][:, k, n * 512:(n + 1) * 512], K).then_inc(s["val_full"], 1)

        pe.wait_ge(s["init_dve"], 5)
        pe.wait_ge(s["init_pool"], 2)
        both(pe, iteration)

    @block.scalar
    def _(act):
        A = nc.scalar.activation

        def square_sums(src, junk, which, ready):
            for tt in range(T):
                A(junk[:, tt, :], src[:, tt, :], ACT.Square, scale=D ** -0.5, accum_out=ss[:, which, tt:tt + 1]).then_inc(ready, 1)

        def iteration(i, front, pairs, ffn, tail):
            a, b, c = shifted(i, 1), shifted(i, -1), shifted(i, -2)
            for slot in range(PAIRS + 4):
                if pairs and slot < PAIRS:
                    p, buf = slot, slot % KV_BUFS
                    act.wait_ge(s["t_full"], at(i, PAIRS, p + 1))
                    for dst, src in ((k_even[0:SLOT, buf, :], TB[0:SLOT, 0, 0:L]),
                                     (k_odd[SLOT:P, buf, :], TB[SLOT:P, 0, 0:L]),
                                     (q_t[:, buf, :], TB[:, 0, L:2 * L])):
                        nc.scalar.copy(dst, src).then_inc(s["kq_ready"], 1)
                if tail and slot == 0:
                    for tt, bk in enumerate((M0, M1)):
                        act.wait_ge(s["hqt_full"], at(c, 2, tt + 1))
                        nc.scalar.copy(hq_t[:, :, tt * P:(tt + 1) * P],
                                       bk.bitcast(BF16).rearrange("p (f n) -> p f n", f=FT)
                                       ).then_inc(s["hqt_ready"], 1)
                if ffn and slot == 0:
                    act.wait_ge(s["xr_ready"], at(b, 1, 1))
                    act.wait_ge(s["ct_full"], at(b, 1, 0))
                    square_sums(xr, bs, 1, s["ss2_ready"])
                if pairs and slot == 1:
                    act.wait_ge(s["xf_ready"], at(i, 1, 1))
                    act.wait_ge(s["xr_ready"], at(i, 1, 0))
                    nc.scalar.copy(xc[:, :, :], xf[:, :, :]).then_inc(s["carried"], 1)
                if ffn and slot == 1:
                    act.wait_ge(s["r2_ready"], at(b, 1, 1))
                    act.wait_ge(s["ss2_ready"], at(b, 2, 2))
                    for tt in range(T):
                        A(bs[:, tt, :], xr[:, tt, :], ACT.Copy, scale=r0[:, 2, tt:tt + 1]
                          ).then_inc(s["bs_ready"], 1)
                if ffn and slot == 2:
                    act.wait_ge(s["bt_ready"], at(b, 2, 2))
                    nc.scalar.copy(bh[:, :, :], bt[:, :, :]).then_inc(s["bh_ready"], 1)
                if ffn and 3 <= slot < 3 + FT:
                    f = slot - 3
                    if f == 0:
                        act.wait_ge(s["out_stored"], at(b, 16, 0))
                    act.wait_ge(s["gu_full"], at(b, FT, f + 1))
                    A(th[:, f % 2, :], (M1, M0)[f % 2][:, 0:L], ACT.Tanh, scale=0.5).then_inc(s["th_ready"], 1)
                if pairs and 3 <= slot < PAIRS + 3:
                    p = slot - 3
                    act.wait_ge(s["st_full"], at(i, PAIRS, p + 1))
                    A(probs[:, p % P_BUFS, :, :, :].rearrange("p h k q -> p (h k q)"),
                      ST[:, :, :].rearrange("p h n -> p (h n)"), ACT.Exp, scale=SCORE_SCALE
                      ).then_inc(s["exp_ready"], 1)
                if ffn and 3 <= slot < 3 + FT:
                    act.wait_ge(s["hf_ready"], at(b, FT, f + 1))
                    nc.scalar.copy(hh[:, f, :], hf[:, f % 2, :]).then_inc(s["hh_ready"], 1)
                if front and slot == PAIRS + 2:
                    act.wait_ge(s["xf_ready"], at(a, 1, 1))
                    act.wait_ge(s["xt_full"], at(a, 1, 0))
                    square_sums(xf, xs, 0, s["ss1_ready"])
                if front and slot == PAIRS + 3:
                    act.wait_ge(s["r1_ready"], at(a, 1, 1))
                    act.wait_ge(s["ss1_ready"], at(a, 2, 2))
                    for tt in range(T):
                        A(xs[:, tt, :], xf[:, tt, :], ACT.Copy, scale=r0[:, 1, tt:tt + 1]
                          ).then_inc(s["xs_ready"], 1)
            if front:
                act.wait_ge(s["xt_ready"], at(a, 2, 2))
                nc.scalar.copy(xh[:, :, :], xt[:, :, :]).then_inc(s["xh_ready"], 1)
            if ffn:
                act.wait_ge(s["at_full"], at(b, 1, 1))
                nc.scalar.copy(bt[:, :, :].rearrange("p k n -> p (k n)"), M0).then_inc(s["at_ready"], 1)
            if pairs:
                act.wait_ge(s["ont_full"], at(i, 1, 1))
                nc.scalar.copy(oh[:, :, :].rearrange("p k n -> p (k n)"), ST[:, 0, :]).then_inc(s["oh_ready"], 1)

            def high_parts(tt):
                act.wait_ge(s["qk_full"], at(a, 2, tt + 1))
                src = S[:, tt, :].rearrange("p (o h e) -> p o h e", o=2, h=HEADS)
                q_dst = q_st[:, tt, :, 0:2 * DH].rearrange("p h (r e) -> p h r e", r=2)
                k_dst = k_st[:, tt, :, :].rearrange("p h (r e) -> p h r e", e=DH)[:, :, 0:3:2, :]
                nc.scalar.copy(q_dst, src[:, 0, :, :].unsqueeze(2).to_broadcast([P, HEADS, 2, DH])
                               ).then_inc(s["qk_hi"], 1)
                nc.scalar.copy(k_dst, src[:, 1, :, :].unsqueeze(2).to_broadcast([P, HEADS, 2, DH])
                               ).then_inc(s["qk_hi"], 1)

            if front:
                high_parts(0)
            if ffn:
                act.wait_ge(s["z_full"], at(b, 1, 1))
                A(zt[:, :], M1[:, 0:L], ACT.Relu, bias=t["bd"][:, 0:1]).then_inc(s["z_ready"], 1)
            if front:
                high_parts(1)
            if ffn:
                act.wait_ge(s["x3_ready"], at(b, 1, 1))
                square_sums(x3, bs, 2, s["ss3_ready"])
                act.wait_ge(s["r3_ready"], at(b, 1, 1))
                act.wait_ge(s["ss3_ready"], at(b, 2, 2))
                for tt in range(T):
                    A(bs[:, tt, :], x3[:, tt, :], ACT.Copy, scale=r0[:, 3, tt:tt + 1]).then_inc(s["cs_ready"], 1)
                act.wait_ge(s["ct_full"], at(b, 1, 1))
                for k in range(K):
                    A(bh[:, k, :], M1[:, k * L:(k + 1) * L], ACT.Copy, scale=col_b[:, 4 + k:5 + k]
                      ).then_inc(s["ch_ready"], 1)
                for r in range(2 * T):
                    act.wait_ge(s["gate_full"], at(b, 4, r + 1))
                    A(ge[:, r % 2, :], M0, ACT.Gelu).then_inc(s["ge_ready"], 1)

        both(act, iteration)

    @block.vector
    def _(dve):
        dve.memset(v_ext[:, :, :, :], 1.0).then_inc(s["init_dve"], 1)
        dve.memset(k_even[:, :, :].bitcast(F32), 0.0).then_inc(s["init_dve"], 1)
        dve.memset(k_odd[:, :, :].bitcast(F32), 0.0).then_inc(s["init_dve"], 1)
        dve.memset(half[:, :], -0.5).then_inc(s["init_dve"], 1)
        dve.memset(eps[:, :], EPS_RMS).then_inc(s["init_dve"], 1)
        dve.wait_ge(s["init_pool"], 2)

        def modulated(dst, src, col, ready):
            for k in range(K):
                dve.tensor_scalar(dst[:, k, :], src[:, k * L:(k + 1) * L], col[:, k:k + 1], col[:, 2 + k:3 + k],
                                  ALU.mult, ALU.add).then_inc(ready, 1)

        def iteration(i, front, pairs, ffn, tail):
            a, b, c = shifted(i, 1), shifted(i, -1), shifted(i, -2)

            def hidden_lo(f):
                dve.wait_ge(s["hh_ready"], at(b, FT, f + 1))
                dve.tensor_tensor(hl[:, f, :], hf[:, f % 2, :], hh[:, f, :], ALU.subtract
                                  ).then_inc(s["hl_ready"], 1)

            for slot in range(PAIRS + 4):
                if tail and slot == 1:
                    dve.wait_ge(s["ly_full"], at(c, 1, 1))
                    for tt in range(T):
                        dve.scalar_tensor_tensor(out=th[:, tt, :], in0=M0[:, tt * D:(tt + 1) * D],
                                                 scalar=qi[:, tt:tt + 1], in1=x3[:, tt, :], op0=ALU.mult,
                                                 op1=ALU.add).then_inc(s["out_ready"], 1)
                if ffn and 4 <= slot < 4 + FT:
                    hidden_lo(slot - 4)
                if pairs and 1 <= slot <= PAIRS:
                    p = slot - 1
                    dve.wait_ge(s["s_full"], at(i, PAIRS, p + 1))
                    dve.tensor_reduce(mx[:, :, 2 * p:2 * p + 2], S[:, :, :].rearrange("p t (h n) -> p t h n", h=2),
                                      AX.X, ALU.max).then_inc(s["max_ready"], 1)
                    dve.wait_ge(s["max_ready"], at(i, PAIRS, p + 1))
                    dve.tensor_scalar(q_st[:, :, 2 * p:2 * p + 2, SHIFT_ROW], mx[:, :, 2 * p:2 * p + 2], -1.0,
                                      None, ALU.mult).then_inc(s["shift_ready"], 1)
                if ffn and slot == 2:
                    dve.wait_ge(s["bt_full"], at(b, 1, 1))
                    dve.wait_ge(s["col_b_loaded"], at(b, 16, 16))
                    modulated(bt, M0, col_b, s["bt_ready"])
                if pairs and 2 <= slot < PAIRS + 2:
                    p = slot - 2
                    dve.wait_ge(s["tm_full"], at(i, PAIRS, p + 1))
                    dve.tensor_copy(q_t[:, p % KV_BUFS, :], TB[:, 0, 0:L]).then_inc(s["qm_ready"], 1)
                if ffn and slot == 2:
                    dve.wait_ge(s["bh_ready"], at(b, 1, 1))
                    dve.tensor_tensor(bl[:, :, :], bt[:, :, :], bh[:, :, :], ALU.subtract
                                      ).then_inc(s["bl_ready"], 1)
                if ffn and 3 <= slot < 3 + FT:
                    f = slot - 3
                    bk = (M1, M0)[f % 2]
                    dve.wait_ge(s["th_ready"], at(b, FT, f + 1))
                    dve.scalar_tensor_tensor(out=gp[:, :], in0=th[:, f % 2, :], scalar=1.0, in1=bk[:, 0:L],
                                             op0=ALU.add, op1=ALU.mult).then_inc(s["gp_ready"], 1)
                    dve.wait_ge(s["gp_ready"], at(b, FT, f + 1))
                    dve.scalar_tensor_tensor(out=hf[:, f % 2, :], in0=gp[:, :], scalar=0.5, in1=bk[:, L:2 * L],
                                             op0=ALU.mult, op1=ALU.mult).then_inc(s["hf_ready"], 1)
                if pairs and slot in (7, 11):
                    n = (slot - 7) // 4
                    dve.wait_ge(s["pv_done"], at(i, 4, 2 * n + 2))
                    dve.tensor_copy(o_t[:, 2 * n:2 * n + 2, :].rearrange("p g n -> p (g n)"), OB[:, 0, :]
                                    ).then_inc(s["ot_ready"], 1)
                if front and slot == PAIRS:
                    dve.wait_ge(s["x_loaded"], at(a, 16, 16))
                    for tt in range(T):
                        dve.bn_stats(stat[:, tt, :], xin[:, tt, :]).then_inc(s["stat_ready"], 1)
                    dve.wait_ge(s["stat_ready"], at(a, 2, 2))
                    for n, (j, op) in enumerate(((1, ALU.add), (1, ALU.subtract), (2, ALU.add))):
                        dve.tensor_tensor(mv[:, :, n], stat[:, :, j], stat[:, :, j + 3], op
                                          ).then_inc(s["mean_steps"], 1)
                    dve.wait_ge(s["mean_steps"], at(a, 5, 3))
                    dve.tensor_tensor(mv[:, :, 1], mv[:, :, 1], mv[:, :, 1], ALU.mult
                                      ).then_inc(s["mean_steps"], 1)
                    dve.tensor_scalar(mv[:, :, 0], mv[:, :, 0], 0.5, None, ALU.mult
                                      ).then_inc(s["mean_ready"], 1)
                    dve.wait_ge(s["mean_steps"], at(a, 5, 4))
                    dve.scalar_tensor_tensor(out=mv[:, :, 2], in0=mv[:, :, 1], scalar=D / 4.0, in1=mv[:, :, 2],
                                             op0=ALU.mult, op1=ALU.add).then_inc(s["mean_steps"], 1)
                    dve.wait_ge(s["mean_steps"], at(a, 5, 5))
                    dve.tensor_scalar(v0[:, 0, :], mv[:, :, 2], 1.0 / D, EPS_LN, ALU.mult, ALU.add
                                      ).then_inc(s["var0_ready"], 1)
                if front and slot == PAIRS + 1:
                    dve.wait_ge(s["rstd0_ready"], at(a, 1, 1))
                    dve.wait_ge(s["mean_ready"], at(a, 1, 1))
                    dve.wait_ge(s["carried"], at(a, 1, 0))
                    dve.wait_ge(s["xs_ready"], at(a, 2, 0))
                    for tt in range(T):
                        dve.tensor_scalar(xf[:, tt, :], xin[:, tt, :], mv[:, tt, 0:1], r0[:, 0, tt:tt + 1],
                                          ALU.subtract, ALU.mult).then_inc(s["norm_steps"], 1)
                    dve.wait_ge(s["norm_steps"], at(a, 2, 2))
                    dve.tensor_tensor(xf[:, :, :], xf[:, :, :], t["w2"][:, :].unsqueeze(1).to_broadcast([P, T, D]),
                                      ALU.mult).then_inc(s["w2_ready"], 1)
                    dve.wait_ge(s["w2_ready"], at(a, 1, 1))
                    dve.wait_ge(s["c0_loaded"], at(a, 16, 16))
                    dve.tensor_tensor(xf[:, :, :], xf[:, :, :], c0[:, :].unsqueeze(1).to_broadcast([P, T, D]),
                                      ALU.add).then_inc(s["xf_ready"], 1)
            if ffn:
                dve.wait_ge(s["f_full"], at(b, 1, 1))
                dve.wait_ge(s["frow_loaded"], at(b, 16, 16))
                dve.tensor_tensor(hf[:, :, :], M1.rearrange("p (t n) -> p t n", t=T),
                                  frow[:, 0, :].unsqueeze(1).to_broadcast([P, T, D]), ALU.mult
                                  ).then_inc(s["fy_ready"], 1)
                dve.wait_ge(s["fy_ready"], at(b, 1, 1))
                dve.wait_ge(s["xb_ready"], at(b, 1, 1))
                dve.tensor_tensor(x2[:, :, :], xb[:, :, :], hf[:, :, :], ALU.add).then_inc(s["x2_ready"], 1)
            if pairs:
                for tt in range(T):
                    dve.wait_ge(s["otok_full"], at(i, 2, tt + 1))
                    src = S[:, tt, :].rearrange("p (h e) -> p h e", e=2 * DH)
                    dve.reciprocal(rden[:, tt, :], src[:, :, DH]).then_inc(s["rden_ready"], 1)
                    dve.wait_ge(s["rden_ready"], at(i, 2, tt + 1))
                    dve.tensor_tensor(o_tok[:, tt, :, :], src[:, :, 0:DH],
                                      rden[:, tt, :].unsqueeze(2).to_broadcast([P, HEADS, DH]), ALU.mult
                                      ).then_inc(s["otok_ready"], 1)
            if front:
                dve.wait_ge(s["xt_full"], at(a, 1, 1))
                dve.wait_ge(s["col_a_loaded"], at(a, 16, 16))
                modulated(xt, TB[:, 0, :], col_a, s["xt_ready"])
                dve.wait_ge(s["xh_ready"], at(a, 1, 1))
                dve.tensor_tensor(xl[:, :, :], xt[:, :, :], xh[:, :, :], ALU.subtract).then_inc(s["xl_ready"], 1)
            if pairs:
                dve.wait_ge(s["oh_ready"], at(i, 1, 1))
                dve.tensor_tensor(ol[:, :, :].rearrange("p k n -> p (k n)"), ST[:, 0, :],
                                  oh[:, :, :].rearrange("p k n -> p (k n)"), ALU.subtract
                                  ).then_inc(s["ol_ready"], 1)

            def low_parts(tt):
                dve.wait_ge(s["qk_hi"], at(a, 4, 2 * tt + 2))
                dve.memset(q_st[:, tt, :, SHIFT_ROW:SHIFT_ROW + 1].bitcast(F32), 0.0)
                src = S[:, tt, :].rearrange("p (o h e) -> p o h e", o=2, h=HEADS)
                dve.tensor_tensor(q_st[:, tt, :, 2 * DH:3 * DH], src[:, 0, :, :], q_st[:, tt, :, 0:DH],
                                  ALU.subtract).then_inc(s["qk_lo"], 1)
                dve.tensor_tensor(k_st[:, tt, :, DH:2 * DH], src[:, 1, :, :], k_st[:, tt, :, 0:DH],
                                  ALU.subtract).then_inc(s["qk_lo"], 1)

            if front:
                low_parts(0)
                low_parts(1)
            if ffn:
                dve.wait_ge(s["up_full"], at(b, 1, 1))
                dve.wait_ge(s["x2b_ready"], at(b, 1, 1))
                dve.tensor_tensor(x3[:, :, :].rearrange("p t n -> p (t n)"), M0,
                                  xb[:, :, :].rearrange("p t n -> p (t n)"), ALU.add).then_inc(s["x3_ready"], 1)
            if front:
                dve.wait_ge(s["v_full"], at(a, 1, 1))
                dve.tensor_copy(v_ext[:, :, :, 0:DH],
                                TB[:, 0, :].rearrange("p (t h e) -> p t h e", t=T, h=HEADS)
                                ).then_inc(s["v_ready"], 1)
            if pairs:
                dve.wait_ge(s["y_full"], at(i, 1, 1))
                dve.wait_ge(s["alpha_loaded"], at(i, 16, 16))
                dve.tensor_tensor(hf[:, :, :], OB[:, 0, :].rearrange("p (t n) -> p t n", t=T),
                                  alpha[:, :].unsqueeze(1).to_broadcast([P, T, D]), ALU.mult
                                  ).then_inc(s["y_ready"], 1)
                dve.wait_ge(s["y_ready"], at(i, 1, 1))
                dve.wait_ge(s["carried"], at(i, 1, 1))
                dve.tensor_tensor(xr[:, :, :], xc[:, :, :], hf[:, :, :], ALU.add).then_inc(s["xr_ready"], 1)
            if ffn:
                for k in range(K):
                    dve.wait_ge(s["ch_ready"], at(b, 2, 2))
                    dve.scalar_tensor_tensor(out=bl[:, k, :], in0=M1[:, k * L:(k + 1) * L],
                                             scalar=col_b[:, 4 + k:5 + k], in1=bh[:, k, :], op0=ALU.mult,
                                             op1=ALU.subtract).then_inc(s["cl_ready"], 1)

                def gated(r):
                    tt, n = r // 2, r % 2
                    dve.wait_ge(s["val_full"], at(b, 4, r + 1))
                    dve.wait_ge(s["ge_ready"], at(b, 4, r + 1))
                    dve.tensor_tensor(h3[:, tt, n * 512:(n + 1) * 512], ge[:, r % 2, :], M1, ALU.mult
                                      ).then_inc(s["h3_ready"], 1)

                def quantise(tt):
                    dve.wait_ge(s["h3_ready"], at(b, 4, 2 * tt + 2))
                    dve.tensor_reduce(am[:, tt:tt + 1], h3[:, tt, :], AX.X, ALU.max, apply_absolute_value=True
                                      ).then_inc(s["am_ready"], 1)
                    dve.wait_ge(s["am_ready"], at(b, 2, tt + 1))
                    dve.tensor_scalar(am[:, tt:tt + 1], am[:, tt:tt + 1], EPS_Q, None, ALU.max
                                      ).then_inc(s["quant_steps"], 1)
                    dve.wait_ge(s["quant_steps"], at(b, 8, 4 * tt + 1))
                    dve.reciprocal(qs[:, tt:tt + 1], am[:, tt:tt + 1]).then_inc(s["quant_steps"], 1)
                    dve.tensor_scalar(qi[:, tt:tt + 1], am[:, tt:tt + 1], t["wmean"][:, 0:1], None, ALU.mult
                                      ).then_inc(s["quant_steps"], 1)
                    dve.wait_ge(s["quant_steps"], at(b, 8, 4 * tt + 2))
                    dve.tensor_scalar(qs[:, tt:tt + 1], qs[:, tt:tt + 1], QMAX, None, ALU.mult
                                      ).then_inc(s["quant_steps"], 1)
                    dve.wait_ge(s["quant_steps"], at(b, 8, 4 * tt + 4))
                    dve.tensor_scalar(h3[:, tt, :], h3[:, tt, :], qs[:, tt:tt + 1], ROUND, ALU.mult, ALU.add
                                      ).then_inc(s["hr_ready"], 1)
                    dve.wait_ge(s["hr_ready"], at(b, 2, tt + 1))
                    dve.tensor_scalar(hq[:, tt, :], h3[:, tt, :], ROUND, QMAX, ALU.subtract, ALU.min
                                      ).then_inc(s["hq_ready"], 1)

                gated(0)
                gated(1)
                gated(2)
                quantise(0)
                gated(3)
                quantise(1)

        both(dve, iteration)

    @block.gpsimd
    def _(pool):
        pool.memset(q_st[:, :, :, :].bitcast(F32), 0.0).then_inc(s["init_pool"], 1)
        pool.memset(k_st[:, :, :, :].bitcast(F32), 1.0).then_inc(s["init_pool"], 1)
        pool.wait_ge(s["init_dve"], 5)

        def inverse_root(which, ready):
            pool.tensor_tensor(r0[:, which, :], v0[:, which, :], half[:, :], ALU.pow).then_inc(ready, 1)

        def rms(which, step, ready, seq):
            pool.tensor_tensor(v0[:, which, :], ss[:, which - 1, :], eps[:, :], ALU.add).then_inc(step, 1)
            pool.wait_ge(step, at(seq, 1, 1))
            inverse_root(which, ready)

        def iteration(i, front, pairs, ffn, tail):
            a, b = shifted(i, 1), shifted(i, -1)
            if ffn:
                pool.wait_ge(s["ss2_ready"], at(b, 2, 2))
                rms(2, s["var2_ready"], s["r2_ready"], b)
                pool.wait_ge(s["frow_loaded"], at(b, 16, 16))
                pool.wait_ge(s["xr_ready"], at(b, 1, 1))
                pool.wait_ge(s["x3_ready"], at(b, 1, 0))
                pool.tensor_tensor(xb[:, :, :], xr[:, :, :], frow[:, 1, :].unsqueeze(1).to_broadcast([P, T, D]),
                                   ALU.add).then_inc(s["xb_ready"], 1)
            if front:
                pool.wait_ge(s["var0_ready"], at(a, 1, 1))
                inverse_root(0, s["rstd0_ready"])
                pool.wait_ge(s["ss1_ready"], at(a, 2, 2))
                rms(1, s["var1_ready"], s["r1_ready"], a)
            if ffn:
                pool.wait_ge(s["x2_ready"], at(b, 1, 1))
                pool.tensor_tensor(xb[:, :, :], x2[:, :, :], t["bu"][:, :].unsqueeze(1).to_broadcast([P, T, D]),
                                   ALU.add).then_inc(s["x2b_ready"], 1)
                pool.wait_ge(s["ss3_ready"], at(b, 2, 2))
                rms(3, s["var3_ready"], s["r3_ready"], b)

        both(pool, iteration)


def build(nc, x, condT, ln_w, ln_b, lin, colw, roww, out_b, wqkv, wo, wgh, wout, wup, wdn, hyper, hbase, bd, bu,
          ident, out):
    d = dict(x=x, condT=condT, ln_w=ln_w, ln_b=ln_b, lin=lin, colw=colw, roww=roww, out_b=out_b, wqkv=wqkv, wo=wo,
             wgh=wgh, wout=wout, wup=wup, wdn=wdn, hyper=hyper, hbase=hbase, bd=bd, bu=bu, ident=ident, out=out)
    d["hyp"] = nc.dram_tensor("hyp_scratch", (SEQS, P, 2, 2, P), F32).ap()
    d["cols"] = nc.dram_tensor("cols_scratch", (SEQS, P, 10), F32).ap()
    d["rows"] = nc.dram_tensor("rows_scratch", (SEQS, 4, D), F32).ap()
    with ExitStack() as ctx:
        def sb(name, shape, dt=F32):
            return ctx.enter_context(nc.sbuf_tensor(name, shape, dt))

        def split(name, shape):
            return [sb(f"{name}_hi", shape, F32R), sb(f"{name}_lo", shape, F32R)]

        t = {
            "wqkv": split("wqkv", [P, K, 3 * D]), "wo": split("wo", [P, K, D]), "wgh": split("wgh", [P, K, 2 * HID]),
            "wout": split("wout", [P, FT, D]), "wup": split("wup", [P, K, 2 * HID]),
            "wdq": sb("wdq", [P, FT, D], BF16), "ident": sb("ident", [P, P]), "ident_r": sb("ident_r", [P, P], F32R),
            "ident_b": sb("ident_b", [P, P], BF16), "w2": sb("w2", [P, D]), "bu": sb("bu", [P, D]),
            "bd": sb("bd", [P, 1]), "wmean": sb("wmean", [P, 1]),
        }
        setup_block(nc, ctx, d, t)
        main_block(nc, ctx, d, t)


def kernel(**inputs):
    import numpy as _np
    import concourse.bacc as _bacc
    from concourse import mybir as _mybir
    from concourse.bass_utils import run_bass_kernel_spmd as _run

    a = {n: _np.asarray(v) for n, v in inputs.items()}
    L1, L2 = "L1_cond_", "L2_cond_"
    down_w = _np.concatenate([a[L2 + "Wdd"].T, a[L2 + "bdd"][None, :]])
    down_w = down_w.reshape(C + 1, BN, K, P).transpose(0, 2, 1, 3).reshape(C + 1, -1)
    up_w = _np.concatenate([a[L2 + "Wdu"].T, a[L2 + "bdu"][None, :]])
    base = a[L2 + "Wd"].T.reshape(K, P, BN).transpose(1, 0, 2).reshape(P, K * BN)
    arrays = {
        "x": a["x"], "condT": a["cond_256"].T, "ln_w": a["L0_cond_weight"], "ln_b": a["L0_cond_bias"],
        "lin": _np.concatenate([a["L0_cond_lin_w"].T, a["L0_cond_lin_b"][None, :]]),
        "colw": _np.stack([a[n].T for n in (L1 + "attn_gamma_w", L1 + "attn_beta_w", L1 + "ffn_gamma_w",
                                            L1 + "ffn_beta_w", "L3_cond_norm_w")], axis=1),
        "roww": _np.stack([a[L1 + "attn_alpha_w"].T, a[L1 + "ffn_alpha_w"].T], axis=1),
        "out_b": a[L1 + "out_b"],
        "wqkv": _np.concatenate([a[L1 + "W_q"].T, a[L1 + "W_k"].T, a[L1 + "W_v"].T], axis=1),
        "wo": a[L1 + "W_o"].T, "wgh": _np.concatenate([a[L1 + "gate_w"].T, a[L1 + "hidden_w"].T], axis=1),
        "wout": a[L1 + "out_w"].T, "wup": a["L3_cond_up_w"].T, "wdn": a["L3_cond_down_w"].T,
        "hyper": _np.concatenate([down_w, up_w], axis=1).reshape(C + 1, 2 * 16, 16 * P),
        "hbase": _np.concatenate([base, a[L2 + "Wu"].T], axis=1),
        "bd": a[L2 + "bd"][:, None], "bu": a[L2 + "bu"], "ident": _np.eye(P, dtype=_np.float32),
    }
    arrays = {n: _np.ascontiguousarray(v) for n, v in arrays.items()}
    nc = _bacc.Bacc("TRN2", target_bir_lowering=False, num_devices=1)
    aps = {n: nc.dram_tensor(f"in_{n}", v.shape, _mybir.dt.from_np(v.dtype), kind="ExternalInput").ap()
           for n, v in arrays.items()}
    out = nc.dram_tensor("out_0", (SEQS, L, D), _mybir.dt.float32, kind="ExternalOutput").ap()
    build(nc, out=out, **aps)
    r = _run(nc, [{f"in_{n}": v for n, v in arrays.items()}], core_ids=[0])
    return r.results[0]["out_0"]
```

```python
from contextlib import ExitStack

import concourse.bass as bass
from concourse import mybir

F32 = mybir.dt.float32
F32R = mybir.dt.float32r
BF16 = mybir.dt.bfloat16
ALU = mybir.AluOpType
ACT = mybir.ActivationFunctionType
AX = mybir.AxisListType

P = 128
SEQS, L, D, C = 32, 256, 256, 64
T = L // P
K = D // P
HEADS, DH = 16, 16
PAIRS = HEADS // 2
SLOT = 64
SHIFT_ROW = 3 * DH
HID = 1024
FT = HID // P
BN = 128
UNITS = 2 * BN + D
DELTA = 0.1
EPS_LN, EPS_RMS, EPS_Q = 1e-5, 1e-6, 1e-5
QMAX = 127.0
ROUND = 12582912.0
SCORE_SCALE = 0.25
KV_BUFS, P_BUFS = 4, 3
PASSES = ((0, 0), (0, 1), (1, 0))


def at(seq, per, n):
    reg, off = seq
    return off * per + n if reg is None else reg * per + (off * per + n)


def shifted(seq, by):
    return (seq[0], seq[1] + by)


def setup_block(nc, ctx, d, t):
    with ExitStack() as tmp:
        def sb(name, shape, dt=F32):
            return tmp.enter_context(nc.sbuf_tensor(name, shape, dt))

        def sem(name):
            return tmp.enter_context(nc.semaphore(name))

        LOAD_BUFS, BANKS = 4, 4
        SIDES = P // SEQS
        FILLS = P // SIDES
        TURN = 2 * BANKS
        stage_w = sb("stage_w", [P, 2, 2048])
        hload = sb("hload", [C + 2, LOAD_BUFS, SIDES, UNITS])
        hout = sb("hout", [P, 2, BANKS, UNITS])
        cond2 = sb("cond2", [C + 2, SEQS])
        cond1 = sb("cond1", [C + 1, SEQS])
        lin1 = sb("lin1", [C + 1, D])
        colw = sb("colw", [C, 5, D])
        roww = sb("roww", [C, 2, D])
        lnw = sb("lnw", [P, D])
        lnb = sb("lnb", [SEQS, D])
        outb = sb("outb", [SEQS, D])
        cols = sb("cols", [P, SEQS, 10])
        rows = sb("rows", [SEQS, 4, D])
        ones = sb("ones", [P, P])
        wsum = sb("wsum", [P, 1])
        wrec = sb("wrec", [P, 1])
        ps = tmp.enter_context(nc.psum_tensor("ps_setup", [P, 8, 512], F32))

        s_small = sem("small_loaded")
        s_w = sem("w_loaded")
        s_w2 = sem("w_loaded_odd")
        s_whi = sem("w_hi_ready")
        s_wlo = sem("w_lo_ready")
        s_h = [sem(f"h_loaded{n}") for n in range(LOAD_BUFS)]
        s_c2 = sem("scaled_cond_steps")
        s_hmm = sem("h_product_ready")
        s_hev = sem("h_scaled")
        s_hst = [sem(f"h_stored{n}") for n in range(2)]
        s_ms = sem("constants_ready")
        s_cmm = sem("cond_products_ready")
        s_tanh = sem("tanh_ready")
        s_row = sem("row_steps")
        s_col = sem("col_steps")
        s_st = sem("cond_stored")
        s_abs = sem("down_abs_steps")
        s_sum = sem("down_sum_ready")
        s_dn = sem("down_quantised")

        def pieces():
            yield d["wqkv"].rearrange("(k p) n -> p k n", p=P), t["wqkv"], K, 768
            yield d["wo"].rearrange("(k p) n -> p k n", p=P), t["wo"], K, D
            for k in range(K):
                yield d["wgh"][k * P:(k + 1) * P, :].unsqueeze(1), [w[:, k:k + 1, :] for w in t["wgh"]], 1, 2 * HID
            yield d["wout"].rearrange("(k p) n -> p k n", p=P), t["wout"], FT, D
            for k in range(K):
                yield d["wup"][k * P:(k + 1) * P, :].unsqueeze(1), [w[:, k:k + 1, :] for w in t["wup"]], 1, 2 * HID

        PIECES = list(pieces())
        N_SMALL = 10

        block = tmp.enter_context(nc.Block())

        def staged(n, k, cols_):
            return stage_w[:, n % 2, 0:k * cols_].rearrange("p (k n) -> p k n", k=k)

        @block.sync
        def _(sp):
            for dst, src in ((cond1[0:C, :], d["condT"]), (lin1[:, :], d["lin"]), (colw[:, :, :], d["colw"]),
                             (roww[:, :, :], d["roww"]), (lnw[:, :], d["ln_w"].partition_broadcast(P)),
                             (lnb[:, :], d["ln_b"].partition_broadcast(SEQS)),
                             (outb[:, :], d["out_b"].partition_broadcast(SEQS)),
                             (t["ident"][:, :], d["ident"]), (t["bd"][:, :], d["bd"]),
                             (t["bu"][:, :], d["bu"].partition_broadcast(P))):
                sp.dma_start(dst, src).then_inc(s_small, 16)
            for half in range(2):
                sp.sem_inc(s_hst[half], 16)

            def load(n, first=0):
                sp.wait_ge(s_hmm, first + (n + 1))
                sp.dma_start(hload[:, n % LOAD_BUFS, :, :], d["hyper"][:, first + n, :, :]
                             ).then_inc(s_h[n % LOAD_BUFS], 16)

            def turn(first, q, loads):
                for n in range(1, loads + 1):
                    load(n, first)
                    if n == BANKS:
                        store(first, q, 0)
                store(first, q, 1)

            def store(first, q, half):
                sp.wait_ge(s_hev, first + (BANKS + BANKS * (half + 1)))
                for j in range(SIDES):
                    sp.dma_start(d["hyp"][:, j, q, half, :, :],
                                 hout[j * SEQS:(j + 1) * SEQS, half, :, :]).then_inc(s_hst[half], 16)

            load(0)
            with sp.Fori(0, FILLS // TURN - 1) as r:
                turn(r * TURN, r, TURN)
            turn(FILLS - TURN, FILLS // TURN - 1, TURN - 1)
            sp.wait_ge(s_col, 2)
            sp.dma_start(d["cols"].rearrange("b p v -> p b v"), cols[:, :, :]).then_inc(s_st, 16)
            sp.wait_ge(s_row, 6)
            sp.dma_start(d["rows"], rows[:, :, :]).then_inc(s_st, 16)
            sp.wait_ge(s_st, 32)
            for half in range(2):
                sp.wait_ge(s_hst[half], 16 + 16 * SIDES * (FILLS // TURN))

        @block.scalar
        def _(act):
            act.dma_start(stage_w[:, 0, :].rearrange("p (k n) -> p k n", k=FT),
                          d["wdn"].rearrange("(k p) n -> p k n", p=P)).then_inc(s_w, 16)
            act.dma_start(staged(1, PIECES[0][2], PIECES[0][3]), PIECES[0][0]).then_inc(s_w2, 16)
            act.wait_ge(s_cmm, 1)
            nc.scalar.activation(rows[:, 0, :], ps[0:SEQS, 6, 0:D], ACT.Tanh).then_inc(s_tanh, 1)
            act.wait_ge(s_small, 16 * N_SMALL)
            nc.scalar.copy(t["ident_r"][:, :], t["ident"][:, :]).then_inc(s_ms, 1)
            nc.scalar.copy(t["ident_b"][:, :], t["ident"][:, :]).then_inc(s_ms, 1)
            for n, (src, tiles, k, cols_) in enumerate(PIECES):
                m = n + 1
                if m < len(PIECES):
                    if n >= 1:
                        act.wait_ge(s_wlo, n)
                    else:
                        act.wait_ge(s_dn, 3)
                    act.dma_start(staged(m + 1, PIECES[m][2], PIECES[m][3]),
                                  PIECES[m][0]).then_inc(s_w if (m + 1) % 2 == 0 else s_w2, 16)
                buf = (n + 1) % 2
                act.wait_ge(s_w2 if buf else s_w, 16 * (n // 2 + 1 + (0 if buf else 1)))
                nc.scalar.copy(tiles[0][:, 0:k, :], staged(buf, k, cols_)).then_inc(s_whi, 1)

        @block.vector
        def _(dve):
            dve.memset(ones[:, :], 1.0).then_inc(s_abs, 1)
            dve.memset(cond1[C:C + 1, :], 1.0).then_inc(s_abs, 1)
            dve.memset(cond2[C:C + 2, :], DELTA).then_inc(s_c2, 1)
            dve.wait_ge(s_c2, 1)
            dve.memset(cond2[C:C + 1, :], 1.0).then_inc(s_c2, 1)
            dve.wait_ge(s_small, 16 * N_SMALL)
            dve.tensor_scalar(cond2[0:C, :], cond1[0:C, :], DELTA, None, ALU.mult).then_inc(s_c2, 1)
            wdn = stage_w[:, 0, :]
            dve.wait_ge(s_w, 16)
            dve.tensor_reduce(wsum[:, :], wdn, AX.X, ALU.add, apply_absolute_value=True).then_inc(s_abs, 1)
            dve.wait_ge(s_sum, 1)
            dve.tensor_scalar(t["wmean"][:, :], ps[:, 7, 0:1], 1.0 / (HID * D), EPS_Q, ALU.mult,
                              ALU.max).then_inc(s_abs, 1)
            dve.wait_ge(s_abs, 4)
            dve.reciprocal(wrec[:, :], t["wmean"][:, :]).then_inc(s_abs, 1)
            dve.wait_ge(s_abs, 5)
            dve.tensor_scalar(wdn, wdn, wrec[:, 0:1], ROUND, ALU.mult, ALU.add).then_inc(s_dn, 1)
            dve.wait_ge(s_dn, 1)
            dve.tensor_scalar(wdn, wdn, ROUND, 1.0, ALU.subtract, ALU.min).then_inc(s_dn, 1)
            dve.wait_ge(s_dn, 2)
            dve.tensor_scalar(t["wdq"][:, :, :], wdn.rearrange("p (k n) -> p k n", k=FT), -1.0, None,
                              ALU.max).then_inc(s_dn, 1)
            dve.wait_ge(s_cmm, 3)
            cps = ps[:, 4, 0:10 * SEQS].rearrange("p (v b) -> p v b", b=SEQS)
            cview = cols[:, :, :].rearrange("p b v -> p v b")
            dve.tensor_copy(cview[:, 0:8, :], cps[:, 0:8, :]).then_inc(s_col, 1)
            dve.tensor_scalar(cview[:, 8:10, :], cps[:, 8:10, :], 1.0, None, ALU.add).then_inc(s_col, 1)
            dve.wait_ge(s_small, 16 * N_SMALL)
            dve.tensor_copy(rows[:, 1:3, :], ps[0:SEQS, 5, :].rearrange("p (a n) -> p a n", a=2)).then_inc(s_row, 1)
            dve.wait_ge(s_tanh, 1)
            dve.tensor_tensor(rows[:, 0, :], rows[:, 0, :], lnb[:, :], ALU.add).then_inc(s_row, 1)
            dve.wait_ge(s_row, 2)
            dve.tensor_tensor(rows[:, 0, :], rows[:, 0, :], lnw[0:SEQS, :], ALU.mult).then_inc(s_row, 1)
            dve.wait_ge(s_row, 3)
            dve.tensor_tensor(rows[:, 0, :], rows[:, 0, :], lnb[:, :], ALU.add).then_inc(s_row, 1)
            dve.tensor_tensor(rows[:, 3, :], rows[:, 2, :], outb[:, :], ALU.mult).then_inc(s_row, 1)
            dve.tensor_tensor(t["w2"][:, :], lnw[:, :], lnw[:, :], ALU.mult).then_inc(s_row, 1)
            dve.tensor_scalar(t["wmean"][:, :], t["wmean"][:, :], 1.0 / QMAX, None, ALU.mult).then_inc(s_abs, 1)
            dve.sem_inc(s_hev, BANKS)
            with dve.Fori(0, FILLS // TURN) as r:
                for n in range(TURN):
                    dve.wait_ge(s_hmm, r * TURN + (LOAD_BUFS + n + 1))
                    half = n // BANKS
                    dve.wait_ge(s_hst[half], r * (16 * SIDES) + 16)
                    dve.tensor_copy(hout[:, half, n % BANKS, :], ps[:, n % BANKS, :]).then_inc(s_hev, 1)

        @block.gpsimd
        def _(pool):
            for n, (src, tiles, k, cols_) in enumerate(PIECES):
                pool.wait_ge(s_whi, n + 1)
                pool.tensor_tensor(tiles[1][:, 0:k, :], staged((n + 1) % 2, k, cols_), tiles[0][:, 0:k, :],
                                   ALU.subtract).then_inc(s_wlo, 1)

        @block.tensor
        def _(pe):
            pe.wait_ge(s_small, 16 * N_SMALL)
            pe.wait_ge(s_abs, 2)
            pe.matmul(ps[0:SEQS, 6, 0:D], cond1[:, :], lin1[:, :], start=True, stop=True).then_inc(s_cmm, 1)
            pe.matmul(ps[0:SEQS, 5, :], cond1[0:C, :], roww[:, :, :], start=True, stop=True).then_inc(s_cmm, 1)
            for v in range(5):
                for k in range(K):
                    c = (2 * v + k) * SEQS
                    mm = pe.matmul(ps[:, 4, c:c + SEQS], colw[:, v, k * P:(k + 1) * P], cond1[0:C, :],
                                   start=True, stop=True)
            mm.then_inc(s_cmm, 1)
            pe.wait_ge(s_abs, 3)
            pe.matmul(ps[:, 7, 0:1], ones[:, :], wsum[:, :], start=True, stop=True).then_inc(s_sum, 1)
            pe.sem_inc(s_hmm, LOAD_BUFS)
            pe.wait_ge(s_c2, 3)
            with pe.Fori(0, FILLS // TURN) as r:
                for n in range(TURN):
                    pe.wait_ge(s_h[n % LOAD_BUFS], r * (16 * (TURN // LOAD_BUFS)) + 16 * (n // LOAD_BUFS + 1))
                    pe.wait_ge(s_hev, r * TURN + (n + 1))
                    for j in range(SIDES):
                        mm = pe.matmul(ps[j * SEQS:(j + 1) * SEQS, n % BANKS, :], cond2[:, :],
                                       hload[:, n % LOAD_BUFS, j, :], start=True, stop=True)
                    mm.then_inc(s_hmm, 1)


def main_block(nc, ctx, d, t):
    def sb(name, shape, dt=F32):
        return ctx.enter_context(nc.sbuf_tensor(name, shape, dt))

    def over(name, host, offset, shape, dt):
        return nc.alloc_sbuf_tensor_at(name, shape, dt, offset=nc.lookup_mloc(host).addr + offset)

    def sem(name):
        return ctx.enter_context(nc.semaphore(name))

    KB = 1024
    xin = sb("xin", [P, T, D])
    xf = sb("xf", [P, T, D])
    xc = sb("xc", [P, T, D])
    q_st = sb("q_st", [P, T, HEADS, SLOT], F32R)
    k_st = sb("k_st", [P, T, HEADS, SLOT], F32R)
    v_ext = sb("v_ext", [P, T, HEADS, 2 * DH])
    k_even = sb("k_even", [P, KV_BUFS, L], F32R)
    k_odd = sb("k_odd", [P, KV_BUFS, L], F32R)
    q_t = sb("q_t", [P, KV_BUFS, L], F32R)
    probs = sb("probs", [P, P_BUFS, 2, T, L])
    o_t = sb("o_t", [P, HEADS // 4, L])
    xr = sb("xr", [P, T, D])
    o_tok = over("o_tok", probs, 0, [P, T, HEADS, DH], F32)
    oh = over("oh", probs, 2 * KB, [P, K, L], F32R)
    ol = over("ol", probs, 4 * KB, [P, K, L], F32R)
    xt = over("xt", probs, 6 * KB, [P, K, L], F32)
    xh = over("xh", probs, 8 * KB, [P, K, L], F32R)
    xl = over("xl", probs, 10 * KB, [P, K, L], F32R)
    xs = sb("xs", [P, T, D])
    bs = sb("bs", [P, T, D])
    bt = sb("bt", [P, K, L])
    bh = sb("bh", [P, K, L], F32R)
    bl = sb("bl", [P, K, L], F32R)
    xb = sb("xb", [P, T, D])
    th = sb("th", [P, T, D])
    gp = sb("gp", [P, L])
    hf = sb("hf", [P, 2, L])
    hh = sb("hh", [P, FT, L], F32R)
    hl = sb("hl", [P, FT, L], F32R)
    x2 = sb("x2", [P, T, D])
    x3 = sb("x3", [P, T, D])
    hyp = sb("hyp", [P, UNITS])
    hq = sb("hq", [P, T, HID], BF16)
    zt = over("zt", gp, 0, [P, L], F32)
    h3 = over("h3", hl, 0, [P, T, HID], F32)
    ge = over("ge", hh, 0, [P, 2, 512], F32)
    hq_t = over("hq_t", hh, 4 * KB, [P, FT, L], BF16)
    out_t = over("out_t", hq, 0, [P, T, D], F32)
    c0 = sb("c0", [P, D])
    alpha = sb("alpha", [P, D])
    frow = sb("frow", [P, 2, D])
    col_a = sb("col_a", [P, 4])
    col_f = sb("col_f", [P, 4])
    col_c = sb("col_c", [P, 2])
    stat = sb("stat", [P, T, 6])
    mv = sb("mv", [P, T, 3])
    v0 = sb("v0", [P, 4, T])
    r0 = sb("r0", [P, 4, T])
    ss = sb("ss", [P, 3, T])
    eps = sb("eps", [P, T])
    half = sb("half", [P, T])
    mx = sb("mx", [P, T, HEADS])
    rden = sb("rden", [P, T, HEADS])
    am = sb("am", [P, T])
    qs = sb("qs", [P, T])
    qi = sb("qi", [P, T])

    def bank(name, n):
        return ctx.enter_context(nc.psum_tensor(name, [P, n, 512], F32))

    S = bank("S", 2)
    ST = bank("ST", 2)
    TB = bank("TB", 1)
    OB = bank("OB", 1)
    M = bank("M", 2)
    M0, M1 = M[:, 0, :], M[:, 1, :]

    names = """x_loaded c0_loaded col_a_loaded alpha_loaded frow_loaded col_f_loaded col_c_loaded hyp_loaded out_stored
        init_dve init_pool init_act stat_ready mean_steps mean_ready var0_ready rstd0_ready norm_steps w2_ready xf_ready ss1_ready
        var1_ready r1_ready xs_ready xt_full xt_ready xh_ready xl_ready qk_full qk_hi qk_lo v_full v_ready carried
        t_full kq_ready s_full max_ready shift_ready tm_full qm_ready st_full exp_ready pv_done ot_ready otok_full
        rden_ready otok_ready ont_full oh_ready ol_ready y_full y_ready xr_ready
        ss2_ready var2_ready r2_ready bs_ready xb_ready bt_full bt_ready bh_ready bl_ready gu_full th_ready gp_ready
        hf_ready hh_ready hl_ready f_full fy_ready x2_ready x2b_ready at_full at_ready z_full z_ready up_full x3_ready
        ss3_ready var3_ready r3_ready ct_full ch_ready cl_ready gate_full ge_ready val_full h3_ready am_ready
        quant_steps hr_ready hq_ready hqt_full hqt_ready ly_full out_ready""".split()
    s = {n: sem(n) for n in names}

    block = ctx.enter_context(nc.Block())

    EARLY, SLOTS = 3, PAIRS + 4
    TILE_AT = {3: 0, 4: 1, 6: 2, 7: 3, 8: 4, 9: 5, 10: 6, 11: 7}
    TAIL_AT = 5

    def run(iteration):
        def one(i, reg=None):
            here = (reg, i)
            flag = (lambda o: True) if reg is not None else (lambda o: 0 <= i + o < SEQS)
            iteration(here, flag(1), flag(0), flag(-1), flag(-2))
        return one

    def both(eng, iteration):
        one = run(iteration)
        for i in (-1, 0, 1):
            one(i)
        with eng.Fori(0, SEQS - 3) as r:
            one(2, r)
        for i in (SEQS - 1, SEQS, SEQS + 1):
            one(i)

    def rows_of(x):
        return x.rearrange("(p t) n -> p t n", t=T)

    @block.sync
    def _(sp):
        def index(seq):
            reg, off = seq
            return off if reg is None else reg + off

        def iteration(i, front, pairs, ffn, tail):
            a, b, c = shifted(i, 1), shifted(i, -1), shifted(i, -2)
            if ffn:
                sp.wait_ge(s["xb_ready"], at(b, 1, 0))
                sp.wait_ge(s["fy_ready"], at(b, 1, 0))
                sp.dma_start(frow[:, :, :], d["rows"][index(b), 2:4, :].partition_broadcast(P)
                             ).then_inc(s["frow_loaded"], 16)
            if front:
                sp.wait_ge(s["norm_steps"], at(a, 2, 0))
                sp.dma_start(xin[:, :, :], rows_of(d["x"][index(a)])).then_inc(s["x_loaded"], 16)
                sp.wait_ge(s["xf_ready"], at(a, 1, 0))
                sp.dma_start(c0[:, :], d["rows"][index(a), 0, :].partition_broadcast(P)
                             ).then_inc(s["c0_loaded"], 16)
                sp.wait_ge(s["xt_ready"], at(a, 2, 0))
                sp.dma_start(col_a[:, :], d["cols"][index(a), :, 0:4]).then_inc(s["col_a_loaded"], 16)
            if pairs:
                sp.wait_ge(s["bt_ready"], at(i, 2, 0))
                sp.dma_start(col_f[:, :], d["cols"][index(i), :, 4:8]).then_inc(s["col_f_loaded"], 16)
            if ffn:
                sp.wait_ge(s["cl_ready"], at(b, 2, 0))
                sp.dma_start(col_c[:, :], d["cols"][index(b), :, 8:10]).then_inc(s["col_c_loaded"], 16)
                sp.wait_ge(s["up_full"], at(b, 1, 0))
                sp.dma_start(hyp[:, :], d["hyp"][index(b)].rearrange("j q h m u -> (j q h m) u")
                             ).then_inc(s["hyp_loaded"], 16)
            if pairs:
                sp.wait_ge(s["y_ready"], at(i, 1, 0))
                sp.dma_start(alpha[:, :], d["rows"][index(i), 1, :].partition_broadcast(P)
                             ).then_inc(s["alpha_loaded"], 16)
            if tail:
                sp.wait_ge(s["out_ready"], at(c, 2, 2))
                sp.dma_start(rows_of(d["out"][index(c)]), out_t[:, :, :]).then_inc(s["out_stored"], 16)

        both(sp, iteration)
        sp.wait_ge(s["out_stored"], 16 * SEQS)

    @block.tensor
    def _(pe):
        ident, ident_r, ident_b = t["ident"], t["ident_r"], t["ident_b"]

        def product(out, left, right, chunks, start=True, stop=True):
            for k in range(chunks):
                for n, (x, y) in enumerate(PASSES):
                    mm = pe.matmul(out, left(x, k), right(y, k), start=(start and k == 0 and n == 0),
                                   stop=(stop and k == chunks - 1 and n == len(PASSES) - 1))
            return mm

        def to_features(out, src):
            for k in range(K):
                for tt in range(T):
                    c = (k * T + tt) * P
                    mm = pe.transpose(out[:, c:c + P], src[:, tt, k * P:(k + 1) * P], ident[:, :])
            return mm

        xparts, bparts, oparts = (xh, xl), (bh, bl), (oh, ol)

        def pair_in(i, p):
            if p == 0:
                pe.wait_ge(s["qk_lo"], at(i, 4, 4))
                pe.wait_ge(s["v_ready"], at(i, 1, 1))
            elif p <= 2:
                pe.wait_ge(s["kq_ready"], at(i, 3 * PAIRS, 3 * p))
            else:
                pe.wait_ge(s["qm_ready"], at(i, PAIRS, p - 2))
            for c, st in ((0, k_st), (L, q_st)):
                for tt in range(T):
                    mm = pe.transpose(TB[:, 0, c + tt * P:c + (tt + 1) * P].bitcast(F32R),
                                      st[:, tt, 2 * p:2 * p + 2, :], ident_r[:, :])
            mm.then_inc(s["t_full"], 1)

        def scores(i, p):
            pe.wait_ge(s["kq_ready"], at(i, 3 * PAIRS, 3 * p + 3))
            if p >= 1:
                pe.wait_ge(s["max_ready"], at(i, PAIRS, p))
            for tt in range(T):
                for h, kk in enumerate((k_even, k_odd)):
                    mm = pe.matmul(S[:, tt, h * L:(h + 1) * L], q_t[:, p % KV_BUFS, tt * P:(tt + 1) * P],
                                   kk[:, p % KV_BUFS, :], start=True, stop=True)
            mm.then_inc(s["s_full"], 1)

        def pair_shift(i, p):
            pe.wait_ge(s["shift_ready"], at(i, PAIRS, p + 1))
            if p == 0:
                pe.wait_ge(s["kq_ready"], at(i, 3 * PAIRS, 9))
            elif p < PAIRS - 2:
                pe.wait_ge(s["kq_ready"], at(i, 3 * PAIRS, 3 * (p + 3)))
            else:
                pe.wait_ge(s["qm_ready"], at(i, PAIRS, p))
            for tt in range(T):
                mm = pe.transpose(TB[:, 0, tt * P:(tt + 1) * P].bitcast(F32R), q_st[:, tt, 2 * p:2 * p + 2, :],
                                  ident_r[:, :])
            mm.then_inc(s["tm_full"], 1)

        def key_scores(i, p):
            pe.wait_ge(s["qm_ready"], at(i, PAIRS, p + 1))
            if p >= 1:
                pe.wait_ge(s["exp_ready"], at(i, PAIRS, p))
            else:
                pe.wait_ge(s["ol_ready"], at(i, 1, 0))
                pe.wait_ge(s["bt_ready"], at(i, 2, 0))
            for h, kk in enumerate((k_even, k_odd)):
                for kb in range(T):
                    mm = pe.matmul(ST[:, h, kb * L:(kb + 1) * L], kk[:, p % KV_BUFS, kb * P:(kb + 1) * P],
                                   q_t[:, p % KV_BUFS, :], start=True, stop=True)
            mm.then_inc(s["st_full"], 1)

        def values(i, g):
            pe.wait_ge(s["exp_ready"], at(i, PAIRS, 2 * g + 2))
            if g == 0:
                pe.wait_ge(s["y_ready"], at(i, 1, 0))
            if g == 2:
                pe.wait_ge(s["ot_ready"], at(i, 2, 1))
            for kb in range(T):
                for j in range(4):
                    mm = pe.matmul(OB[32 * j:32 * j + 32, 0, (g % 2) * L:(g % 2 + 1) * L],
                                   v_ext[:, kb, 4 * g + j, :], probs[:, (2 * g + j // 2) % P_BUFS, j % 2, kb, :],
                                   start=(kb == 0), stop=(kb == T - 1))
            mm.then_inc(s["pv_done"], 1)

        def hidden_tile(b, tail, f):
            if f == 0:
                pe.wait_ge(s["bl_ready"], at(b, 1, 1))
                pe.wait_ge(s["h3_ready"], at(b, 4, 0))
            elif f == 1:
                pe.wait_ge(s["ge_ready"], at(b, 4, 0))
            else:
                pe.wait_ge(s["hf_ready"], at(b, FT, f - 1))
            if tail and f == 2:
                pe.wait_ge(s["hqt_ready"], at(b, 2, 0))
            if tail and f == 3:
                pe.wait_ge(s["out_ready"], at(b, 2, 0))
            for g in range(2):
                mm = product((M1, M0)[f % 2][:, g * L:(g + 1) * L],
                             lambda x, k: t["wgh"][x][:, k, g * HID + f * P:g * HID + (f + 1) * P],
                             lambda y, k: bparts[y][:, k, :], K)
            mm.then_inc(s["gu_full"], 1)

        def quantised_to_features(c, ffn, tt):
            pe.wait_ge(s["hq_ready"], at(c, 2, tt + 1))
            if ffn:
                pe.wait_ge(s["hf_ready"], at(c, FT, FT + tt + 1))
            elif tt == 0:
                pe.wait_ge(s["h3_ready"], at(c, 4, 4))
            else:
                pe.wait_ge(s["ge_ready"], at(c, 4, 4))
            for f in range(FT):
                mm = pe.transpose((M1, M0)[tt].bitcast(BF16)[:, f * P:(f + 1) * P], hq[:, tt, f * P:(f + 1) * P],
                                  ident_b[:, :])
            mm.then_inc(s["hqt_full"], 1)

        def quantised_down(c):
            pe.wait_ge(s["hqt_ready"], at(c, 2, 2))
            for tt in range(T):
                for f in range(FT):
                    mm = pe.matmul(M0[:, tt * D:(tt + 1) * D], hq_t[:, f, tt * P:(tt + 1) * P], t["wdq"][:, f, :],
                                   start=(f == 0), stop=(f == FT - 1))
            mm.then_inc(s["ly_full"], 1)

        def hidden_down(tt, chunks):
            for f in chunks:
                mm = product(M1[:, tt * D:(tt + 1) * D], lambda x, k: (hh, hl)[x][:, f, tt * P:(tt + 1) * P],
                             lambda y, k: t["wout"][y][:, f, :], 1, start=(f == 0), stop=(f == FT - 1))
            return mm

        def qk_project(tt):
            product(S[:, tt, :], lambda x, k: xparts[x][:, k, tt * P:(tt + 1) * P],
                    lambda y, k: t["wqkv"][y][:, k, 0:2 * D], K).then_inc(s["qk_full"], 1)

        def out_project(i, tt):
            pe.wait_ge(s["ol_ready"], at(i, 1, 1))
            return product(OB[:, 0, tt * D:(tt + 1) * D], lambda x, k: oparts[x][:, k, tt * P:(tt + 1) * P],
                           lambda y, k: t["wo"][y][:, k, :], K)

        def iteration(i, front, pairs, ffn, tail):
            a, b, c = shifted(i, 1), shifted(i, -1), shifted(i, -2)
            for slot in range(EARLY, SLOTS):
                if pairs and slot < PAIRS:
                    pair_in(i, slot)
                if pairs and EARLY < slot <= PAIRS:
                    scores(i, slot - 1)
                if tail and slot == TAIL_AT:
                    for tt in range(T):
                        quantised_to_features(c, ffn, tt)
                if ffn and slot in TILE_AT:
                    hidden_tile(b, tail, TILE_AT[slot])
                if pairs and slot < PAIRS + 2:
                    pair_shift(i, slot - 2)
                if pairs and slot < PAIRS + 3:
                    key_scores(i, slot - 3)
                if pairs and slot >= 5 and slot % 2 and slot < SLOTS - 1:
                    values(i, (slot - 5) // 2)
                if tail and slot == TAIL_AT:
                    quantised_down(c)
            if ffn:
                pe.wait_ge(s["hl_ready"], at(b, FT, FT - 2))
                pe.wait_ge(s["hf_ready"], at(b, FT, FT - 1))
                hidden_down(0, range(FT - 2))
                pe.wait_ge(s["hl_ready"], at(b, FT, FT - 1))
                hidden_down(0, (FT - 2,))
            if pairs:
                values(i, HEADS // 4 - 1)
            if ffn:
                pe.wait_ge(s["hl_ready"], at(b, FT, FT))
                hidden_down(0, (FT - 1,))
            if front:
                pe.wait_ge(s["xs_ready"], at(a, 2, 2))
                pe.wait_ge(s["qm_ready"], at(a, PAIRS, 0))
                to_features(TB[:, 0, :], xs).then_inc(s["xt_full"], 1)
            if ffn:
                hidden_down(1, range(FT // 2))
            if pairs:
                pe.wait_ge(s["ot_ready"], at(i, 2, 2))
                pe.wait_ge(s["max_ready"], at(i, PAIRS, PAIRS))
                for tt in range(T):
                    for g in range(HEADS // 4):
                        mm = pe.transpose(S[:, tt, g * P:(g + 1) * P], o_t[:, g, tt * P:(tt + 1) * P], ident[:, :])
                    mm.then_inc(s["otok_full"], 1)
            if ffn:
                hidden_down(1, range(FT // 2, FT)).then_inc(s["f_full"], 1)
            if pairs:
                pe.wait_ge(s["otok_ready"], at(i, 2, 2))
                pe.wait_ge(s["exp_ready"], at(i, PAIRS, PAIRS))
                to_features(ST[:, 0, :], o_tok[:, :, :, :].rearrange("p t h e -> p t (h e)")
                            ).then_inc(s["ont_full"], 1)
            if front:
                pe.wait_ge(s["xl_ready"], at(a, 1, 1))
                pe.wait_ge(s["otok_ready"], at(a, 2, 0))
                qk_project(0)
            if ffn:
                pe.wait_ge(s["x2_ready"], at(b, 1, 1))
                to_features(M0, x2).then_inc(s["at_full"], 1)
            if front:
                qk_project(1)
            if ffn:
                pe.wait_ge(s["at_ready"], at(b, 1, 1))
                pe.wait_ge(s["hyp_loaded"], at(b, 16, 16))
                for k in range(K):
                    mm = pe.matmul(M1[:, 0:L], hyp[:, k * BN:(k + 1) * BN], bt[:, k, :], start=(k == 0),
                                   stop=(k == K - 1))
                mm.then_inc(s["z_full"], 1)
            if pairs:
                out_project(i, 0)
            if ffn:
                pe.wait_ge(s["z_ready"], at(b, 1, 1))
                for tt in range(T):
                    mm = pe.matmul(M0[:, tt * D:(tt + 1) * D], zt[:, tt * P:(tt + 1) * P], hyp[:, K * BN:UNITS],
                                   start=True, stop=True)
                mm.then_inc(s["up_full"], 1)
            if pairs:
                out_project(i, 1).then_inc(s["y_full"], 1)
            if ffn:
                pe.wait_ge(s["x3_ready"], at(b, 1, 1))
                to_features(M1, x3).then_inc(s["ct_full"], 1)
            if front:
                for tt in range(T):
                    mm = product(TB[:, 0, tt * D:(tt + 1) * D], lambda x, k: xparts[x][:, k, tt * P:(tt + 1) * P],
                                 lambda y, k: t["wqkv"][y][:, k, 2 * D:3 * D], K)
                mm.then_inc(s["v_full"], 1)
            for r in range(2 * T):
                tt, n = r // 2, r % 2
                if ffn:
                    if r == 0:
                        pe.wait_ge(s["cl_ready"], at(b, 2, 2))
                    else:
                        pe.wait_ge(s["ge_ready"], at(b, 4, r))
                    product(M0, lambda x, k: bparts[x][:, k, tt * P:(tt + 1) * P],
                            lambda y, k: t["wup"][y][:, k, HID + n * 512:HID + (n + 1) * 512], K
                            ).then_inc(s["gate_full"], 1)
                if front and r != 2:
                    pair_in(a, (0, 1, None, 2)[r])
                if pairs and r == 2:
                    pe.wait_ge(s["bs_ready"], at(i, 2, 2))
                    to_features(ST[:, 1, :], bs).then_inc(s["bt_full"], 1)
                if ffn:
                    if r >= 1:
                        pe.wait_ge(s["h3_ready"], at(b, 4, r))
                    product(M1, lambda x, k: bparts[x][:, k, tt * P:(tt + 1) * P],
                            lambda y, k: t["wup"][y][:, k, n * 512:(n + 1) * 512], K).then_inc(s["val_full"], 1)
                if front and r % 2 == 0:
                    scores(a, r // 2)
            if front:
                pair_shift(a, 0)
                scores(a, 2)

        pe.wait_ge(s["init_dve"], 5)
        pe.wait_ge(s["init_pool"], 2)
        both(pe, iteration)

    @block.scalar
    def _(act):
        A = nc.scalar.activation

        def square_sums(src, junk, which, ready):
            for tt in range(T):
                A(junk[:, tt, :], src[:, tt, :], ACT.Square, scale=D ** -0.5, accum_out=ss[:, which, tt:tt + 1]).then_inc(ready, 1)

        def pair_out(i, p):
            buf = p % KV_BUFS
            act.wait_ge(s["t_full"], at(i, PAIRS, p + 1))
            for dst, src in ((k_even[0:SLOT, buf, :], TB[0:SLOT, 0, 0:L]), (k_odd[SLOT:P, buf, :], TB[SLOT:P, 0, 0:L]),
                             (q_t[:, buf, :], TB[:, 0, L:2 * L])):
                nc.scalar.copy(dst, src).then_inc(s["kq_ready"], 1)

        def outputs(i, n):
            act.wait_ge(s["pv_done"], at(i, 4, 2 * n + 2))
            nc.scalar.copy(o_t[:, 2 * n:2 * n + 2, :].rearrange("p g n -> p (g n)"), OB[:, 0, :]
                           ).then_inc(s["ot_ready"], 1)

        def high_parts(a, tt):
            act.wait_ge(s["qk_full"], at(a, 2, tt + 1))
            src = S[:, tt, :].rearrange("p (o h e) -> p o h e", o=2, h=HEADS)
            q_dst = q_st[:, tt, :, 0:2 * DH].rearrange("p h (r e) -> p h r e", r=2)
            k_dst = k_st[:, tt, :, :].rearrange("p h (r e) -> p h r e", e=DH)[:, :, 0:3:2, :]
            nc.scalar.copy(q_dst, src[:, 0, :, :].unsqueeze(2).to_broadcast([P, HEADS, 2, DH])
                           ).then_inc(s["qk_hi"], 1)
            nc.scalar.copy(k_dst, src[:, 1, :, :].unsqueeze(2).to_broadcast([P, HEADS, 2, DH])
                           ).then_inc(s["qk_hi"], 1)

        def iteration(i, front, pairs, ffn, tail):
            a, b, c = shifted(i, 1), shifted(i, -1), shifted(i, -2)
            for slot in range(EARLY, SLOTS):
                if pairs and slot < PAIRS:
                    pair_out(i, slot)
                if tail and slot == TAIL_AT:
                    for tt in range(T):
                        act.wait_ge(s["hqt_full"], at(c, 2, tt + 1))
                        nc.scalar.copy(hq_t[:, :, tt * P:(tt + 1) * P],
                                       (M1, M0)[tt].bitcast(BF16).rearrange("p (f n) -> p f n", f=FT)
                                       ).then_inc(s["hqt_ready"], 1)
                if pairs and slot == 4:
                    act.wait_ge(s["xf_ready"], at(i, 1, 1))
                    act.wait_ge(s["xr_ready"], at(i, 1, 0))
                    nc.scalar.copy(xc[:, :, :], xf[:, :, :]).then_inc(s["carried"], 1)
                if ffn and slot in TILE_AT:
                    f = TILE_AT[slot]
                    act.wait_ge(s["gu_full"], at(b, FT, f + 1))
                    A(th[:, f % 2, :], (M1, M0)[f % 2][:, 0:L], ACT.Tanh, scale=0.5).then_inc(s["th_ready"], 1)
                if pairs and slot < PAIRS + 3:
                    p = slot - 3
                    act.wait_ge(s["st_full"], at(i, PAIRS, p + 1))
                    A(probs[:, p % P_BUFS, :, :, :].rearrange("p h k q -> p (h k q)"),
                      ST[:, :, :].rearrange("p h n -> p (h n)"), ACT.Exp, scale=SCORE_SCALE
                      ).then_inc(s["exp_ready"], 1)
                if ffn and slot in TILE_AT:
                    act.wait_ge(s["hf_ready"], at(b, FT, f + 1))
                    nc.scalar.copy(hh[:, f, :], hf[:, f % 2, :]).then_inc(s["hh_ready"], 1)
                if pairs and slot == 7:
                    outputs(i, 0)
                if front and slot == PAIRS + 2:
                    act.wait_ge(s["xf_ready"], at(a, 1, 1))
                    act.wait_ge(s["xt_full"], at(a, 1, 0))
                    square_sums(xf, xs, 0, s["ss1_ready"])
                if front and slot == PAIRS + 3:
                    act.wait_ge(s["r1_ready"], at(a, 1, 1))
                    act.wait_ge(s["ss1_ready"], at(a, 2, 2))
                    for tt in range(T):
                        A(xs[:, tt, :], xf[:, tt, :], ACT.Copy, scale=r0[:, 1, tt:tt + 1]
                          ).then_inc(s["xs_ready"], 1)
            if pairs:
                outputs(i, 1)
            if front:
                act.wait_ge(s["xt_ready"], at(a, 2, 2))
                nc.scalar.copy(xh[:, :, :], xt[:, :, :]).then_inc(s["xh_ready"], 1)
            if pairs:
                act.wait_ge(s["ont_full"], at(i, 1, 1))
                nc.scalar.copy(oh[:, :, :].rearrange("p k n -> p (k n)"), ST[:, 0, :]).then_inc(s["oh_ready"], 1)
            if front:
                high_parts(a, 0)
            if ffn:
                act.wait_ge(s["at_full"], at(b, 1, 1))
                nc.scalar.copy(bt[:, :, :].rearrange("p k n -> p (k n)"), M0).then_inc(s["at_ready"], 1)
            if front:
                high_parts(a, 1)
            if ffn:
                act.wait_ge(s["z_full"], at(b, 1, 1))
                A(zt[:, :], M1[:, 0:L], ACT.Relu, bias=t["bd"][:, 0:1]).then_inc(s["z_ready"], 1)
                act.wait_ge(s["x3_ready"], at(b, 1, 1))
                act.wait_ge(s["bt_full"], at(b, 1, 1))
                square_sums(x3, bs, 2, s["ss3_ready"])
                act.wait_ge(s["ct_full"], at(b, 1, 1))
                act.wait_ge(s["col_c_loaded"], at(b, 16, 16))
                for k in range(K):
                    A(bh[:, k, :], M1[:, k * L:(k + 1) * L], ACT.Copy, scale=col_c[:, k:k + 1]
                      ).then_inc(s["ch_ready"], 1)
            if front:
                act.wait_ge(s["v_full"], at(a, 1, 1))
                nc.scalar.copy(v_ext[:, :, :, 0:DH], TB[:, 0, :].rearrange("p (t h e) -> p t h e", t=T, h=HEADS)
                               ).then_inc(s["v_ready"], 1)

            def gelu(r):
                if r == 0:
                    act.wait_ge(s["r3_ready"], at(b, 1, 1))
                act.wait_ge(s["gate_full"], at(b, 4, r + 1))
                A(ge[:, r % 2, :], M0, ACT.Gelu, scale=r0[:, 3, r // 2:r // 2 + 1]).then_inc(s["ge_ready"], 1)

            if ffn:
                gelu(0)
            if front:
                pair_out(a, 0)
            if pairs:
                act.wait_ge(s["xr_ready"], at(i, 1, 1))
                act.wait_ge(s["bt_full"], at(i, 1, 0))
                square_sums(xr, bs, 1, s["ss2_ready"])
            if ffn:
                gelu(1)
            if front:
                pair_out(a, 1)
            if pairs:
                act.wait_ge(s["r2_ready"], at(i, 1, 1))
                act.wait_ge(s["ss2_ready"], at(i, 2, 2))
                for tt in range(T):
                    A(bs[:, tt, :], xr[:, tt, :], ACT.Copy, scale=r0[:, 2, tt:tt + 1]).then_inc(s["bs_ready"], 1)
            if ffn:
                gelu(2)
                gelu(3)
            if front:
                pair_out(a, 2)
            if pairs:
                if ffn:
                    act.wait_ge(s["val_full"], at(b, 4, 4))
                act.wait_ge(s["bt_ready"], at(i, 2, 2))
                nc.scalar.copy(bh[:, :, :], bt[:, :, :]).then_inc(s["bh_ready"], 1)

        both(act, iteration)

    @block.vector
    def _(dve):
        dve.memset(v_ext[:, :, :, :], 1.0).then_inc(s["init_dve"], 1)
        dve.memset(k_even[:, :, :].bitcast(F32), 0.0).then_inc(s["init_dve"], 1)
        dve.memset(k_odd[:, :, :].bitcast(F32), 0.0).then_inc(s["init_dve"], 1)
        dve.memset(half[:, :], -0.5).then_inc(s["init_dve"], 1)
        dve.memset(eps[:, :], EPS_RMS).then_inc(s["init_dve"], 1)
        dve.wait_ge(s["init_pool"], 2)

        def modulated(dst, src, col, ready):
            for k in range(K):
                dve.tensor_scalar(dst[:, k, :], src[:, k * L:(k + 1) * L], col[:, k:k + 1], col[:, 2 + k:3 + k],
                                  ALU.mult, ALU.add).then_inc(ready, 1)

        def maximum(i, p):
            dve.wait_ge(s["s_full"], at(i, PAIRS, p + 1))
            dve.tensor_reduce(mx[:, :, 2 * p:2 * p + 2], S[:, :, :].rearrange("p t (h n) -> p t h n", h=2), AX.X,
                              ALU.max).then_inc(s["max_ready"], 1)
            dve.wait_ge(s["max_ready"], at(i, PAIRS, p + 1))
            dve.tensor_scalar(q_st[:, :, 2 * p:2 * p + 2, SHIFT_ROW], mx[:, :, 2 * p:2 * p + 2], -1.0, None,
                              ALU.mult).then_inc(s["shift_ready"], 1)

        def shifted_q(i, p):
            dve.wait_ge(s["tm_full"], at(i, PAIRS, p + 1))
            dve.tensor_copy(q_t[:, p % KV_BUFS, :], TB[:, 0, 0:L]).then_inc(s["qm_ready"], 1)

        def low_parts(a, tt):
            dve.wait_ge(s["qk_hi"], at(a, 4, 2 * tt + 2))
            dve.memset(q_st[:, tt, :, SHIFT_ROW:SHIFT_ROW + 1].bitcast(F32), 0.0)
            src = S[:, tt, :].rearrange("p (o h e) -> p o h e", o=2, h=HEADS)
            dve.tensor_tensor(q_st[:, tt, :, 2 * DH:3 * DH], src[:, 0, :, :], q_st[:, tt, :, 0:DH],
                              ALU.subtract).then_inc(s["qk_lo"], 1)
            dve.tensor_tensor(k_st[:, tt, :, DH:2 * DH], src[:, 1, :, :], k_st[:, tt, :, 0:DH],
                              ALU.subtract).then_inc(s["qk_lo"], 1)

        def gated(b, r):
            tt, n = r // 2, r % 2
            dve.wait_ge(s["val_full"], at(b, 4, r + 1))
            dve.wait_ge(s["ge_ready"], at(b, 4, r + 1))
            dve.scalar_tensor_tensor(out=h3[:, tt, n * 512:(n + 1) * 512], in0=M1, scalar=r0[:, 3, tt:tt + 1],
                                     in1=ge[:, r % 2, :], op0=ALU.mult, op1=ALU.mult).then_inc(s["h3_ready"], 1)

        def largest(b, tt):
            dve.wait_ge(s["h3_ready"], at(b, 4, 2 * tt + 2))
            dve.tensor_reduce(am[:, tt:tt + 1], h3[:, tt, :], AX.X, ALU.max, apply_absolute_value=True
                              ).then_inc(s["am_ready"], 1)

        def quant_scale(b, tt):
            dve.wait_ge(s["am_ready"], at(b, 2, tt + 1))
            dve.tensor_scalar(am[:, tt:tt + 1], am[:, tt:tt + 1], EPS_Q, None, ALU.max).then_inc(s["quant_steps"], 1)
            dve.wait_ge(s["quant_steps"], at(b, 8, 4 * tt + 1))
            dve.reciprocal(qs[:, tt:tt + 1], am[:, tt:tt + 1]).then_inc(s["quant_steps"], 1)
            dve.tensor_scalar(qi[:, tt:tt + 1], am[:, tt:tt + 1], t["wmean"][:, 0:1], None, ALU.mult
                              ).then_inc(s["quant_steps"], 1)
            dve.wait_ge(s["quant_steps"], at(b, 8, 4 * tt + 2))
            dve.tensor_scalar(qs[:, tt:tt + 1], qs[:, tt:tt + 1], QMAX, None, ALU.mult
                              ).then_inc(s["quant_steps"], 1)

        def quantise(b, tt):
            dve.wait_ge(s["quant_steps"], at(b, 8, 4 * tt + 4))
            dve.tensor_scalar(h3[:, tt, :], h3[:, tt, :], qs[:, tt:tt + 1], ROUND, ALU.mult, ALU.add
                              ).then_inc(s["hr_ready"], 1)
            dve.wait_ge(s["hr_ready"], at(b, 2, tt + 1))
            if tt == 0:
                dve.wait_ge(s["out_stored"], at(b, 16, 0))
            dve.tensor_scalar(hq[:, tt, :], h3[:, tt, :], ROUND, QMAX, ALU.subtract, ALU.min
                              ).then_inc(s["hq_ready"], 1)

        def iteration(i, front, pairs, ffn, tail):
            a, b, c = shifted(i, 1), shifted(i, -1), shifted(i, -2)

            def hidden_lo(f):
                dve.wait_ge(s["hh_ready"], at(b, FT, f + 1))
                dve.tensor_tensor(hl[:, f, :], hf[:, f % 2, :], hh[:, f, :], ALU.subtract
                                  ).then_inc(s["hl_ready"], 1)

            for slot in range(EARLY, SLOTS):
                if tail and slot == TAIL_AT + 1:
                    dve.wait_ge(s["ly_full"], at(c, 1, 1))
                    for tt in range(T):
                        dve.scalar_tensor_tensor(out=out_t[:, tt, :], in0=M0[:, tt * D:(tt + 1) * D],
                                                 scalar=qi[:, tt:tt + 1], in1=x3[:, tt, :], op0=ALU.mult,
                                                 op1=ALU.add).then_inc(s["out_ready"], 1)
                if ffn and slot - 1 in TILE_AT:
                    hidden_lo(TILE_AT[slot - 1])
                if pairs and EARLY < slot <= PAIRS:
                    maximum(i, slot - 1)
                if pairs and slot < PAIRS + 2:
                    shifted_q(i, slot - 2)
                if ffn and slot in TILE_AT:
                    f = TILE_AT[slot]
                    bk = (M1, M0)[f % 2]
                    dve.wait_ge(s["th_ready"], at(b, FT, f + 1))
                    dve.scalar_tensor_tensor(out=gp[:, :], in0=th[:, f % 2, :], scalar=1.0, in1=bk[:, 0:L],
                                             op0=ALU.add, op1=ALU.mult).then_inc(s["gp_ready"], 1)
                    dve.wait_ge(s["gp_ready"], at(b, FT, f + 1))
                    dve.scalar_tensor_tensor(out=hf[:, f % 2, :], in0=gp[:, :], scalar=0.5, in1=bk[:, L:2 * L],
                                             op0=ALU.mult, op1=ALU.mult).then_inc(s["hf_ready"], 1)
                if tail and slot == EARLY:
                    quantise(c, 1)
                if front and slot == PAIRS:
                    dve.wait_ge(s["x_loaded"], at(a, 16, 16))
                    for tt in range(T):
                        dve.bn_stats(stat[:, tt, :], xin[:, tt, :]).then_inc(s["stat_ready"], 1)
                    dve.wait_ge(s["stat_ready"], at(a, 2, 2))
                    for n, (j, op) in enumerate(((1, ALU.add), (1, ALU.subtract), (2, ALU.add))):
                        dve.tensor_tensor(mv[:, :, n], stat[:, :, j], stat[:, :, j + 3], op
                                          ).then_inc(s["mean_steps"], 1)
                    dve.wait_ge(s["mean_steps"], at(a, 5, 3))
                    dve.tensor_tensor(mv[:, :, 1], mv[:, :, 1], mv[:, :, 1], ALU.mult
                                      ).then_inc(s["mean_steps"], 1)
                    dve.tensor_scalar(mv[:, :, 0], mv[:, :, 0], 0.5, None, ALU.mult
                                      ).then_inc(s["mean_ready"], 1)
                    dve.wait_ge(s["mean_steps"], at(a, 5, 4))
                    dve.scalar_tensor_tensor(out=mv[:, :, 2], in0=mv[:, :, 1], scalar=D / 4.0, in1=mv[:, :, 2],
                                             op0=ALU.mult, op1=ALU.add).then_inc(s["mean_steps"], 1)
                    dve.wait_ge(s["mean_steps"], at(a, 5, 5))
                    dve.tensor_scalar(v0[:, 0, :], mv[:, :, 2], 1.0 / D, EPS_LN, ALU.mult, ALU.add
                                      ).then_inc(s["var0_ready"], 1)
                if front and slot == PAIRS + 1:
                    dve.wait_ge(s["rstd0_ready"], at(a, 1, 1))
                    dve.wait_ge(s["mean_ready"], at(a, 1, 1))
                    dve.wait_ge(s["carried"], at(a, 1, 0))
                    dve.wait_ge(s["xs_ready"], at(a, 2, 0))
                    for tt in range(T):
                        dve.tensor_scalar(xf[:, tt, :], xin[:, tt, :], mv[:, tt, 0:1], r0[:, 0, tt:tt + 1],
                                          ALU.subtract, ALU.mult).then_inc(s["norm_steps"], 1)
                    dve.wait_ge(s["norm_steps"], at(a, 2, 2))
                    dve.tensor_tensor(xf[:, :, :], xf[:, :, :], t["w2"][:, :].unsqueeze(1).to_broadcast([P, T, D]),
                                      ALU.mult).then_inc(s["w2_ready"], 1)
                    dve.wait_ge(s["w2_ready"], at(a, 1, 1))
                    dve.wait_ge(s["c0_loaded"], at(a, 16, 16))
                    dve.tensor_tensor(xf[:, :, :], xf[:, :, :], c0[:, :].unsqueeze(1).to_broadcast([P, T, D]),
                                      ALU.add).then_inc(s["xf_ready"], 1)
            if ffn:
                hidden_lo(FT - 1)
            if front:
                dve.wait_ge(s["xt_full"], at(a, 1, 1))
                dve.wait_ge(s["col_a_loaded"], at(a, 16, 16))
                modulated(xt, TB[:, 0, :], col_a, s["xt_ready"])
                dve.wait_ge(s["xh_ready"], at(a, 1, 1))
                dve.tensor_tensor(xl[:, :, :], xt[:, :, :], xh[:, :, :], ALU.subtract).then_inc(s["xl_ready"], 1)
            if pairs:
                for tt in range(T):
                    dve.wait_ge(s["otok_full"], at(i, 2, tt + 1))
                    src = S[:, tt, :].rearrange("p (h e) -> p h e", e=2 * DH)
                    dve.reciprocal(rden[:, tt, :], src[:, :, DH]).then_inc(s["rden_ready"], 1)
                for tt in range(T):
                    src = S[:, tt, :].rearrange("p (h e) -> p h e", e=2 * DH)
                    dve.wait_ge(s["rden_ready"], at(i, 2, tt + 1))
                    dve.tensor_tensor(o_tok[:, tt, :, :], src[:, :, 0:DH],
                                      rden[:, tt, :].unsqueeze(2).to_broadcast([P, HEADS, DH]), ALU.mult
                                      ).then_inc(s["otok_ready"], 1)
            if ffn:
                dve.wait_ge(s["f_full"], at(b, 1, 1))
                dve.wait_ge(s["frow_loaded"], at(b, 16, 16))
                dve.tensor_tensor(hf[:, :, :], M1.rearrange("p (t n) -> p t n", t=T),
                                  frow[:, 0, :].unsqueeze(1).to_broadcast([P, T, D]), ALU.mult
                                  ).then_inc(s["fy_ready"], 1)
                dve.wait_ge(s["fy_ready"], at(b, 1, 1))
                dve.wait_ge(s["xb_ready"], at(b, 1, 1))
                dve.tensor_tensor(x2[:, :, :], xb[:, :, :], hf[:, :, :], ALU.add).then_inc(s["x2_ready"], 1)
            if pairs:
                dve.wait_ge(s["oh_ready"], at(i, 1, 1))
                dve.tensor_tensor(ol[:, :, :].rearrange("p k n -> p (k n)"), ST[:, 0, :],
                                  oh[:, :, :].rearrange("p k n -> p (k n)"), ALU.subtract
                                  ).then_inc(s["ol_ready"], 1)
            if front:
                low_parts(a, 0)
                low_parts(a, 1)
            if ffn:
                dve.wait_ge(s["up_full"], at(b, 1, 1))
                dve.wait_ge(s["x2b_ready"], at(b, 1, 1))
                dve.tensor_tensor(x3[:, :, :].rearrange("p t n -> p (t n)"), M0,
                                  xb[:, :, :].rearrange("p t n -> p (t n)"), ALU.add).then_inc(s["x3_ready"], 1)
                dve.wait_ge(s["col_c_loaded"], at(b, 16, 16))
                dve.wait_ge(s["ch_ready"], at(b, 2, 2))
                for k in range(K):
                    dve.scalar_tensor_tensor(out=bl[:, k, :], in0=M1[:, k * L:(k + 1) * L],
                                             scalar=col_c[:, k:k + 1], in1=bh[:, k, :], op0=ALU.mult,
                                             op1=ALU.subtract).then_inc(s["cl_ready"], 1)
            if pairs:
                dve.wait_ge(s["y_full"], at(i, 1, 1))
                dve.wait_ge(s["alpha_loaded"], at(i, 16, 16))
                dve.tensor_tensor(hf[:, :, :], OB[:, 0, :].rearrange("p (t n) -> p t n", t=T),
                                  alpha[:, :].unsqueeze(1).to_broadcast([P, T, D]), ALU.mult
                                  ).then_inc(s["y_ready"], 1)
                dve.wait_ge(s["y_ready"], at(i, 1, 1))
                dve.wait_ge(s["carried"], at(i, 1, 1))
                dve.tensor_tensor(xr[:, :, :], xc[:, :, :], hf[:, :, :], ALU.add).then_inc(s["xr_ready"], 1)
            if ffn:
                dve.wait_ge(s["r3_ready"], at(b, 1, 1))
                gated(b, 0)
            if front:
                maximum(a, 0)
            if ffn:
                gated(b, 1)
                largest(b, 0)
                quant_scale(b, 0)
            if ffn:
                gated(b, 2)
            if front:
                maximum(a, 1)
            if pairs:
                dve.wait_ge(s["bt_full"], at(i, 1, 1))
                dve.wait_ge(s["col_f_loaded"], at(i, 16, 16))
                modulated(bt, ST[:, 1, :], col_f, s["bt_ready"])
            if ffn:
                quantise(b, 0)
                gated(b, 3)
            if front:
                shifted_q(a, 0)
            if pairs:
                dve.wait_ge(s["bh_ready"], at(i, 1, 1))
                dve.tensor_tensor(bl[:, :, :], bt[:, :, :], bh[:, :, :], ALU.subtract).then_inc(s["bl_ready"], 1)
            if ffn:
                largest(b, 1)
            if front:
                maximum(a, 2)
            if ffn:
                quant_scale(b, 1)

        both(dve, iteration)

    @block.gpsimd
    def _(pool):
        pool.memset(q_st[:, :, :, :].bitcast(F32), 0.0).then_inc(s["init_pool"], 1)
        pool.memset(k_st[:, :, :, :].bitcast(F32), 1.0).then_inc(s["init_pool"], 1)
        pool.wait_ge(s["init_dve"], 5)

        def inverse_root(which, ready):
            pool.tensor_tensor(r0[:, which, :], v0[:, which, :], half[:, :], ALU.pow).then_inc(ready, 1)

        def rms(which, step, ready, seq):
            pool.tensor_tensor(v0[:, which, :], ss[:, which - 1, :], eps[:, :], ALU.add).then_inc(step, 1)
            pool.wait_ge(step, at(seq, 1, 1))
            inverse_root(which, ready)

        def iteration(i, front, pairs, ffn, tail):
            a, b = shifted(i, 1), shifted(i, -1)
            if ffn:
                pool.wait_ge(s["frow_loaded"], at(b, 16, 16))
                pool.wait_ge(s["xr_ready"], at(b, 1, 1))
                pool.wait_ge(s["x3_ready"], at(b, 1, 0))
                pool.tensor_tensor(xb[:, :, :], xr[:, :, :], frow[:, 1, :].unsqueeze(1).to_broadcast([P, T, D]),
                                   ALU.add).then_inc(s["xb_ready"], 1)
            if front:
                pool.wait_ge(s["var0_ready"], at(a, 1, 1))
                inverse_root(0, s["rstd0_ready"])
                pool.wait_ge(s["ss1_ready"], at(a, 2, 2))
                rms(1, s["var1_ready"], s["r1_ready"], a)
            if ffn:
                pool.wait_ge(s["x2_ready"], at(b, 1, 1))
                pool.tensor_tensor(xb[:, :, :], x2[:, :, :], t["bu"][:, :].unsqueeze(1).to_broadcast([P, T, D]),
                                   ALU.add).then_inc(s["x2b_ready"], 1)
                pool.wait_ge(s["ss3_ready"], at(b, 2, 2))
                rms(3, s["var3_ready"], s["r3_ready"], b)
            if pairs:
                pool.wait_ge(s["ss2_ready"], at(i, 2, 2))
                rms(2, s["var2_ready"], s["r2_ready"], i)

        both(pool, iteration)


def build(nc, x, condT, ln_w, ln_b, lin, colw, roww, out_b, wqkv, wo, wgh, wout, wup, wdn, hyper, bd, bu,
          ident, out):
    d = dict(x=x, condT=condT, ln_w=ln_w, ln_b=ln_b, lin=lin, colw=colw, roww=roww, out_b=out_b, wqkv=wqkv, wo=wo,
             wgh=wgh, wout=wout, wup=wup, wdn=wdn, hyper=hyper, bd=bd, bu=bu, ident=ident, out=out)
    d["hyp"] = nc.dram_tensor("hyp_scratch", (SEQS, P // SEQS, SEQS // 8, 2, 4, UNITS), F32).ap()
    d["cols"] = nc.dram_tensor("cols_scratch", (SEQS, P, 10), F32).ap()
    d["rows"] = nc.dram_tensor("rows_scratch", (SEQS, 4, D), F32).ap()
    with ExitStack() as ctx:
        def sb(name, shape, dt=F32):
            return ctx.enter_context(nc.sbuf_tensor(name, shape, dt))

        def split(name, shape):
            return [sb(f"{name}_hi", shape, F32R), sb(f"{name}_lo", shape, F32R)]

        t = {
            "wqkv": split("wqkv", [P, K, 3 * D]), "wo": split("wo", [P, K, D]), "wgh": split("wgh", [P, K, 2 * HID]),
            "wout": split("wout", [P, FT, D]), "wup": split("wup", [P, K, 2 * HID]),
            "wdq": sb("wdq", [P, FT, D], BF16), "ident": sb("ident", [P, P]), "ident_r": sb("ident_r", [P, P], F32R),
            "ident_b": sb("ident_b", [P, P], BF16), "w2": sb("w2", [P, D]), "bu": sb("bu", [P, D]),
            "bd": sb("bd", [P, 1]), "wmean": sb("wmean", [P, 1]),
        }
        setup_block(nc, ctx, d, t)
        main_block(nc, ctx, d, t)


def kernel(**inputs):
    import numpy as _np
    import concourse.bacc as _bacc
    from concourse import mybir as _mybir
    from concourse.bass_utils import run_bass_kernel_spmd as _run

    a = {n: _np.asarray(v) for n, v in inputs.items()}
    L1, L2 = "L1_cond_", "L2_cond_"
    rows = [
        _np.concatenate([a[L2 + "Wdd"].T, a[L2 + "Wd"].reshape(1, -1), a[L2 + "bdd"][None, :]]
                        ).reshape(C + 2, BN, K, P).transpose(0, 3, 2, 1).reshape(C + 2, P, K * BN),
        _np.concatenate([a[L2 + "Wdu"].T, a[L2 + "Wu"].reshape(1, -1), a[L2 + "bdu"][None, :]]
                        ).reshape(C + 2, D, BN).transpose(0, 2, 1),
    ]
    hyper = _np.concatenate(rows, axis=2).reshape(C + 2, P // SEQS, SEQS, UNITS).transpose(0, 2, 1, 3)
    arrays = {
        "x": a["x"], "condT": a["cond_256"].T, "ln_w": a["L0_cond_weight"], "ln_b": a["L0_cond_bias"],
        "lin": _np.concatenate([a["L0_cond_lin_w"].T, a["L0_cond_lin_b"][None, :]]),
        "colw": _np.stack([a[n].T for n in (L1 + "attn_gamma_w", L1 + "attn_beta_w", L1 + "ffn_gamma_w",
                                            L1 + "ffn_beta_w", "L3_cond_norm_w")], axis=1),
        "roww": _np.stack([a[L1 + "attn_alpha_w"].T, a[L1 + "ffn_alpha_w"].T], axis=1),
        "out_b": a[L1 + "out_b"],
        "wqkv": _np.concatenate([a[L1 + "W_q"].T, a[L1 + "W_k"].T, a[L1 + "W_v"].T], axis=1),
        "wo": a[L1 + "W_o"].T, "wgh": _np.concatenate([a[L1 + "gate_w"].T, a[L1 + "hidden_w"].T], axis=1),
        "wout": a[L1 + "out_w"].T, "wup": a["L3_cond_up_w"].T, "wdn": a["L3_cond_down_w"].T,
        "hyper": hyper,
        "bd": a[L2 + "bd"][:, None], "bu": a[L2 + "bu"], "ident": _np.eye(P, dtype=_np.float32),
    }
    arrays = {n: _np.ascontiguousarray(v) for n, v in arrays.items()}
    nc = _bacc.Bacc("TRN2", target_bir_lowering=False, num_devices=1)
    aps = {n: nc.dram_tensor(f"in_{n}", v.shape, _mybir.dt.from_np(v.dtype), kind="ExternalInput").ap()
           for n, v in arrays.items()}
    out = nc.dram_tensor("out_0", (SEQS, L, D), _mybir.dt.float32, kind="ExternalOutput").ap()
    build(nc, out=out, **aps)
    r = _run(nc, [{f"in_{n}": v for n, v in arrays.items()}], core_ids=[0])
    return r.results[0]["out_0"]
```

```python
from contextlib import ExitStack

import concourse.bass as bass
from concourse import mybir

F32 = mybir.dt.float32
F32R = mybir.dt.float32r
BF16 = mybir.dt.bfloat16
ALU = mybir.AluOpType
ACT = mybir.ActivationFunctionType
AX = mybir.AxisListType

P = 128
SEQS, L, D, C = 32, 256, 256, 64
T = L // P
K = D // P
HEADS, DH = 16, 16
PAIRS = HEADS // 2
SLOT = 64
SHIFT_ROW = 3 * DH
HID = 1024
FT = HID // P
BN = 128
UNITS = 2 * BN + D
DELTA = 0.1
EPS_LN, EPS_RMS, EPS_Q = 1e-5, 1e-6, 1e-5
QMAX = 127.0
ROUND = 12582912.0
SCORE_SCALE = 0.25
KV_BUFS, P_BUFS = 4, 3
PASSES = ((0, 0), (0, 1), (1, 0))
LEFT_LO_LAST = ((0, 0), (0, 1)), ((1, 0),)
RIGHT_LO_LAST = ((0, 0), (1, 0)), ((0, 1),)


def at(seq, per, n):
    reg, off = seq
    return off * per + n if reg is None else reg * per + (off * per + n)


def shifted(seq, by):
    return (seq[0], seq[1] + by)


def setup_block(nc, ctx, d, t):
    with ExitStack() as tmp:
        def sb(name, shape, dt=F32):
            return tmp.enter_context(nc.sbuf_tensor(name, shape, dt))

        def sem(name):
            return tmp.enter_context(nc.semaphore(name))

        LOAD_BUFS, BANKS = 4, 4
        SIDES = P // SEQS
        FILLS = P // SIDES
        TURN = 2 * BANKS
        stage_w = sb("stage_w", [P, 2, 2048])
        hload = sb("hload", [C + 2, LOAD_BUFS, SIDES, UNITS])
        hout = sb("hout", [P, 2, BANKS, UNITS])
        cond2 = sb("cond2", [C + 2, SEQS])
        cond1 = sb("cond1", [C + 1, SEQS])
        lin1 = sb("lin1", [C + 1, D])
        colw = sb("colw", [C, 5, D])
        roww = sb("roww", [C, 2, D])
        lnw = sb("lnw", [P, D])
        lnb = sb("lnb", [SEQS, D])
        outb = sb("outb", [SEQS, D])
        cols = sb("cols", [P, SEQS, 10])
        rows = sb("rows", [SEQS, 4, D])
        ones = sb("ones", [P, P])
        wsum = sb("wsum", [P, 1])
        wrec = sb("wrec", [P, 1])
        ps = tmp.enter_context(nc.psum_tensor("ps_setup", [P, 8, 512], F32))

        s_small = sem("small_loaded")
        s_w = sem("w_loaded")
        s_w2 = sem("w_loaded_odd")
        s_whi = sem("w_hi_ready")
        s_wlo = sem("w_lo_ready")
        s_h = [sem(f"h_loaded{n}") for n in range(LOAD_BUFS)]
        s_c2 = sem("scaled_cond_steps")
        s_hmm = sem("h_product_ready")
        s_hev = sem("h_scaled")
        s_hst = [sem(f"h_stored{n}") for n in range(2)]
        s_ms = sem("constants_ready")
        s_cmm = sem("cond_products_ready")
        s_tanh = sem("tanh_ready")
        s_row = sem("row_steps")
        s_col = sem("col_steps")
        s_st = sem("cond_stored")
        s_abs = sem("down_abs_steps")
        s_sum = sem("down_sum_ready")
        s_dn = sem("down_quantised")

        def pieces():
            yield d["wqkv"].rearrange("(k p) n -> p k n", p=P), t["wqkv"], K, 768
            yield d["wo"].rearrange("(k p) n -> p k n", p=P), t["wo"], K, D
            for k in range(K):
                yield d["wgh"][k * P:(k + 1) * P, :].unsqueeze(1), [w[:, k:k + 1, :] for w in t["wgh"]], 1, 2 * HID
            yield d["wout"].rearrange("(k p) n -> p k n", p=P), t["wout"], FT, D
            for k in range(K):
                yield d["wup"][k * P:(k + 1) * P, :].unsqueeze(1), [w[:, k:k + 1, :] for w in t["wup"]], 1, 2 * HID

        PIECES = list(pieces())
        N_SMALL = 10

        block = tmp.enter_context(nc.Block())

        def staged(n, k, cols_):
            return stage_w[:, n % 2, 0:k * cols_].rearrange("p (k n) -> p k n", k=k)

        @block.sync
        def _(sp):
            for dst, src in ((cond1[0:C, :], d["condT"]), (lin1[:, :], d["lin"]), (colw[:, :, :], d["colw"]),
                             (roww[:, :, :], d["roww"]), (lnw[:, :], d["ln_w"].partition_broadcast(P)),
                             (lnb[:, :], d["ln_b"].partition_broadcast(SEQS)),
                             (outb[:, :], d["out_b"].partition_broadcast(SEQS)),
                             (t["ident"][:, :], d["ident"]), (t["bd"][:, :], d["bd"]),
                             (t["bu"][:, :], d["bu"].partition_broadcast(P))):
                sp.dma_start(dst, src).then_inc(s_small, 16)
            for half in range(2):
                sp.sem_inc(s_hst[half], 16)

            def loads(fills, first=0):
                for n in fills:
                    sp.wait_ge(s_hmm, first + (n + 1))
                    for rows_ in (slice(0, C), slice(C, C + 2)):
                        sp.dma_start(hload[rows_, n % LOAD_BUFS, :, :], d["hyper"][rows_, first + n, :, :]
                                     ).then_inc(s_h[n % LOAD_BUFS], 16)

            def store(first, q, half):
                sp.wait_ge(s_hev, first + (BANKS + BANKS * (half + 1)))
                for j in range(SIDES):
                    sp.dma_start(d["hyp"][:, j, q, half, :, :],
                                 hout[j * SEQS:(j + 1) * SEQS, half, :, :]).then_inc(s_hst[half], 16)

            loads(range(LOAD_BUFS))
            sp.wait_ge(s_col, 2)
            sp.dma_start(d["cols"].rearrange("b p v -> p b v"), cols[:, :, :]).then_inc(s_st, 16)
            sp.wait_ge(s_row, 6)
            sp.dma_start(d["rows"], rows[:, :, :]).then_inc(s_st, 16)
            with sp.Fori(0, FILLS // TURN - 1) as r:
                for half in range(2):
                    loads(range((half + 1) * BANKS, (half + 2) * BANKS), r * TURN)
                    store(r * TURN, r, half)
            loads(range(BANKS, TURN), FILLS - TURN)
            for half in range(2):
                store(FILLS - TURN, FILLS // TURN - 1, half)
            sp.wait_ge(s_st, 32)
            for half in range(2):
                sp.wait_ge(s_hst[half], 16 + 16 * SIDES * (FILLS // TURN))

        @block.scalar
        def _(act):
            act.dma_start(stage_w[:, 0, :].rearrange("p (k n) -> p k n", k=FT),
                          d["wdn"].rearrange("(k p) n -> p k n", p=P)).then_inc(s_w, 16)
            act.dma_start(staged(1, PIECES[0][2], PIECES[0][3]), PIECES[0][0]).then_inc(s_w2, 16)
            act.wait_ge(s_cmm, 1)
            nc.scalar.activation(rows[:, 0, :], ps[0:SEQS, 6, 0:D], ACT.Tanh).then_inc(s_tanh, 1)
            act.wait_ge(s_small, 16 * N_SMALL)
            nc.scalar.copy(t["ident_r"][:, :], t["ident"][:, :]).then_inc(s_ms, 1)
            nc.scalar.copy(t["ident_b"][:, :], t["ident"][:, :]).then_inc(s_ms, 1)
            for n, (src, tiles, k, cols_) in enumerate(PIECES):
                m = n + 1
                if m < len(PIECES):
                    if n >= 1:
                        act.wait_ge(s_wlo, n)
                    else:
                        act.wait_ge(s_dn, 3)
                    act.dma_start(staged(m + 1, PIECES[m][2], PIECES[m][3]),
                                  PIECES[m][0]).then_inc(s_w if (m + 1) % 2 == 0 else s_w2, 16)
                buf = (n + 1) % 2
                act.wait_ge(s_w2 if buf else s_w, 16 * (n // 2 + 1 + (0 if buf else 1)))
                nc.scalar.copy(tiles[0][:, 0:k, :], staged(buf, k, cols_)).then_inc(s_whi, 1)

        @block.vector
        def _(dve):
            dve.memset(ones[:, :], 1.0).then_inc(s_abs, 1)
            dve.memset(cond1[C:C + 1, :], 1.0).then_inc(s_abs, 1)
            dve.memset(cond2[C:C + 2, :], DELTA).then_inc(s_c2, 1)
            dve.wait_ge(s_c2, 1)
            dve.memset(cond2[C:C + 1, :], 1.0).then_inc(s_c2, 1)
            dve.wait_ge(s_small, 16 * N_SMALL)
            dve.tensor_scalar(cond2[0:C, :], cond1[0:C, :], DELTA, None, ALU.mult).then_inc(s_c2, 1)
            wdn = stage_w[:, 0, :]
            dve.wait_ge(s_w, 16)
            dve.tensor_reduce(wsum[:, :], wdn, AX.X, ALU.add, apply_absolute_value=True).then_inc(s_abs, 1)
            dve.wait_ge(s_sum, 1)
            dve.tensor_scalar(t["wmean"][:, :], ps[:, 7, 0:1], 1.0 / (HID * D), EPS_Q, ALU.mult,
                              ALU.max).then_inc(s_abs, 1)
            dve.wait_ge(s_abs, 4)
            dve.reciprocal(wrec[:, :], t["wmean"][:, :]).then_inc(s_abs, 1)
            dve.wait_ge(s_abs, 5)
            dve.tensor_scalar(wdn, wdn, wrec[:, 0:1], ROUND, ALU.mult, ALU.add).then_inc(s_dn, 1)
            dve.wait_ge(s_dn, 1)
            dve.tensor_scalar(wdn, wdn, ROUND, 1.0, ALU.subtract, ALU.min).then_inc(s_dn, 1)
            dve.wait_ge(s_dn, 2)
            dve.tensor_scalar(t["wdq"][:, :, :], wdn.rearrange("p (k n) -> p k n", k=FT), -1.0, None,
                              ALU.max).then_inc(s_dn, 1)
            dve.wait_ge(s_cmm, 3)
            cps = ps[:, 4, 0:10 * SEQS].rearrange("p (v b) -> p v b", b=SEQS)
            cview = cols[:, :, :].rearrange("p b v -> p v b")
            dve.tensor_copy(cview[:, 0:8, :], cps[:, 0:8, :]).then_inc(s_col, 1)
            dve.tensor_scalar(cview[:, 8:10, :], cps[:, 8:10, :], 1.0, None, ALU.add).then_inc(s_col, 1)
            dve.wait_ge(s_small, 16 * N_SMALL)
            dve.tensor_copy(rows[:, 1:3, :], ps[0:SEQS, 5, :].rearrange("p (a n) -> p a n", a=2)).then_inc(s_row, 1)
            dve.wait_ge(s_tanh, 1)
            dve.tensor_tensor(rows[:, 0, :], rows[:, 0, :], lnb[:, :], ALU.add).then_inc(s_row, 1)
            dve.wait_ge(s_row, 2)
            dve.tensor_tensor(rows[:, 0, :], rows[:, 0, :], lnw[0:SEQS, :], ALU.mult).then_inc(s_row, 1)
            dve.wait_ge(s_row, 3)
            dve.tensor_tensor(rows[:, 0, :], rows[:, 0, :], lnb[:, :], ALU.add).then_inc(s_row, 1)
            dve.tensor_tensor(rows[:, 3, :], rows[:, 2, :], outb[:, :], ALU.mult).then_inc(s_row, 1)
            dve.tensor_tensor(t["w2"][:, :], lnw[:, :], lnw[:, :], ALU.mult).then_inc(s_row, 1)
            dve.sem_inc(s_hev, BANKS)
            with dve.Fori(0, FILLS // TURN) as r:
                for n in range(TURN):
                    dve.wait_ge(s_hmm, r * TURN + (LOAD_BUFS + n + 1))
                    half = n // BANKS
                    dve.wait_ge(s_hst[half], r * (16 * SIDES) + 16)
                    dve.tensor_copy(hout[:, half, n % BANKS, :], ps[:, n % BANKS, :]).then_inc(s_hev, 1)

        @block.gpsimd
        def _(pool):
            for n, (src, tiles, k, cols_) in enumerate(PIECES):
                pool.wait_ge(s_whi, n + 1)
                pool.tensor_tensor(tiles[1][:, 0:k, :], staged((n + 1) % 2, k, cols_), tiles[0][:, 0:k, :],
                                   ALU.subtract).then_inc(s_wlo, 1)

        @block.tensor
        def _(pe):
            pe.wait_ge(s_small, 16 * N_SMALL)
            pe.wait_ge(s_abs, 2)
            pe.matmul(ps[0:SEQS, 6, 0:D], cond1[:, :], lin1[:, :], start=True, stop=True).then_inc(s_cmm, 1)
            pe.matmul(ps[0:SEQS, 5, :], cond1[0:C, :], roww[:, :, :], start=True, stop=True).then_inc(s_cmm, 1)
            for v in range(5):
                for k in range(K):
                    c = (2 * v + k) * SEQS
                    mm = pe.matmul(ps[:, 4, c:c + SEQS], colw[:, v, k * P:(k + 1) * P], cond1[0:C, :],
                                   start=True, stop=True)
            mm.then_inc(s_cmm, 1)
            pe.wait_ge(s_abs, 3)
            pe.matmul(ps[:, 7, 0:1], ones[:, :], wsum[:, :], start=True, stop=True).then_inc(s_sum, 1)
            pe.sem_inc(s_hmm, LOAD_BUFS)
            pe.wait_ge(s_c2, 3)
            with pe.Fori(0, FILLS // TURN) as r:
                for n in range(TURN):
                    pe.wait_ge(s_h[n % LOAD_BUFS], r * (32 * (TURN // LOAD_BUFS)) + 32 * (n // LOAD_BUFS + 1))
                    pe.wait_ge(s_hev, r * TURN + (n + 1))
                    for j in range(SIDES):
                        mm = pe.matmul(ps[j * SEQS:(j + 1) * SEQS, n % BANKS, :], cond2[:, :],
                                       hload[:, n % LOAD_BUFS, j, :], start=True, stop=True)
                    mm.then_inc(s_hmm, 1)


def main_block(nc, ctx, d, t):
    def sb(name, shape, dt=F32):
        return ctx.enter_context(nc.sbuf_tensor(name, shape, dt))

    def over(name, host, offset, shape, dt):
        return nc.alloc_sbuf_tensor_at(name, shape, dt, offset=nc.lookup_mloc(host).addr + offset)

    def sem(name):
        return ctx.enter_context(nc.semaphore(name))

    KB = 1024
    xin = sb("xin", [P, T, D])
    xf = sb("xf", [P, T, D])
    xc = sb("xc", [P, T, D])
    q_st = sb("q_st", [P, T, HEADS, SLOT], F32R)
    k_st = sb("k_st", [P, T, HEADS, SLOT], F32R)
    v_ext = sb("v_ext", [P, T, HEADS, 2 * DH])
    k_even = sb("k_even", [P, KV_BUFS, L], F32R)
    k_odd = sb("k_odd", [P, KV_BUFS, L], F32R)
    q_t = sb("q_t", [P, KV_BUFS, L], F32R)
    probs = sb("probs", [P, P_BUFS, 2, T, L])
    o_t = sb("o_t", [P, HEADS // 4, L])
    xr = sb("xr", [P, T, D])
    o_tok = over("o_tok", probs, 0, [P, T, HEADS, DH], F32)
    oh = over("oh", probs, 2 * KB, [P, K, L], F32R)
    ol = over("ol", probs, 4 * KB, [P, K, L], F32R)
    xt = over("xt", probs, 6 * KB, [P, K, L], F32)
    xh = over("xh", probs, 8 * KB, [P, K, L], F32R)
    xl = over("xl", probs, 10 * KB, [P, K, L], F32R)
    xs = sb("xs", [P, T, D])
    bs = sb("bs", [P, T, D])
    bt = sb("bt", [P, K, L])
    bh = sb("bh", [P, K, L], F32R)
    bl = sb("bl", [P, K, L], F32R)
    xb = sb("xb", [P, T, D])
    th = sb("th", [P, T, D])
    gp = sb("gp", [P, L])
    hf = sb("hf", [P, 2, L])
    hh = sb("hh", [P, FT, L], F32R)
    hl = sb("hl", [P, FT, L], F32R)
    x2 = sb("x2", [P, T, D])
    x3 = sb("x3", [P, T, D])
    hyp = sb("hyp", [P, UNITS])
    hq = sb("hq", [P, T, HID], BF16)
    zt = over("zt", gp, 0, [P, L], F32)
    h3 = over("h3", hl, 0, [P, T, HID], F32)
    ge = over("ge", hh, 0, [P, 2, 512], F32)
    hq_t = over("hq_t", hh, 4 * KB, [P, FT, L], BF16)
    out_t = over("out_t", hq, 0, [P, T, D], F32)
    c0 = sb("c0", [P, D])
    alpha = sb("alpha", [P, D])
    frow = sb("frow", [P, 2, D])
    col_a = sb("col_a", [P, 4])
    col_f = sb("col_f", [P, 4])
    col_c = sb("col_c", [P, 2])
    stat = sb("stat", [P, T, 6])
    mv = sb("mv", [P, T, 3])
    v0 = sb("v0", [P, 4, T])
    r0 = sb("r0", [P, 4, T])
    ss = sb("ss", [P, 3, T])
    eps = sb("eps", [P, T])
    half = sb("half", [P, T])
    warm = sb("warm", [P, 1])
    mx = sb("mx", [P, T, HEADS])
    rden = sb("rden", [P, T, HEADS])
    am = sb("am", [P, T])
    am_half = sb("am_half", [P, 1])[:, 0:1]
    qs = sb("qs", [P, T])
    qi = sb("qi", [P, T])

    def bank(name, n):
        return ctx.enter_context(nc.psum_tensor(name, [P, n, 512], F32))

    S = bank("S", 2)
    ST = bank("ST", 2)
    TB = bank("TB", 1)
    OB = bank("OB", 1)
    M = bank("M", 2)
    M0, M1 = M[:, 0, :], M[:, 1, :]

    names = """table_loaded x_loaded c0_loaded col_a_loaded alpha_loaded frow_loaded col_f_loaded col_c_loaded
        hyp_loaded out_stored init_dve init_pool stat_ready mean_steps mean_ready var0_ready rstd0_ready
        norm_steps w2_ready xf_ready ss1_ready var1_ready r1_ready xs_ready xt_full xt_ready xh_ready xl_ready
        qk_full qk_hi qk_lo v_full v_ready carried t_full kq_ready s_full max_ready shift_ready tm_full
        qm_ready st_full exp_ready pv_done ot_ready otok_full rden_ready otok_ready ont_full oh_ready ol_ready
        y_full y_ready xr_ready ss2_ready var2_ready r2_ready bs_ready xb_ready bt_full bt_ready bh_ready
        bl_ready gu_full th_ready gp_ready hf_ready hh_ready hl_ready f_full fy_ready x2_ready x2b_ready
        at_full at_ready z_full z_ready up_full x3_ready ss3_ready var3_ready r3_ready ct_full ch_ready
        cl_ready gate_full ge_ready val_full h3_ready am_ready quant_steps hr_ready hq_ready hqt_full hqt_ready
        ly_full out_ready""".split()
    s = {n: sem(n) for n in names}

    block = ctx.enter_context(nc.Block())

    EARLY, SLOTS = 3, PAIRS + 4
    TILE_AT = {3: 0, 4: 1, 5: 2, 7: 3, 8: 4, 9: 5, 10: 6, 11: 7}
    TAIL_AT = 6

    def tile_bank(f):
        return (M0, M1)[(f if f < 3 else f + 1) % 2]

    def run(iteration):
        def one(i, reg=None):
            here = (reg, i)
            flag = (lambda o: True) if reg is not None else (lambda o: 0 <= i + o < SEQS)
            iteration(here, flag(1), flag(0), flag(-1), flag(-2))
        return one

    def both(eng, iteration):
        one = run(iteration)
        for i in (-1, 0, 1):
            one(i)
        with eng.Fori(0, SEQS - 3) as r:
            one(2, r)
        for i in (SEQS - 1, SEQS, SEQS + 1):
            one(i)

    def rows_of(x):
        return x.rearrange("(p t) n -> p t n", t=T)

    @block.sync
    def _(sp):
        def index(seq):
            reg, off = seq
            return off if reg is None else reg + off

        def iteration(i, front, pairs, ffn, tail):
            a, b, c = shifted(i, 1), shifted(i, -1), shifted(i, -2)
            if ffn:
                sp.wait_ge(s["xb_ready"], at(b, 1, 0))
                sp.wait_ge(s["fy_ready"], at(b, 1, 0))
                sp.dma_start(frow[:, :, :], d["rows"][index(b), 2:4, :].partition_broadcast(P)
                             ).then_inc(s["frow_loaded"], 16)
            if front:
                sp.wait_ge(s["norm_steps"], at(a, 2, 0))
                sp.dma_start(xin[:, :, :], rows_of(d["x"][index(a)])).then_inc(s["x_loaded"], 16)
                sp.wait_ge(s["xf_ready"], at(a, 1, 0))
                sp.dma_start(c0[:, :], d["rows"][index(a), 0, :].partition_broadcast(P)
                             ).then_inc(s["c0_loaded"], 16)
                sp.wait_ge(s["xt_ready"], at(a, 2, 0))
                sp.dma_start(col_a[:, :], d["cols"][index(a), :, 0:4]).then_inc(s["col_a_loaded"], 16)
            if pairs:
                sp.wait_ge(s["bt_ready"], at(i, 2, 0))
                sp.dma_start(col_f[:, :], d["cols"][index(i), :, 4:8]).then_inc(s["col_f_loaded"], 16)
            if ffn:
                sp.wait_ge(s["cl_ready"], at(b, 2, 0))
                sp.dma_start(col_c[:, :], d["cols"][index(b), :, 8:10]).then_inc(s["col_c_loaded"], 16)
                sp.wait_ge(s["up_full"], at(b, 1, 0))
                sp.dma_start(hyp[:, :], d["hyp"][index(b)].rearrange("j q h m u -> (j q h m) u")
                             ).then_inc(s["hyp_loaded"], 16)
            if pairs:
                sp.wait_ge(s["y_ready"], at(i, 1, 0))
                sp.dma_start(alpha[:, :], d["rows"][index(i), 1, :].partition_broadcast(P)
                             ).then_inc(s["alpha_loaded"], 16)
            if tail:
                sp.wait_ge(s["out_ready"], at(c, 2, 2))
                sp.dma_start(rows_of(d["out"][index(c)]), out_t[:, :, :]).then_inc(s["out_stored"], 16)

        both(sp, iteration)
        sp.wait_ge(s["out_stored"], 16 * SEQS)

    @block.tensor
    def _(pe):
        ident, ident_r, ident_b = t["ident"], t["ident_r"], t["ident_b"]

        def product(out, left, right, chunks, start=True, stop=True):
            for k in range(chunks):
                for n, (x, y) in enumerate(PASSES):
                    mm = pe.matmul(out, left(x, k), right(y, k), start=(start and k == 0 and n == 0),
                                   stop=(stop and k == chunks - 1 and n == len(PASSES) - 1))
            return mm

        def product_as_ready(out, left, right, chunks, steps, lo_ready):
            for step, passes in enumerate(steps):
                if step == 1 and lo_ready is not None:
                    lo_ready()
                for k in range(chunks):
                    for n, (x, y) in enumerate(passes):
                        mm = pe.matmul(out, left(x, k), right(y, k), start=(step == 0 and k == 0 and n == 0),
                                       stop=(step == 1 and k == chunks - 1 and n == len(passes) - 1))
            return mm

        def to_features(out, src):
            for k in range(K):
                for tt in range(T):
                    c = (k * T + tt) * P
                    mm = pe.transpose(out[:, c:c + P], src[:, tt, k * P:(k + 1) * P], ident[:, :])
            return mm

        xparts, bparts, oparts = (xh, xl), (bh, bl), (oh, ol)

        def pair_in(i, p):
            if p == 0:
                pe.wait_ge(s["qk_lo"], at(i, 4, 4))
                pe.wait_ge(s["qm_ready"], at(i, PAIRS, 0))
            elif p <= 2:
                pe.wait_ge(s["kq_ready"], at(i, 3 * PAIRS, 3 * p))
            else:
                pe.wait_ge(s["qm_ready"], at(i, PAIRS, p - 2))
            for c, st in ((0, k_st), (L, q_st)):
                for tt in range(T):
                    mm = pe.transpose(TB[:, 0, c + tt * P:c + (tt + 1) * P].bitcast(F32R),
                                      st[:, tt, 2 * p:2 * p + 2, :], ident_r[:, :])
            mm.then_inc(s["t_full"], 1)

        def scores(i, p):
            pe.wait_ge(s["kq_ready"], at(i, 3 * PAIRS, 3 * p + 3))
            if p >= 1:
                pe.wait_ge(s["max_ready"], at(i, PAIRS, p))
            for tt in range(T):
                for h, kk in enumerate((k_even, k_odd)):
                    mm = pe.matmul(S[:, tt, h * L:(h + 1) * L], q_t[:, p % KV_BUFS, tt * P:(tt + 1) * P],
                                   kk[:, p % KV_BUFS, :], start=True, stop=True)
            mm.then_inc(s["s_full"], 1)

        def pair_shift(i, p):
            pe.wait_ge(s["shift_ready"], at(i, PAIRS, p + 1))
            if p == 0:
                pe.wait_ge(s["kq_ready"], at(i, 3 * PAIRS, 9))
            elif p < PAIRS - 2:
                pe.wait_ge(s["kq_ready"], at(i, 3 * PAIRS, 3 * (p + 3)))
            else:
                pe.wait_ge(s["qm_ready"], at(i, PAIRS, p))
            for tt in range(T):
                mm = pe.transpose(TB[:, 0, tt * P:(tt + 1) * P].bitcast(F32R), q_st[:, tt, 2 * p:2 * p + 2, :],
                                  ident_r[:, :])
            mm.then_inc(s["tm_full"], 1)

        def key_scores(i, p):
            pe.wait_ge(s["qm_ready"], at(i, PAIRS, p + 1))
            if p >= 1:
                pe.wait_ge(s["exp_ready"], at(i, PAIRS, p))
            else:
                pe.wait_ge(s["ol_ready"], at(i, 1, 0))
                pe.wait_ge(s["bt_ready"], at(i, 2, 0))
                pe.wait_ge(s["v_ready"], at(i, 1, 1))
            for h, kk in enumerate((k_even, k_odd)):
                for kb in range(T):
                    mm = pe.matmul(ST[:, h, kb * L:(kb + 1) * L], kk[:, p % KV_BUFS, kb * P:(kb + 1) * P],
                                   q_t[:, p % KV_BUFS, :], start=True, stop=True)
            mm.then_inc(s["st_full"], 1)

        def values(i, g):
            pe.wait_ge(s["exp_ready"], at(i, PAIRS, 2 * g + 2))
            if g == 0:
                pe.wait_ge(s["y_ready"], at(i, 1, 0))
            if g == 2:
                pe.wait_ge(s["ot_ready"], at(i, 2, 1))
            for kb in range(T):
                for j in range(4):
                    mm = pe.matmul(OB[32 * j:32 * j + 32, 0, (g % 2) * L:(g % 2 + 1) * L],
                                   v_ext[:, kb, 4 * g + j, :], probs[:, (2 * g + j // 2) % P_BUFS, j % 2, kb, :],
                                   start=(kb == 0), stop=(kb == T - 1))
            mm.then_inc(s["pv_done"], 1)

        def hidden_tile(b, tail, f, halves=(0, 1)):
            if f == 0 and 0 in halves:
                pe.wait_ge(s["bh_ready"], at(b, 2, 2))
                pe.wait_ge(s["ge_ready"], at(b, 4, 0))
            elif f == 1:
                pe.wait_ge(s["h3_ready"], at(b, 4, 0))
            elif f >= 2:
                pe.wait_ge(s["hf_ready"], at(b, FT, 3 if f == 3 else f - 1))
            if tail and f == 3:
                pe.wait_ge(s["hqt_ready"], at(b, 2, 0))
            if tail and f == 4:
                pe.wait_ge(s["out_ready"], at(b, 2, 0))
            def low_ready():
                pe.wait_ge(s["bl_ready"], at(b, 2, 2))

            for g in halves:
                mm = product_as_ready(tile_bank(f)[:, g * L:(g + 1) * L],
                                      lambda x, k: t["wgh"][x][:, k, g * HID + f * P:g * HID + (f + 1) * P],
                                      lambda y, k: bparts[y][:, k, :], K, RIGHT_LO_LAST,
                                      low_ready if f == 0 and g == 0 else None)
            if 1 in halves:
                mm.then_inc(s["gu_full"], 1)

        def quantised_to_features(c, ffn, tt):
            pe.wait_ge(s["hq_ready"], at(c, 2, tt + 1))
            if ffn:
                pe.wait_ge(s["hf_ready"], at(c, FT, FT + tt + 2))
            elif tt == 0:
                pe.wait_ge(s["h3_ready"], at(c, 4, 4))
            else:
                pe.wait_ge(s["ge_ready"], at(c, 4, 4))
            for f in range(FT):
                mm = pe.transpose((M1, M0)[tt].bitcast(BF16)[:, f * P:(f + 1) * P], hq[:, tt, f * P:(f + 1) * P],
                                  ident_b[:, :])
            mm.then_inc(s["hqt_full"], 1)

        def quantised_down(c):
            pe.wait_ge(s["hqt_ready"], at(c, 2, 2))
            for tt in range(T):
                for f in range(FT):
                    mm = pe.matmul(M1[:, tt * D:(tt + 1) * D], hq_t[:, f, tt * P:(tt + 1) * P], t["wdq"][:, f, :],
                                   start=(f == 0), stop=(f == FT - 1))
            mm.then_inc(s["ly_full"], 1)

        def hidden_down(tt, chunks):
            for f in chunks:
                mm = product(TB[:, 0, tt * D:(tt + 1) * D], lambda x, k: (hh, hl)[x][:, f, tt * P:(tt + 1) * P],
                             lambda y, k: t["wout"][y][:, f, :], 1, start=(f == 0), stop=(f == FT - 1))
            return mm

        def qk_project(tt):
            product(S[:, tt, :], lambda x, k: xparts[x][:, k, tt * P:(tt + 1) * P],
                    lambda y, k: t["wqkv"][y][:, k, 0:2 * D], K).then_inc(s["qk_full"], 1)

        def v_project(tt, chunks):
            for k in chunks:
                mm = product(ST[:, 1, tt * D:(tt + 1) * D], lambda x, _: xparts[x][:, k, tt * P:(tt + 1) * P],
                             lambda y, _: t["wqkv"][y][:, k, 2 * D:3 * D], 1, start=(k == 0), stop=(k == K - 1))
            return mm

        def out_project(i, tt):
            pe.wait_ge(s["ol_ready"], at(i, 1, 1))
            return product(OB[:, 0, tt * D:(tt + 1) * D], lambda x, k: oparts[x][:, k, tt * P:(tt + 1) * P],
                           lambda y, k: t["wo"][y][:, k, :], K)

        def up(bank, b, r, half):
            tt, n = r // 2, r % 2

            def low_ready():
                pe.wait_ge(s["cl_ready"], at(b, 2, 2))

            return product_as_ready(
                bank, lambda x, k: bparts[x][:, k, tt * P:(tt + 1) * P],
                lambda y, k: t["wup"][y][:, k, half * HID + n * 512:half * HID + (n + 1) * 512], K, LEFT_LO_LAST,
                low_ready if r == 0 and half == 1 else None)

        def gate(b, r):
            if r >= 1:
                pe.wait_ge(s["ge_ready"], at(b, 4, r))
            up(M0, b, r, 1).then_inc(s["gate_full"], 1)

        def value(b, r, bank):
            if r in (1, 2):
                pe.wait_ge(s["h3_ready"], at(b, 4, r))
            up(bank, b, r, 0).then_inc(s["val_full"], 1)

        def iteration(i, front, pairs, ffn, tail):
            a, b, c = shifted(i, 1), shifted(i, -1), shifted(i, -2)
            for slot in range(EARLY, SLOTS):
                if slot == EARLY:
                    if ffn:
                        hidden_tile(b, tail, 0, (0,))
                    if pairs:
                        pair_in(i, slot)
                    if ffn:
                        hidden_tile(b, tail, 0, (1,))
                    if pairs:
                        key_scores(i, slot - 3)
                        pair_shift(i, slot - 2)
                    continue
                if pairs and slot <= TAIL_AT:
                    scores(i, slot - 1)
                if pairs and slot < PAIRS:
                    pair_in(i, slot)
                if pairs and TAIL_AT < slot <= PAIRS:
                    scores(i, slot - 1)
                if tail and slot == TAIL_AT:
                    quantised_to_features(c, ffn, 0)
                if tail and slot == TAIL_AT + 1:
                    quantised_down(c)
                if ffn and slot in TILE_AT:
                    hidden_tile(b, tail, TILE_AT[slot])
                if pairs and slot == TAIL_AT:
                    values(i, 0)
                if pairs and slot < PAIRS + 2:
                    pair_shift(i, slot - 2)
                if pairs and slot < PAIRS + 3:
                    key_scores(i, slot - 3)
                if tail and slot == TAIL_AT:
                    quantised_to_features(c, ffn, 1)
                if pairs and slot >= 7 and slot % 2 and slot < SLOTS - 1:
                    values(i, (slot - 5) // 2)
            if ffn:
                pe.wait_ge(s["hl_ready"], at(b, FT, FT - 2))
                if pairs:
                    pe.wait_ge(s["qm_ready"], at(i, PAIRS, PAIRS))
                hidden_down(0, range(FT - 2))
                pe.wait_ge(s["hl_ready"], at(b, FT, FT - 1))
                hidden_down(0, (FT - 2,))
            if pairs:
                values(i, HEADS // 4 - 1)
            if ffn:
                pe.wait_ge(s["hl_ready"], at(b, FT, FT))
                hidden_down(0, (FT - 1,))
            if front:
                pe.wait_ge(s["xs_ready"], at(a, 2, 2))
                to_features(M1, xs).then_inc(s["xt_full"], 1)
            if ffn:
                hidden_down(1, range(FT // 2))
            if pairs:
                pe.wait_ge(s["ot_ready"], at(i, 2, 2))
                pe.wait_ge(s["max_ready"], at(i, PAIRS, PAIRS))
                for tt in range(T):
                    for g in range(HEADS // 4):
                        mm = pe.transpose(S[:, tt, g * P:(g + 1) * P], o_t[:, g, tt * P:(tt + 1) * P], ident[:, :])
                    mm.then_inc(s["otok_full"], 1)
            if ffn:
                hidden_down(1, range(FT // 2, FT)).then_inc(s["f_full"], 1)
            if pairs:
                pe.wait_ge(s["otok_ready"], at(i, 2, 2))
                pe.wait_ge(s["exp_ready"], at(i, PAIRS, PAIRS))
                to_features(ST[:, 0, :], o_tok[:, :, :, :].rearrange("p t h e -> p t (h e)")
                            ).then_inc(s["ont_full"], 1)
            if front:
                pe.wait_ge(s["xl_ready"], at(a, 1, 1))
                pe.wait_ge(s["otok_ready"], at(a, 2, 0))
                qk_project(0)
            if ffn:
                pe.wait_ge(s["x2_ready"], at(b, 1, 1))
                to_features(M0, x2).then_inc(s["at_full"], 1)
            if front:
                qk_project(1)
            if ffn:
                pe.wait_ge(s["at_ready"], at(b, 1, 1))
                pe.wait_ge(s["hyp_loaded"], at(b, 16, 16))
                for k in range(K):
                    mm = pe.matmul(M1[:, 0:L], hyp[:, k * BN:(k + 1) * BN], bt[:, k, :], start=(k == 0),
                                   stop=(k == K - 1))
                mm.then_inc(s["z_full"], 1)
            if pairs:
                out_project(i, 0)
            if ffn:
                pe.wait_ge(s["z_ready"], at(b, 1, 1))
                for tt in range(T):
                    mm = pe.matmul(M0[:, tt * D:(tt + 1) * D], zt[:, tt * P:(tt + 1) * P], hyp[:, K * BN:UNITS],
                                   start=True, stop=True)
                mm.then_inc(s["up_full"], 1)
            if pairs:
                out_project(i, 1).then_inc(s["y_full"], 1)
            if front:
                v_project(0, (0,))
            if ffn:
                pe.wait_ge(s["x3_ready"], at(b, 1, 1))
                to_features(M1, x3).then_inc(s["ct_full"], 1)
            if front:
                v_project(0, (1,))
                v_project(1, (0, 1)).then_inc(s["v_full"], 1)
                pair_in(a, 0)
            if ffn:
                pe.wait_ge(s["ch_ready"], at(b, 2, 2))
                gate(b, 0)
            if front:
                scores(a, 0)
            if ffn:
                value(b, 0, M1)
                gate(b, 1)
            if front:
                pair_in(a, 1)
            if ffn:
                value(b, 1, M1)
                gate(b, 2)
            if front:
                scores(a, 1)
            if pairs:
                pe.wait_ge(s["bs_ready"], at(i, 2, 2))
                if front:
                    pe.wait_ge(s["v_ready"], at(a, 1, 1))
                to_features(ST[:, 1, :], bs).then_inc(s["bt_full"], 1)
            if front:
                pair_in(a, 2)
            if ffn:
                gate(b, 3)
                value(b, 2, M1)
                if pairs:
                    pe.wait_ge(s["y_ready"], at(i, 1, 1))
                value(b, 3, OB[:, 0, :])
            if front:
                pair_shift(a, 0)
                scores(a, 2)

        pe.wait_ge(s["init_dve"], 5)
        pe.wait_ge(s["init_pool"], 2)
        both(pe, iteration)

    @block.scalar
    def _(act):
        A = nc.scalar.activation

        def square_sums(src, junk, which, ready):
            for tt in range(T):
                A(junk[:, tt, :], src[:, tt, :], ACT.Square, scale=D ** -0.5, accum_out=ss[:, which, tt:tt + 1]
                  ).then_inc(ready, 1)

        def pair_out(i, p):
            buf = p % KV_BUFS
            act.wait_ge(s["t_full"], at(i, PAIRS, p + 1))
            for dst, src in ((k_even[0:SLOT, buf, :], TB[0:SLOT, 0, 0:L]), (k_odd[SLOT:P, buf, :], TB[SLOT:P, 0, 0:L]),
                             (q_t[:, buf, :], TB[:, 0, L:2 * L])):
                nc.scalar.copy(dst, src).then_inc(s["kq_ready"], 1)

        def shifted_q(i, p):
            act.wait_ge(s["tm_full"], at(i, PAIRS, p + 1))
            nc.scalar.copy(q_t[:, p % KV_BUFS, :], TB[:, 0, 0:L]).then_inc(s["qm_ready"], 1)

        def quantised_out(c):
            act.wait_ge(s["hqt_full"], at(c, 2, 1))
            nc.scalar.copy(hq_t[:, :, 0:P],
                           M1.bitcast(BF16).rearrange("p (f n) -> p f n", f=FT)).then_inc(s["hqt_ready"], 1)

        def hidden_high(b, f):
            act.wait_ge(s["hf_ready"], at(b, FT, f + 1))
            nc.scalar.copy(hh[:, f, :], hf[:, f % 2, :]).then_inc(s["hh_ready"], 1)

        def outputs(i, n):
            act.wait_ge(s["pv_done"], at(i, 4, 2 * n + 2))
            nc.scalar.copy(o_t[:, 2 * n:2 * n + 2, :].rearrange("p g n -> p (g n)"), OB[:, 0, :]
                           ).then_inc(s["ot_ready"], 1)

        def high_parts(a, tt):
            act.wait_ge(s["qk_full"], at(a, 2, tt + 1))
            src = S[:, tt, :].rearrange("p (o h e) -> p o h e", o=2, h=HEADS)
            q_dst = q_st[:, tt, :, 0:2 * DH].rearrange("p h (r e) -> p h r e", r=2)
            k_dst = k_st[:, tt, :, :].rearrange("p h (r e) -> p h r e", e=DH)[:, :, 0:3:2, :]
            nc.scalar.copy(q_dst, src[:, 0, :, :].unsqueeze(2).to_broadcast([P, HEADS, 2, DH])
                           ).then_inc(s["qk_hi"], 1)
            nc.scalar.copy(k_dst, src[:, 1, :, :].unsqueeze(2).to_broadcast([P, HEADS, 2, DH])
                           ).then_inc(s["qk_hi"], 1)

        def iteration(i, front, pairs, ffn, tail):
            a, b, c = shifted(i, 1), shifted(i, -1), shifted(i, -2)
            for slot in range(EARLY, SLOTS):
                if pairs and slot < PAIRS:
                    pair_out(i, slot)
                if ffn and slot in (EARLY + 1, EARLY + 2):
                    hidden_high(b, TILE_AT[slot - 1])
                if pairs and EARLY < slot <= EARLY + 2:
                    shifted_q(i, slot - 2)
                if ffn and slot in TILE_AT:
                    f = TILE_AT[slot]
                    act.wait_ge(s["gu_full"], at(b, FT, f + 1))
                    A(th[:, f % 2, :], tile_bank(f)[:, 0:L], ACT.Tanh, scale=0.5).then_inc(s["th_ready"], 1)
                if pairs and slot < PAIRS + 2 and slot not in (EARLY + 1, EARLY + 2):
                    shifted_q(i, slot - 2)
                if tail and slot == TAIL_AT:
                    quantised_out(c)
                if pairs and slot < PAIRS + 3:
                    p = slot - 3
                    act.wait_ge(s["st_full"], at(i, PAIRS, p + 1))
                    A(probs[:, p % P_BUFS, :, :, :].rearrange("p h k q -> p (h k q)"),
                      ST[:, :, :].rearrange("p h n -> p (h n)"), ACT.Exp, scale=SCORE_SCALE
                      ).then_inc(s["exp_ready"], 1)
                if ffn and slot in TILE_AT and slot > EARLY + 1:
                    hidden_high(b, TILE_AT[slot])
                if pairs and slot == 7:
                    outputs(i, 0)
                if front and slot == PAIRS + 2:
                    act.wait_ge(s["xf_ready"], at(a, 1, 1))
                    act.wait_ge(s["xt_full"], at(a, 1, 0))
                    square_sums(xf, xs, 0, s["ss1_ready"])
                if front and slot == PAIRS + 3:
                    act.wait_ge(s["r1_ready"], at(a, 1, 1))
                    act.wait_ge(s["ss1_ready"], at(a, 2, 2))
                    for tt in range(T):
                        A(xs[:, tt, :], xf[:, tt, :], ACT.Copy, scale=r0[:, 1, tt:tt + 1]
                          ).then_inc(s["xs_ready"], 1)
            if pairs:
                outputs(i, 1)
            if front:
                act.wait_ge(s["xt_ready"], at(a, 2, 2))
                nc.scalar.copy(xh[:, :, :], xt[:, :, :]).then_inc(s["xh_ready"], 1)
            if pairs:
                act.wait_ge(s["ont_full"], at(i, 1, 1))
                nc.scalar.copy(oh[:, :, :].rearrange("p k n -> p (k n)"), ST[:, 0, :]).then_inc(s["oh_ready"], 1)
            if front:
                high_parts(a, 0)
            if ffn:
                act.wait_ge(s["at_full"], at(b, 1, 1))
                nc.scalar.copy(bt[:, :, :].rearrange("p k n -> p (k n)"), M0).then_inc(s["at_ready"], 1)
            if front:
                high_parts(a, 1)
            if ffn:
                act.wait_ge(s["z_full"], at(b, 1, 1))
                A(zt[:, :], M1[:, 0:L], ACT.Relu, bias=t["bd"][:, 0:1]).then_inc(s["z_ready"], 1)
                act.wait_ge(s["x3_ready"], at(b, 1, 1))
                act.wait_ge(s["bt_full"], at(b, 1, 1))
                square_sums(x3, bs, 2, s["ss3_ready"])
                act.wait_ge(s["ct_full"], at(b, 1, 1))
                act.wait_ge(s["col_c_loaded"], at(b, 16, 16))
                for k in range(K):
                    A(bh[:, k, :], M1[:, k * L:(k + 1) * L], ACT.Copy, scale=col_c[:, k:k + 1]
                      ).then_inc(s["ch_ready"], 1)
            if front:
                act.wait_ge(s["v_full"], at(a, 1, 1))
                nc.scalar.copy(v_ext[:, :, :, 0:DH], ST[:, 1, :].rearrange("p (t h e) -> p t h e", t=T, h=HEADS)
                               ).then_inc(s["v_ready"], 1)

            def feed_high(tt):
                if ffn:
                    act.wait_ge(s["val_full"], at(b, 4, 2 * tt + 2))
                act.wait_ge(s["bt_ready"], at(i, 2, 2))
                nc.scalar.copy(bh[:, :, tt * P:(tt + 1) * P], bt[:, :, tt * P:(tt + 1) * P]
                               ).then_inc(s["bh_ready"], 1)

            def gelu(r):
                if r == 0:
                    act.wait_ge(s["r3_ready"], at(b, 1, 1))
                if r >= 2:
                    act.wait_ge(s["h3_ready"], at(b, 4, r - 1))
                act.wait_ge(s["gate_full"], at(b, 4, r + 1))
                A(ge[:, r % 2, :], M0, ACT.Gelu, scale=r0[:, 3, r // 2:r // 2 + 1]).then_inc(s["ge_ready"], 1)

            if front:
                pair_out(a, 0)
            if ffn:
                gelu(0)
            if pairs:
                act.wait_ge(s["xr_ready"], at(i, 1, 1))
                act.wait_ge(s["bt_full"], at(i, 1, 0))
                square_sums(xr, bs, 1, s["ss2_ready"])
            if ffn:
                gelu(1)
            if front:
                pair_out(a, 1)
            if pairs:
                act.wait_ge(s["r2_ready"], at(i, 1, 1))
                act.wait_ge(s["ss2_ready"], at(i, 2, 2))
                for tt in range(T):
                    A(bs[:, tt, :], xr[:, tt, :], ACT.Copy, scale=r0[:, 2, tt:tt + 1]).then_inc(s["bs_ready"], 1)
            if front:
                act.wait_ge(s["xf_ready"], at(a, 1, 1))
                act.wait_ge(s["xr_ready"], at(a, 1, 0))
                nc.scalar.copy(xc[:, :, :], xf[:, :, :]).then_inc(s["carried"], 1)
            if ffn:
                gelu(2)
            if pairs:
                act.wait_ge(s["bt_full"], at(i, 1, 1))
                act.wait_ge(s["col_f_loaded"], at(i, 16, 16))
                for k in range(K):
                    A(bt[:, k, :], ST[:, 1, k * L:(k + 1) * L], ACT.Identity, scale=col_f[:, k:k + 1],
                      bias=col_f[:, 2 + k:3 + k]).then_inc(s["bt_ready"], 1)
                feed_high(0)
            if front:
                pair_out(a, 2)
            if ffn:
                gelu(3)
                act.wait_ge(s["table_loaded"], at(b, 1, 0))
                A(warm[:, :], eps[:, 0:1], ACT.Exp).then_inc(s["table_loaded"], 1)
            if pairs:
                feed_high(1)
            if front:
                shifted_q(a, 0)

        both(act, iteration)

    @block.vector
    def _(dve):
        dve.memset(half[:, :], -0.5).then_inc(s["init_dve"], 1)
        dve.memset(eps[:, :], EPS_RMS).then_inc(s["init_dve"], 1)
        dve.memset(v_ext[:, :, :, :], 1.0).then_inc(s["init_dve"], 1)
        dve.memset(k_even[:, :, :].bitcast(F32), 0.0).then_inc(s["init_dve"], 1)
        dve.memset(k_odd[:, :, :].bitcast(F32), 0.0).then_inc(s["init_dve"], 1)

        def modulated(dst, src, col, ready):
            for k in range(K):
                dve.tensor_scalar(dst[:, k, :], src[:, k * L:(k + 1) * L], col[:, k:k + 1], col[:, 2 + k:3 + k],
                                  ALU.mult, ALU.add).then_inc(ready, 1)

        def maximum(i, p):
            dve.wait_ge(s["s_full"], at(i, PAIRS, p + 1))
            dve.tensor_reduce(mx[:, :, 2 * p:2 * p + 2], S[:, :, :].rearrange("p t (h n) -> p t h n", h=2), AX.X,
                              ALU.max).then_inc(s["max_ready"], 1)
            dve.wait_ge(s["max_ready"], at(i, PAIRS, p + 1))
            dve.tensor_scalar(q_st[:, :, 2 * p:2 * p + 2, SHIFT_ROW], mx[:, :, 2 * p:2 * p + 2], -1.0, None,
                              ALU.mult).then_inc(s["shift_ready"], 1)

        def low_parts(a, tt):
            dve.wait_ge(s["qk_hi"], at(a, 4, 2 * tt + 2))
            dve.memset(q_st[:, tt, :, SHIFT_ROW:SHIFT_ROW + 1].bitcast(F32), 0.0)
            src = S[:, tt, :].rearrange("p (o h e) -> p o h e", o=2, h=HEADS)
            dve.tensor_tensor(q_st[:, tt, :, 2 * DH:3 * DH], src[:, 0, :, :], q_st[:, tt, :, 0:DH],
                              ALU.subtract).then_inc(s["qk_lo"], 1)
            dve.tensor_tensor(k_st[:, tt, :, DH:2 * DH], src[:, 1, :, :], k_st[:, tt, :, 0:DH],
                              ALU.subtract).then_inc(s["qk_lo"], 1)

        def gated(b, r):
            tt, n = r // 2, r % 2
            dve.wait_ge(s["val_full"], at(b, 4, r + 1))
            dve.wait_ge(s["ge_ready"], at(b, 4, r + 1))
            dve.scalar_tensor_tensor(out=h3[:, tt, n * 512:(n + 1) * 512], in0=M1 if r < 3 else OB[:, 0, :],
                                     scalar=r0[:, 3, tt:tt + 1],
                                     in1=ge[:, r % 2, :], op0=ALU.mult, op1=ALU.mult).then_inc(s["h3_ready"], 1)

        def largest(b):
            dve.wait_ge(s["h3_ready"], at(b, 4, 2))
            dve.tensor_reduce(am[:, 0:1], h3[:, 0, :], AX.X, ALU.max, apply_absolute_value=True
                              ).then_inc(s["am_ready"], 1)

        def largest_half(b, n):
            dve.wait_ge(s["h3_ready"], at(b, 4, 3 + n))
            dve.tensor_reduce((am_half, am[:, 1:2])[n], h3[:, 1, n * 512:(n + 1) * 512], AX.X, ALU.max,
                              apply_absolute_value=True).then_inc(s["am_ready"], 1)

        def floor_of_half(b):
            dve.wait_ge(s["am_ready"], at(b, 3, 2))
            dve.tensor_scalar(am_half, am_half, EPS_Q, 1.0 / QMAX, ALU.max, ALU.mult).then_inc(s["quant_steps"], 1)

        def quant_scale(b, tt):
            if tt == 0:
                dve.wait_ge(s["am_ready"], at(b, 3, 1))
                dve.tensor_scalar(am[:, 0:1], am[:, 0:1], EPS_Q, 1.0 / QMAX, ALU.max, ALU.mult
                                  ).then_inc(s["quant_steps"], 1)
            else:
                dve.wait_ge(s["am_ready"], at(b, 3, 3))
                dve.wait_ge(s["quant_steps"], at(b, 5, 3))
                dve.tensor_scalar(am[:, 1:2], am[:, 1:2], 1.0 / QMAX, am_half, ALU.mult, ALU.max
                                  ).then_inc(s["quant_steps"], 1)
            dve.wait_ge(s["quant_steps"], at(b, 5, 3 * tt + 1))
            dve.reciprocal(qs[:, tt:tt + 1], am[:, tt:tt + 1]).then_inc(s["quant_steps"], 1)
            dve.tensor_scalar(qi[:, tt:tt + 1], am[:, tt:tt + 1], t["wmean"][:, 0:1], None, ALU.mult)

        def scaled_up(b, tt):
            dve.wait_ge(s["quant_steps"], at(b, 5, 3 * tt + 2))
            dve.tensor_scalar(h3[:, tt, :], h3[:, tt, :], qs[:, tt:tt + 1], ROUND, ALU.mult, ALU.add
                              ).then_inc(s["hr_ready"], 1)

        def quantise(b, tt):
            dve.wait_ge(s["hr_ready"], at(b, 2, tt + 1))
            if tt == 0:
                dve.wait_ge(s["out_stored"], at(b, 16, 0))
            dve.tensor_scalar(hq[:, tt, :], h3[:, tt, :], ROUND, QMAX, ALU.subtract, ALU.min
                              ).then_inc(s["hq_ready"], 1)

        def iteration(i, front, pairs, ffn, tail):
            a, b, c = shifted(i, 1), shifted(i, -1), shifted(i, -2)

            for slot in range(EARLY, SLOTS):
                if pairs and EARLY < slot <= PAIRS:
                    maximum(i, slot - 1)
                if tail and slot == TAIL_AT:
                    dve.wait_ge(s["hqt_full"], at(c, 2, 2))
                    dve.wait_ge(s["hqt_ready"], at(c, 2, 1))
                    dve.tensor_copy(hq_t[:, :, P:2 * P], M0.bitcast(BF16).rearrange("p (f n) -> p f n", f=FT)
                                    ).then_inc(s["hqt_ready"], 1)
                if tail and slot == EARLY + 1:
                    largest_half(c, 1)
                if tail and slot == TAIL_AT + 1:
                    dve.wait_ge(s["ly_full"], at(c, 1, 1))
                    for tt in range(T):
                        dve.scalar_tensor_tensor(out=out_t[:, tt, :], in0=M1[:, tt * D:(tt + 1) * D],
                                                 scalar=qi[:, tt:tt + 1], in1=x3[:, tt, :], op0=ALU.mult,
                                                 op1=ALU.add).then_inc(s["out_ready"], 1)
                if ffn and slot in TILE_AT:
                    f = TILE_AT[slot]
                    bk = tile_bank(f)
                    dve.wait_ge(s["th_ready"], at(b, FT, f + 1))
                    dve.scalar_tensor_tensor(out=gp[:, :], in0=th[:, f % 2, :], scalar=1.0, in1=bk[:, 0:L],
                                             op0=ALU.add, op1=ALU.mult).then_inc(s["gp_ready"], 1)
                    dve.wait_ge(s["gp_ready"], at(b, FT, f + 1))
                    if f >= 2:
                        dve.wait_ge(s["hl_ready"], at(b, FT, f - 1))
                    dve.scalar_tensor_tensor(out=hf[:, f % 2, :], in0=gp[:, :], scalar=0.5, in1=bk[:, L:2 * L],
                                             op0=ALU.mult, op1=ALU.mult).then_inc(s["hf_ready"], 1)
                if tail and slot == TAIL_AT - 1:
                    quant_scale(c, 1)
                    scaled_up(c, 1)
                    quantise(c, 1)
                if front and slot == PAIRS - 1:
                    dve.wait_ge(s["x_loaded"], at(a, 16, 16))
                    for tt in range(T):
                        dve.bn_stats(stat[:, tt, :], xin[:, tt, :]).then_inc(s["stat_ready"], 1)
                    dve.wait_ge(s["stat_ready"], at(a, 2, 2))
                    for n, (j, op) in enumerate(((1, ALU.add), (1, ALU.subtract), (2, ALU.add))):
                        dve.tensor_tensor(mv[:, :, n], stat[:, :, j], stat[:, :, j + 3], op
                                          ).then_inc(s["mean_steps"], 1)
                    dve.wait_ge(s["mean_steps"], at(a, 5, 3))
                    dve.tensor_tensor(mv[:, :, 1], mv[:, :, 1], mv[:, :, 1], ALU.mult
                                      ).then_inc(s["mean_steps"], 1)
                    dve.tensor_scalar(mv[:, :, 0], mv[:, :, 0], 0.5, None, ALU.mult
                                      ).then_inc(s["mean_ready"], 1)
                    dve.wait_ge(s["mean_steps"], at(a, 5, 4))
                    dve.scalar_tensor_tensor(out=mv[:, :, 2], in0=mv[:, :, 1], scalar=D / 4.0, in1=mv[:, :, 2],
                                             op0=ALU.mult, op1=ALU.add).then_inc(s["mean_steps"], 1)
                    dve.wait_ge(s["mean_steps"], at(a, 5, 5))
                    dve.tensor_scalar(v0[:, 0, :], mv[:, :, 2], 1.0 / D, EPS_LN, ALU.mult, ALU.add
                                      ).then_inc(s["var0_ready"], 1)
                if front and slot == PAIRS:
                    dve.wait_ge(s["rstd0_ready"], at(a, 1, 1))
                    dve.wait_ge(s["mean_ready"], at(a, 1, 1))
                    dve.wait_ge(s["carried"], at(a, 1, 0))
                    dve.wait_ge(s["xs_ready"], at(a, 2, 0))
                    for tt in range(T):
                        dve.tensor_scalar(xf[:, tt, :], xin[:, tt, :], mv[:, tt, 0:1], r0[:, 0, tt:tt + 1],
                                          ALU.subtract, ALU.mult).then_inc(s["norm_steps"], 1)
            if front:
                dve.wait_ge(s["xt_full"], at(a, 1, 1))
                dve.wait_ge(s["col_a_loaded"], at(a, 16, 16))
                modulated(xt, M1, col_a, s["xt_ready"])
                dve.wait_ge(s["xh_ready"], at(a, 1, 1))
                dve.tensor_tensor(xl[:, :, :], xt[:, :, :], xh[:, :, :], ALU.subtract).then_inc(s["xl_ready"], 1)
            if pairs:
                for tt in range(T):
                    dve.wait_ge(s["otok_full"], at(i, 2, tt + 1))
                    src = S[:, tt, :].rearrange("p (h e) -> p h e", e=2 * DH)
                    dve.reciprocal(rden[:, tt, :], src[:, :, DH]).then_inc(s["rden_ready"], 1)
                for tt in range(T):
                    src = S[:, tt, :].rearrange("p (h e) -> p h e", e=2 * DH)
                    dve.wait_ge(s["rden_ready"], at(i, 2, tt + 1))
                    dve.tensor_tensor(o_tok[:, tt, :, :], src[:, :, 0:DH],
                                      rden[:, tt, :].unsqueeze(2).to_broadcast([P, HEADS, DH]), ALU.mult
                                      ).then_inc(s["otok_ready"], 1)
            if ffn:
                dve.wait_ge(s["f_full"], at(b, 1, 1))
                dve.wait_ge(s["frow_loaded"], at(b, 16, 16))
                dve.tensor_tensor(hf[:, :, :], TB[:, 0, :].rearrange("p (t n) -> p t n", t=T),
                                  frow[:, 0, :].unsqueeze(1).to_broadcast([P, T, D]), ALU.mult
                                  ).then_inc(s["fy_ready"], 1)
                dve.wait_ge(s["fy_ready"], at(b, 1, 1))
                dve.wait_ge(s["xb_ready"], at(b, 1, 1))
                dve.tensor_tensor(x2[:, :, :], xb[:, :, :], hf[:, :, :], ALU.add).then_inc(s["x2_ready"], 1)
            if pairs:
                dve.wait_ge(s["oh_ready"], at(i, 1, 1))
                dve.tensor_tensor(ol[:, :, :].rearrange("p k n -> p (k n)"), ST[:, 0, :],
                                  oh[:, :, :].rearrange("p k n -> p (k n)"), ALU.subtract
                                  ).then_inc(s["ol_ready"], 1)
            if front:
                low_parts(a, 0)
                low_parts(a, 1)
            if ffn:
                dve.wait_ge(s["up_full"], at(b, 1, 1))
                dve.wait_ge(s["x2b_ready"], at(b, 1, 1))
                dve.tensor_tensor(x3[:, :, :].rearrange("p t n -> p (t n)"), M0,
                                  xb[:, :, :].rearrange("p t n -> p (t n)"), ALU.add).then_inc(s["x3_ready"], 1)
                dve.wait_ge(s["col_c_loaded"], at(b, 16, 16))
                dve.wait_ge(s["ch_ready"], at(b, 2, 2))
                for k in range(K):
                    dve.scalar_tensor_tensor(out=bl[:, k, :], in0=M1[:, k * L:(k + 1) * L],
                                             scalar=col_c[:, k:k + 1], in1=bh[:, k, :], op0=ALU.mult,
                                             op1=ALU.subtract).then_inc(s["cl_ready"], 1)
            if pairs:
                dve.wait_ge(s["y_full"], at(i, 1, 1))
                dve.wait_ge(s["alpha_loaded"], at(i, 16, 16))
                dve.tensor_tensor(hf[:, :, :], OB[:, 0, :].rearrange("p (t n) -> p t n", t=T),
                                  alpha[:, :].unsqueeze(1).to_broadcast([P, T, D]), ALU.mult
                                  ).then_inc(s["y_ready"], 1)
                dve.wait_ge(s["y_ready"], at(i, 1, 1))
                dve.wait_ge(s["carried"], at(i, 1, 1))
                dve.tensor_tensor(xr[:, :, :], xc[:, :, :], hf[:, :, :], ALU.add).then_inc(s["xr_ready"], 1)
            if ffn:
                dve.wait_ge(s["r3_ready"], at(b, 1, 1))
                gated(b, 0)
            if front:
                maximum(a, 0)
            if ffn:
                gated(b, 1)
                largest(b)
                quant_scale(b, 0)
            def feed_low(tt):
                dve.wait_ge(s["bh_ready"], at(i, 2, tt + 1))
                cols_ = slice(tt * P, (tt + 1) * P)
                dve.tensor_tensor(bl[:, :, cols_], bt[:, :, cols_], bh[:, :, cols_], ALU.subtract
                                  ).then_inc(s["bl_ready"], 1)

            if front:
                maximum(a, 1)
            if ffn:
                scaled_up(b, 0)
                gated(b, 2)
            if pairs:
                feed_low(0)
            if ffn:
                largest_half(b, 0)
            if pairs:
                feed_low(1)
            if ffn:
                gated(b, 3)
            if front:
                maximum(a, 2)
            if ffn:
                floor_of_half(b)
                quantise(b, 0)

        both(dve, iteration)

    @block.gpsimd
    def _(pool):
        pool.memset(q_st[:, :, :, :].bitcast(F32), 0.0).then_inc(s["init_pool"], 1)
        pool.memset(k_st[:, :, :, :].bitcast(F32), 1.0).then_inc(s["init_pool"], 1)
        pool.wait_ge(s["init_dve"], 5)

        def inverse_root(which, ready):
            pool.tensor_tensor(r0[:, which, :], v0[:, which, :], half[:, :], ALU.pow).then_inc(ready, 1)

        def rms(which, step, ready, seq):
            pool.tensor_tensor(v0[:, which, :], ss[:, which - 1, :], eps[:, :], ALU.add).then_inc(step, 1)
            pool.wait_ge(step, at(seq, 1, 1))
            inverse_root(which, ready)

        def hidden_lo(b, f):
            pool.wait_ge(s["hh_ready"], at(b, FT, f + 1))
            pool.tensor_tensor(hl[:, f, :], hf[:, f % 2, :], hh[:, f, :], ALU.subtract).then_inc(s["hl_ready"], 1)

        def iteration(i, front, pairs, ffn, tail):
            a, b = shifted(i, 1), shifted(i, -1)
            if ffn:
                pool.wait_ge(s["frow_loaded"], at(b, 16, 16))
                pool.wait_ge(s["xr_ready"], at(b, 1, 1))
                pool.wait_ge(s["x3_ready"], at(b, 1, 0))
                pool.tensor_tensor(xb[:, :, :], xr[:, :, :], frow[:, 1, :].unsqueeze(1).to_broadcast([P, T, D]),
                                   ALU.add).then_inc(s["xb_ready"], 1)
            for slot in range(EARLY, SLOTS):
                if ffn and slot - 1 in TILE_AT:
                    hidden_lo(b, TILE_AT[slot - 1])
                if front and slot == PAIRS:
                    pool.wait_ge(s["var0_ready"], at(a, 1, 1))
                    inverse_root(0, s["rstd0_ready"])
                    pool.wait_ge(s["norm_steps"], at(a, 2, 2))
                    pool.tensor_tensor(xf[:, :, :], xf[:, :, :], t["w2"][:, :].unsqueeze(1).to_broadcast([P, T, D]),
                                       ALU.mult).then_inc(s["w2_ready"], 1)
                    pool.wait_ge(s["w2_ready"], at(a, 1, 1))
                    pool.wait_ge(s["c0_loaded"], at(a, 16, 16))
                    pool.tensor_tensor(xf[:, :, :], xf[:, :, :], c0[:, :].unsqueeze(1).to_broadcast([P, T, D]),
                                       ALU.add).then_inc(s["xf_ready"], 1)
                if front and slot == PAIRS + 3:
                    pool.wait_ge(s["ss1_ready"], at(a, 2, 2))
                    rms(1, s["var1_ready"], s["r1_ready"], a)
            if ffn:
                hidden_lo(b, FT - 1)
            if ffn:
                pool.wait_ge(s["x2_ready"], at(b, 1, 1))
                pool.tensor_tensor(xb[:, :, :], x2[:, :, :], t["bu"][:, :].unsqueeze(1).to_broadcast([P, T, D]),
                                   ALU.add).then_inc(s["x2b_ready"], 1)
                pool.wait_ge(s["ss3_ready"], at(b, 2, 2))
                rms(3, s["var3_ready"], s["r3_ready"], b)
            if pairs:
                pool.wait_ge(s["ss2_ready"], at(i, 2, 2))
                rms(2, s["var2_ready"], s["r2_ready"], i)

        both(pool, iteration)


def build(nc, x, condT, ln_w, ln_b, lin, colw, roww, out_b, wqkv, wo, wgh, wout, wup, wdn, hyper, bd, bu,
          ident, out):
    d = dict(x=x, condT=condT, ln_w=ln_w, ln_b=ln_b, lin=lin, colw=colw, roww=roww, out_b=out_b, wqkv=wqkv, wo=wo,
             wgh=wgh, wout=wout, wup=wup, wdn=wdn, hyper=hyper, bd=bd, bu=bu, ident=ident, out=out)
    d["hyp"] = nc.dram_tensor("hyp_scratch", (SEQS, P // SEQS, SEQS // 8, 2, 4, UNITS), F32).ap()
    d["cols"] = nc.dram_tensor("cols_scratch", (SEQS, P, 10), F32).ap()
    d["rows"] = nc.dram_tensor("rows_scratch", (SEQS, 4, D), F32).ap()
    with ExitStack() as ctx:
        def sb(name, shape, dt=F32):
            return ctx.enter_context(nc.sbuf_tensor(name, shape, dt))

        def split(name, shape):
            return [sb(f"{name}_hi", shape, F32R), sb(f"{name}_lo", shape, F32R)]

        t = {
            "wqkv": split("wqkv", [P, K, 3 * D]), "wo": split("wo", [P, K, D]), "wgh": split("wgh", [P, K, 2 * HID]),
            "wout": split("wout", [P, FT, D]), "wup": split("wup", [P, K, 2 * HID]),
            "wdq": sb("wdq", [P, FT, D], BF16), "ident": sb("ident", [P, P]), "ident_r": sb("ident_r", [P, P], F32R),
            "ident_b": sb("ident_b", [P, P], BF16), "w2": sb("w2", [P, D]), "bu": sb("bu", [P, D]),
            "bd": sb("bd", [P, 1]), "wmean": sb("wmean", [P, 1]),
        }
        setup_block(nc, ctx, d, t)
        main_block(nc, ctx, d, t)


def kernel(**inputs):
    import numpy as _np
    import concourse.bacc as _bacc
    from concourse import mybir as _mybir
    from concourse.bass_utils import run_bass_kernel_spmd as _run

    a = {n: _np.asarray(v) for n, v in inputs.items()}
    L1, L2 = "L1_cond_", "L2_cond_"
    rows = [
        _np.concatenate([a[L2 + "Wdd"].T, a[L2 + "Wd"].reshape(1, -1), a[L2 + "bdd"][None, :]]
                        ).reshape(C + 2, BN, K, P).transpose(0, 3, 2, 1).reshape(C + 2, P, K * BN),
        _np.concatenate([a[L2 + "Wdu"].T, a[L2 + "Wu"].reshape(1, -1), a[L2 + "bdu"][None, :]]
                        ).reshape(C + 2, D, BN).transpose(0, 2, 1),
    ]
    hyper = _np.concatenate(rows, axis=2).reshape(C + 2, P // SEQS, SEQS, UNITS).transpose(0, 2, 1, 3)
    arrays = {
        "x": a["x"], "condT": a["cond_256"].T, "ln_w": a["L0_cond_weight"], "ln_b": a["L0_cond_bias"],
        "lin": _np.concatenate([a["L0_cond_lin_w"].T, a["L0_cond_lin_b"][None, :]]),
        "colw": _np.stack([a[n].T for n in (L1 + "attn_gamma_w", L1 + "attn_beta_w", L1 + "ffn_gamma_w",
                                            L1 + "ffn_beta_w", "L3_cond_norm_w")], axis=1),
        "roww": _np.stack([a[L1 + "attn_alpha_w"].T, a[L1 + "ffn_alpha_w"].T], axis=1),
        "out_b": a[L1 + "out_b"],
        "wqkv": _np.concatenate([a[L1 + "W_q"].T, a[L1 + "W_k"].T, a[L1 + "W_v"].T], axis=1),
        "wo": a[L1 + "W_o"].T, "wgh": _np.concatenate([a[L1 + "gate_w"].T, a[L1 + "hidden_w"].T], axis=1),
        "wout": a[L1 + "out_w"].T, "wup": a["L3_cond_up_w"].T, "wdn": a["L3_cond_down_w"].T,
        "hyper": hyper,
        "bd": a[L2 + "bd"][:, None], "bu": a[L2 + "bu"], "ident": _np.eye(P, dtype=_np.float32),
    }
    arrays = {n: _np.ascontiguousarray(v) for n, v in arrays.items()}
    nc = _bacc.Bacc("TRN2", target_bir_lowering=False, num_devices=1)
    aps = {n: nc.dram_tensor(f"in_{n}", v.shape, _mybir.dt.from_np(v.dtype), kind="ExternalInput").ap()
           for n, v in arrays.items()}
    out = nc.dram_tensor("out_0", (SEQS, L, D), _mybir.dt.float32, kind="ExternalOutput").ap()
    build(nc, out=out, **aps)
    r = _run(nc, [{f"in_{n}": v for n, v in arrays.items()}], core_ids=[0])
    return r.results[0]["out_0"]
```
